# Optimizing a Trainium2 kernel written in Bass

```python
import numpy as np
import jax
import jax.numpy as jnp

def _softmax(x, axis=-1):
    return jax.nn.softmax(x, axis=axis)

def _gelu(x):
    return jax.nn.gelu(x, approximate=True)

def _silu(x):
    return jax.nn.silu(x)

def _sigmoid(x):
    return jax.nn.sigmoid(x)

def _layernorm(x, axis=-1, eps=1e-05):
    m = jnp.mean(x, axis=axis, keepdims=True)
    v = jnp.var(x, axis=axis, keepdims=True)
    return (x - m) / jnp.sqrt(v + eps)

def _scatter_add(tgt, idx, src, axis=0):
    return tgt.at[idx].add(src)

def _segment_sum(src, seg, n):
    return jax.ops.segment_sum(src, seg, n)
kernel_name = 'mk_flamingo_gated_d2_seqx_r4_68ba2a'

def setup_inputs(seed: int=0):
    np.random.seed(seed)
    _w = jnp.asarray

    def _rec_inputs():
        import jax
        import jax.numpy as jnp
        _rk = jax.random.key(seed)
        x = 7.22e-05 + 1 * jax.random.normal(jax.random.fold_in(_rk, 1), (8, 100, 256), jnp.float32)
        _lenS = 100 - jax.random.randint(jax.random.fold_in(_rk, 7), (8,), 0, max(1, 100 // 4) + 1, jnp.int32)
        _lenS2 = 361 - jax.random.randint(jax.random.fold_in(_rk, 8), (8,), 0, max(1, 361 // 4) + 1, jnp.int32)
        _ctx_1024P = jax.random.normal(jax.random.fold_in(_rk, 11), (8, 16, 256), jnp.float32)
        _ctx_1024c = jax.random.dirichlet(jax.random.fold_in(_rk, 511), 0.3 * jnp.ones((16,), jnp.float32), (8, 361))
        _ctx_1024t = jnp.einsum('bsk,bkd->bsd', _ctx_1024c, _ctx_1024P)
        _ctx_1024t = _ctx_1024t * jax.lax.rsqrt(jnp.mean(jnp.square(_ctx_1024t)) + 1e-12) * 0.953939
        ctx_1024 = 4.13588e-05 + 0.999923 * (_ctx_1024t + 0.3 * jax.random.normal(jax.random.fold_in(_rk, 611), (8, 361, 256), jnp.float32))
        _validS = jnp.arange(100)[None, :] < _lenS[:, None]
        _validS2 = jnp.arange(361)[None, :] < _lenS2[:, None]
        _causal = jnp.tril(jnp.ones((100, 100), dtype=bool))
        mask_BxSxS2_bk1 = jnp.broadcast_to(_validS2[:, None, :], (8, 100, 361))
        _g = jax.random.normal(jax.random.fold_in(_rk, 9001), (2, 2), jnp.float32)
        _g = jnp.sign(_g) * jnp.maximum(jnp.abs(_g), 1.0) + (_g == 0) * 1.0
        g_xattn = _g[0]
        g_ffn = _g[1]
        return (x, ctx_1024, mask_BxSxS2_bk1, g_xattn, g_ffn)
    x, ctx_1024, mask_BxSxS2_bk1, g_xattn, g_ffn = _rec_inputs()

    def _L0_xattn_setup():
        import jax, jax.numpy as jnp
        import numpy as np
        import math
        N, K, M = (4, 512, 256)
        DQ, DV = (256, 256)

        def _xavier_uniform(k, shape, fan_in, fan_out):
            bound = math.sqrt(6.0 / (fan_in + fan_out))
            return jax.random.uniform(k, shape, jnp.float32, -bound, bound)
        key = jax.random.key(seed)
        ks = jax.random.split(key, 9)
        query = jax.random.normal(ks[0], (N, K, M), jnp.float32)
        key_t = jax.random.normal(ks[1], (N, K, M), jnp.float32)
        value = jax.random.normal(ks[2], (N, K, M), jnp.float32)
        mask = jnp.broadcast_to(jnp.triu(jnp.ones((K, K), bool), k=1), (N, K, K))
        Wq = _xavier_uniform(ks[3], (DQ, M), M, DQ)
        bq = jax.random.uniform(ks[4], (DQ,), jnp.float32, -1 / math.sqrt(M), 1 / math.sqrt(M))
        Wk = _xavier_uniform(ks[5], (DQ, M), M, DQ)
        bk = jax.random.uniform(ks[6], (DQ,), jnp.float32, -1 / math.sqrt(M), 1 / math.sqrt(M))
        Wv = _xavier_uniform(ks[7], (DV, M), M, DV)
        bv = jax.random.uniform(ks[8], (DV,), jnp.float32, -1 / math.sqrt(M), 1 / math.sqrt(M))
        return {'query': query, 'key': key_t, 'value': value, 'mask': mask, 'Wq': Wq, 'bq': bq, 'Wk': Wk, 'bk': bk, 'Wv': Wv, 'bv': bv}
    _L0_xattn_all = _L0_xattn_setup()
    _L0_xattn_in = {k: v for k, v in _L0_xattn_all.items() if k in ('Wq', 'bq', 'Wk', 'bk', 'Wv', 'bv')}
    del _L0_xattn_all

    def _L0_ffn_setup():
        import jax, jax.numpy as jnp
        import numpy as np
        E = 16
        H = 256
        F = 512
        TOP_K = 1
        B, S = (2, 256)
        key = jax.random.key(seed)
        ks = jax.random.split(key, 7)
        s = 0.02
        return {'hidden_states': jax.random.normal(ks[0], (B, S, H), jnp.float32), 'w_router': jax.random.normal(ks[1], (E, H), jnp.float32) * s, 'gate_up_proj': jax.random.normal(ks[2], (E, H, 2 * F), jnp.float32) * s, 'down_proj': jax.random.normal(ks[3], (E, F, H), jnp.float32) * s, 'w_gate': jax.random.normal(ks[4], (F, H), jnp.float32) * s, 'w_up': jax.random.normal(ks[5], (F, H), jnp.float32) * s, 'w_down': jax.random.normal(ks[6], (H, F), jnp.float32) * s}
    _L0_ffn_all = _L0_ffn_setup()
    _L0_ffn_in = {k: v for k, v in _L0_ffn_all.items() if k in ('w_router', 'gate_up_proj', 'down_proj', 'w_gate', 'w_up', 'w_down')}
    del _L0_ffn_all

    def _L1_xattn_setup():
        import jax, jax.numpy as jnp
        import numpy as np
        DIM = 256
        HEADS = 16
        HEAD_DIM = DIM // HEADS
        SCALE = HEAD_DIM ** (-0.5)
        key = jax.random.key(seed)
        ks = jax.random.split(key, 7)
        b, n = (2, 512)
        x1 = jax.random.normal(ks[0], (b, n, DIM), dtype=jnp.float32)
        x2 = jax.random.normal(ks[1], (b, n, DIM), dtype=jnp.float32)
        s = DIM ** (-0.5)
        wq = jax.random.normal(ks[2], (DIM, DIM), dtype=jnp.float32) * s
        wk = jax.random.normal(ks[3], (DIM, DIM), dtype=jnp.float32) * s
        wv = jax.random.normal(ks[4], (DIM, DIM), dtype=jnp.float32) * s
        wo = jax.random.normal(ks[5], (DIM, DIM), dtype=jnp.float32) * s
        bo = jax.random.normal(ks[6], (DIM,), dtype=jnp.float32) * 0.01
        return {'x1': x1, 'x2': x2, 'wq': wq, 'wk': wk, 'wv': wv, 'wo': wo, 'bo': bo}
    _L1_xattn_all = _L1_xattn_setup()
    _L1_xattn_in = {k: v for k, v in _L1_xattn_all.items() if k in ('wq', 'wk', 'wv', 'wo', 'bo')}
    del _L1_xattn_all

    def _L1_ffn_setup():
        import jax, jax.numpy as jnp
        import numpy as np
        D = 256
        H = 16
        DH = D // H
        DC = D // 4
        HID = 512
        G = 2
        EPG = 4
        E = G * EPG
        TOPK = 2
        EPS = 1e-06
        B, T = (2, 512)

        def _rope_sincos(t, dh):
            inv_freq = 1.0 / 10000.0 ** (jnp.arange(0, dh, 2, dtype=jnp.float32) / dh)
            ang = jnp.arange(t, dtype=jnp.float32)[:, None] * inv_freq[None, :]
            return (jnp.sin(ang), jnp.cos(ang))

        def _apply_rope(x, sin, cos):
            x1 = x[..., ::2]
            x2 = x[..., 1::2]
            r = jnp.stack([x1 * cos - x2 * sin, x1 * sin + x2 * cos], axis=-1)
            return r.reshape(x.shape)

        def _swiglu(x):
            a, b = jnp.split(x, 2, axis=-1)
            return jax.nn.silu(a) * b

        def _rmsnorm(x, w):
            return x * jax.lax.rsqrt(jnp.mean(x * x, axis=-1, keepdims=True) + EPS) * w
        key = jax.random.key(seed)
        ks = jax.random.split(key, 14)
        s = 0.02
        return {'src': jax.random.normal(ks[0], (B, T, D), jnp.float32), 'Wq': jax.random.normal(ks[1], (D, D), jnp.float32) * s, 'Wk_c': jax.random.normal(ks[2], (D, DC), jnp.float32) * s, 'Wv_c': jax.random.normal(ks[3], (D, DC), jnp.float32) * s, 'Wk': jax.random.normal(ks[4], (DC, D), jnp.float32) * s, 'Wv': jax.random.normal(ks[5], (DC, D), jnp.float32) * s, 'Wo': jax.random.normal(ks[6], (D, D), jnp.float32) * s, 'W_shared_in': jax.random.normal(ks[7], (D, 2 * HID), jnp.float32) * s, 'W_shared_out': jax.random.normal(ks[8], (HID, D), jnp.float32) * s, 'W1_shared': jax.random.normal(ks[9], (D, 2 * HID), jnp.float32) * s, 'W2_experts': jax.random.normal(ks[10], (E, HID, D), jnp.float32) * s, 'Wg_gate': jax.random.normal(ks[11], (D, G), jnp.float32) * s, 'We_gate': jax.random.normal(ks[12], (D, E), jnp.float32) * s, 'group_bias': jnp.zeros((G,), jnp.float32), 'expert_bias': jnp.zeros((E,), jnp.float32), 'norm1_w': jnp.ones((D,), jnp.float32), 'norm2_w': jnp.ones((D,), jnp.float32)}
    _L1_ffn_all = _L1_ffn_setup()
    _L1_ffn_in = {k: v for k, v in _L1_ffn_all.items() if k in ('Wq', 'Wk_c', 'Wv_c', 'Wk', 'Wv', 'Wo', 'W_shared_in', 'W_shared_out', 'W1_shared', 'W2_experts', 'Wg_gate', 'We_gate', 'group_bias', 'expert_bias', 'norm1_w', 'norm2_w')}
    del _L1_ffn_all
    return {'x': x, 'ctx_1024': ctx_1024, 'mask_BxSxS2_bk1': mask_BxSxS2_bk1, 'g_xattn': g_xattn, 'g_ffn': g_ffn, 'L0_xattn_Wq': _L0_xattn_in['Wq'], 'L0_xattn_bq': _L0_xattn_in['bq'], 'L0_xattn_Wk': _L0_xattn_in['Wk'], 'L0_xattn_bk': _L0_xattn_in['bk'], 'L0_xattn_Wv': _L0_xattn_in['Wv'], 'L0_xattn_bv': _L0_xattn_in['bv'], 'L0_ffn_w_router': _L0_ffn_in['w_router'], 'L0_ffn_gate_up_proj': _L0_ffn_in['gate_up_proj'], 'L0_ffn_down_proj': _L0_ffn_in['down_proj'], 'L0_ffn_w_gate': _L0_ffn_in['w_gate'], 'L0_ffn_w_up': _L0_ffn_in['w_up'], 'L0_ffn_w_down': _L0_ffn_in['w_down'], 'L1_xattn_wq': _L1_xattn_in['wq'], 'L1_xattn_wk': _L1_xattn_in['wk'], 'L1_xattn_wv': _L1_xattn_in['wv'], 'L1_xattn_wo': _L1_xattn_in['wo'], 'L1_xattn_bo': _L1_xattn_in['bo'], 'L1_ffn_Wq': _L1_ffn_in['Wq'], 'L1_ffn_Wk_c': _L1_ffn_in['Wk_c'], 'L1_ffn_Wv_c': _L1_ffn_in['Wv_c'], 'L1_ffn_Wk': _L1_ffn_in['Wk'], 'L1_ffn_Wv': _L1_ffn_in['Wv'], 'L1_ffn_Wo': _L1_ffn_in['Wo'], 'L1_ffn_W_shared_in': _L1_ffn_in['W_shared_in'], 'L1_ffn_W_shared_out': _L1_ffn_in['W_shared_out'], 'L1_ffn_W1_shared': _L1_ffn_in['W1_shared'], 'L1_ffn_W2_experts': _L1_ffn_in['W2_experts'], 'L1_ffn_Wg_gate': _L1_ffn_in['Wg_gate'], 'L1_ffn_We_gate': _L1_ffn_in['We_gate'], 'L1_ffn_group_bias': _L1_ffn_in['group_bias'], 'L1_ffn_expert_bias': _L1_ffn_in['expert_bias'], 'L1_ffn_norm1_w': _L1_ffn_in['norm1_w'], 'L1_ffn_norm2_w': _L1_ffn_in['norm2_w']}

def reference(x, ctx_1024, mask_BxSxS2_bk1, g_xattn, g_ffn, L0_xattn_Wq, L0_xattn_bq, L0_xattn_Wk, L0_xattn_bk, L0_xattn_Wv, L0_xattn_bv, L0_ffn_w_router, L0_ffn_gate_up_proj, L0_ffn_down_proj, L0_ffn_w_gate, L0_ffn_w_up, L0_ffn_w_down, L1_xattn_wq, L1_xattn_wk, L1_xattn_wv, L1_xattn_wo, L1_xattn_bo, L1_ffn_Wq, L1_ffn_Wk_c, L1_ffn_Wv_c, L1_ffn_Wk, L1_ffn_Wv, L1_ffn_Wo, L1_ffn_W_shared_in, L1_ffn_W_shared_out, L1_ffn_W1_shared, L1_ffn_W2_experts, L1_ffn_Wg_gate, L1_ffn_We_gate, L1_ffn_group_bias, L1_ffn_expert_bias, L1_ffn_norm1_w, L1_ffn_norm2_w):
    import jax
    import jax.numpy as jnp

    def _L0_xattn_ref(query, key, value, mask, Wq, bq, Wk, bk, Wv, bv):
        import jax, jax.numpy as jnp
        import numpy as np
        import math
        N, K, M = (4, 512, 256)
        DQ, DV = (256, 256)

        def _xavier_uniform(k, shape, fan_in, fan_out):
            bound = math.sqrt(6.0 / (fan_in + fan_out))
            return jax.random.uniform(k, shape, jnp.float32, -bound, bound)
        Q = jnp.einsum('nkm,dm->nkd', query, Wq) + bq
        Kp = jnp.einsum('nkm,dm->nkd', key, Wk) + bk
        V = jnp.einsum('nkm,dm->nkd', value, Wv) + bv
        scores = jnp.einsum('nqd,nkd->nqk', Q, Kp) / jnp.sqrt(jnp.float32(DQ))
        scores = jnp.where(mask, jnp.float32(-1000000000.0), scores)
        w = jax.nn.softmax(scores, axis=2)
        y = jnp.einsum('nqk,nkd->nqd', w, V)
        return y

    def _L0_ffn_ref(hidden_states, w_router, gate_up_proj, down_proj, w_gate, w_up, w_down):
        import jax, jax.numpy as jnp
        import numpy as np
        E = 16
        H = 256
        F = 512
        TOP_K = 1
        B, S = (2, 256)
        b, s, h = hidden_states.shape
        x = hidden_states.reshape(-1, h)
        logits = x @ w_router.T
        _, top_idx = jax.lax.top_k(logits, TOP_K)
        mask = jax.nn.one_hot(top_idx, E, dtype=logits.dtype).sum(axis=1)
        scores = jax.nn.sigmoid(logits) * mask
        masked_inputs = scores.T[:, :, None] * x[None, :, :]
        gate_up = jnp.einsum('eth,ehf->etf', masked_inputs, gate_up_proj)
        gate, up = jnp.split(gate_up, 2, axis=-1)
        expert_out = jnp.einsum('etf,efh->eth', up * jax.nn.silu(gate), down_proj)
        shared = jax.nn.silu(x @ w_gate.T) * (x @ w_up.T) @ w_down.T
        out = shared + expert_out.sum(axis=0)
        return out.reshape(b, s, h)

    def _L1_xattn_ref(x1, x2, wq, wk, wv, wo, bo):
        import jax, jax.numpy as jnp
        import numpy as np
        DIM = 256
        HEADS = 16
        HEAD_DIM = DIM // HEADS
        SCALE = HEAD_DIM ** (-0.5)
        b, n, _ = x1.shape
        m = x2.shape[1]
        q = (x1 @ wq.T).reshape(b, n, HEADS, HEAD_DIM).transpose(0, 2, 1, 3)
        k = (x2 @ wk.T).reshape(b, m, HEADS, HEAD_DIM).transpose(0, 2, 1, 3)
        v = (x2 @ wv.T).reshape(b, m, HEADS, HEAD_DIM).transpose(0, 2, 1, 3)
        dots = jnp.einsum('bhnd,bhmd->bhnm', q, k) * SCALE
        attn = jax.nn.softmax(dots, axis=-1)
        out = jnp.einsum('bhnm,bhmd->bhnd', attn, v)
        out = out.transpose(0, 2, 1, 3).reshape(b, n, DIM)
        return out @ wo.T + bo

    def _L1_ffn_ref(src, Wq, Wk_c, Wv_c, Wk, Wv, Wo, W_shared_in, W_shared_out, W1_shared, W2_experts, Wg_gate, We_gate, group_bias, expert_bias, norm1_w, norm2_w):
        import jax, jax.numpy as jnp
        import numpy as np
        D = 256
        H = 16
        DH = D // H
        DC = D // 4
        HID = 512
        G = 2
        EPG = 4
        E = G * EPG
        TOPK = 2
        EPS = 1e-06
        B, T = (2, 512)

        def _rope_sincos(t, dh):
            inv_freq = 1.0 / 10000.0 ** (jnp.arange(0, dh, 2, dtype=jnp.float32) / dh)
            ang = jnp.arange(t, dtype=jnp.float32)[:, None] * inv_freq[None, :]
            return (jnp.sin(ang), jnp.cos(ang))

        def _apply_rope(x, sin, cos):
            x1 = x[..., ::2]
            x2 = x[..., 1::2]
            r = jnp.stack([x1 * cos - x2 * sin, x1 * sin + x2 * cos], axis=-1)
            return r.reshape(x.shape)

        def _swiglu(x):
            a, b = jnp.split(x, 2, axis=-1)
            return jax.nn.silu(a) * b

        def _rmsnorm(x, w):
            return x * jax.lax.rsqrt(jnp.mean(x * x, axis=-1, keepdims=True) + EPS) * w
        Bb, Tt, C = src.shape
        q = (src @ Wq).reshape(Bb, Tt, H, DH).transpose(0, 2, 1, 3)
        k = (src @ Wk_c @ Wk).reshape(Bb, Tt, H, DH).transpose(0, 2, 1, 3)
        v = (src @ Wv_c @ Wv).reshape(Bb, Tt, H, DH).transpose(0, 2, 1, 3)
        sin, cos = _rope_sincos(Tt, DH)
        q = _apply_rope(q, sin, cos)
        k = _apply_rope(k, sin, cos)
        attn = jnp.einsum('bhqd,bhkd->bhqk', q, k) / np.sqrt(DH).astype(np.float32)
        attn = jax.nn.softmax(attn, axis=-1)
        sa = jnp.einsum('bhqk,bhkd->bhqd', attn, v)
        sa = sa.transpose(0, 2, 1, 3).reshape(Bb, Tt, C) @ Wo
        x = _rmsnorm(src + sa, norm1_w)
        S = Bb * Tt
        flat = x.reshape(S, C)
        shared = _swiglu(flat @ W_shared_in) @ W_shared_out
        g_probs = jax.nn.softmax(flat @ Wg_gate + group_bias, -1)
        g_idx = jnp.argmax(g_probs, axis=-1)
        e_logits = flat @ We_gate + expert_bias
        e_group = jnp.arange(E) // EPG
        in_group = e_group[None, :] == g_idx[:, None]
        e_probs = jax.nn.softmax(jnp.where(in_group, e_logits, -jnp.inf), -1)
        g_prob = jnp.take_along_axis(g_probs, g_idx[:, None], axis=1)
        p_expert = e_probs * g_prob
        topv, topi = jax.lax.top_k(p_expert, TOPK)
        w = jnp.zeros((S, E), flat.dtype).at[jnp.arange(S)[:, None], topi].set(topv)
        h = _swiglu(flat @ W1_shared)
        routed = jnp.zeros_like(shared)
        for e in range(E):
            routed = routed + h @ W2_experts[e] * w[:, e:e + 1]
        out = x + (shared + routed).reshape(Bb, Tt, C)
        return _rmsnorm(out, norm2_w)
    x = x + jnp.tanh(g_xattn[0]) * _L0_xattn_ref(_layernorm(x, axis=-1), ctx_1024, ctx_1024, mask_BxSxS2_bk1, L0_xattn_Wq, L0_xattn_bq, L0_xattn_Wk, L0_xattn_bk, L0_xattn_Wv, L0_xattn_bv)
    x = x + jnp.tanh(g_ffn[0]) * _L0_ffn_ref(_layernorm(x, axis=-1), L0_ffn_w_router, L0_ffn_gate_up_proj, L0_ffn_down_proj, L0_ffn_w_gate, L0_ffn_w_up, L0_ffn_w_down)
    x = x + jnp.tanh(g_xattn[1]) * _L1_xattn_ref(_layernorm(x, axis=-1), ctx_1024, L1_xattn_wq, L1_xattn_wk, L1_xattn_wv, L1_xattn_wo, L1_xattn_bo)
    x = x + jnp.tanh(g_ffn[1]) * _L1_ffn_ref(_layernorm(x, axis=-1), L1_ffn_Wq, L1_ffn_Wk_c, L1_ffn_Wv_c, L1_ffn_Wk, L1_ffn_Wv, L1_ffn_Wo, L1_ffn_W_shared_in, L1_ffn_W_shared_out, L1_ffn_W1_shared, L1_ffn_W2_experts, L1_ffn_Wg_gate, L1_ffn_We_gate, L1_ffn_group_bias, L1_ffn_expert_bias, L1_ffn_norm1_w, L1_ffn_norm2_w)
    return x

_drawn_inputs = setup_inputs


def setup_inputs(seed=0):
    import zlib

    import numpy as np

    out = dict(_drawn_inputs(seed))
    spreads = {'g_ffn': (-1.0, 0.6),
     'L1_ffn_group_bias': (0.0, 2.0),
     'L1_ffn_expert_bias': (0.0, 2.0),
     'L1_ffn_norm1_w': (1.0, 0.2),
     'L1_ffn_norm2_w': (1.0, 0.6)}
    factors = {'L0_xattn_bq': 8.0,
     'L0_xattn_bk': 200.0,
     'L0_ffn_w_router': 8.0,
     'L0_ffn_gate_up_proj': 8.0,
     'L0_ffn_down_proj': 8.0,
     'L0_ffn_w_gate': 3.735,
     'L0_ffn_w_up': 3.694,
     'L0_ffn_w_down': 3.663,
     'L1_xattn_bo': 50.307,
     'L1_ffn_Wq': 8.0,
     'L1_ffn_Wk_c': 8.0,
     'L1_ffn_Wv_c': 3.389,
     'L1_ffn_Wk': 8.0,
     'L1_ffn_Wv': 3.459,
     'L1_ffn_Wo': 3.423,
     'L1_ffn_W1_shared': 18.0,
     'L1_ffn_W2_experts': 17.785,
     'L1_ffn_Wg_gate': 36.244,
     'L1_ffn_We_gate': 35.206,
     'L1_xattn_wq': 3.087,
     'L1_xattn_wk': 3.107,
     'L1_ffn_W_shared_in': 8.0,
     'L1_ffn_W_shared_out': 8.0}
    for name, (base, spread) in spreads.items():
        noise = np.random.default_rng([zlib.crc32(name.encode()), seed]).standard_normal(out[name].shape)
        drawn = base * np.exp(spread * noise) if base else spread * noise
        out[name] = jnp.asarray(drawn.astype(out[name].dtype))
    for name, factor in factors.items():
        out[name] = (out[name] * factor).astype(out[name].dtype)
    return out
```

```python
import numpy as np
import concourse.bass as bass
from concourse import mybir
from contextlib import ExitStack

NB, T, D = 8, 100, 256
CTX = 361
KT = D // 128
KEYS = 121
NJ = 3
CPAD = KEYS * NJ
NT = NB * T
HALF = NT // 2
NH, DH = 16, 16
NG = NH // 4
F = 512
FT = F // 128
NE, CAP = 16, 64
NPAIR = NE // 2
NSLOT = NE * CAP
FULL = CAP
SKIP = 1 << 20
NX, EPG = 8, 4
DC = 64
LN_EPS, RMS_EPS = 1e-5, 1e-6
NEG = -1000000000.0
RING = 2
KV_AT = [2, 5, 8, 11, 14]
SWAP_PAIRS = [i ^ 1 for i in range(32)]
UPPER_HALF = [16 + i % 16 for i in range(32)]

CONSTS = dict(ident=128, headmask=8, lower=T, cos=T, sin=T, rev16=NE, base16=NE, rev8=NX)


def const_slices():
    at, out = 0, {}
    for name, width in CONSTS.items():
        out[name] = slice(at, at + width)
        at += width
    return out, at


def build(nc, A, out):
    f32, i32, u8 = mybir.dt.float32, mybir.dt.int32, mybir.dt.uint8
    ALU, ACT, AX = mybir.AluOpType, mybir.ActivationFunctionType, mybir.AxisListType

    ctx = ExitStack()
    with ctx:
        def sb(name, shape, dt=f32):
            return ctx.enter_context(nc.sbuf_tensor(name, shape, dt))

        def sem(name):
            return ctx.enter_context(nc.semaphore(name))

        cs, ncols = const_slices()
        consts = sb("consts", [128, ncols])
        ident = consts[:, cs["ident"]]
        ones = sb("ones", [128, CPAD])
        zero_rows = sb("zero_rows", [128, D])
        eps_ln = sb("eps_ln", [128, 1])
        eps_rms = sb("eps_rms", [128, 1])
        gates = sb("gates", [128, 4])
        tg = sb("tg", [128, 4])
        x = sb("x", [T, NB, D])
        hN = sb("hN", [T, NB, D])
        hT = sb("hT", [128, KT, NT])
        bn6 = sb("bn6", [T, NB, 6])
        mv = sb("mv", [T, NB, 2])
        std = sb("std", [T, NB])
        rstd = sb("rstd", [T, NB])
        ctxT = sb("ctxT", [128, KT, NB, CPAD])
        brow = {n: sb("row_" + n, [T, D]) for n in ("bv", "bo", "n1", "n2")}
        grow = sb("grow", [T, D])
        big = sb("big", [128, NB * NJ * D + 256])
        ctxN = big[:, 0:NB * NJ * D].rearrange("p (b j d) -> p b j d", b=NB, j=NJ)
        arena = sb("arena", [128, 6656])

        def carve(start, *dims, rows=128):
            n = int(np.prod(dims))
            names = "abcd"[:len(dims)]
            part = arena[0:rows, start:start + n]
            if len(dims) == 1:
                return part
            return part.rearrange(f"p ({' '.join(names)}) -> p {' '.join(names)}",
                                  **dict(zip(names[:-1], dims[:-1])))

        W = KT * D
        wq0 = carve(0, KT, D)
        wk0 = carve(W, KT, D)
        wv0 = carve(2 * W, KT, D)
        fold = carve(3 * W, KT, D)
        keep = carve(4 * W, 2, CTX, rows=T)
        drop = carve(4 * W + 2 * CTX, 2, CTX, rows=T)
        sc = carve(4 * W + 4 * CTX, 2, CTX, rows=T)
        bqk = sb("bqk", [128, 2, KT])
        foldv = sb("foldv", [128, 4])
        fold0 = sb("fold0", [1, 1])
        tT = sb("tT", [128, KT, NT])
        sil = sb("sil", [128, 2, F])
        row_T = sil[:].rearrange("p a b -> p (a b)")
        cT = row_T[0:1, 0:NT]
        mask8 = sb("mask8", [T, NB, CTX], u8)
        NP_ = 4
        prob = sb("prob", [T, NP_, CPAD])
        nmx = sb("nmx", [T, 4, NB])
        rsum = sb("rsum", [T, NB])
        rg = sb("rg", [T, NB])
        pT = sb("pT", [128, 2, NJ * T])
        mixT = sb("mixT", [128, 2, KT, T])
        ring = sb("ring", [128, RING, 2, 2 * KT * F + FT * D])
        wr = sb("wr", [128, KT, NE])
        wgu = sb("wgu", [128, KT, 2, F])
        wdn = sb("wdn", [128, FT, D])
        hid = big[:, 0:FT * NT].rearrange("p (f t) -> p f t", f=FT)
        lgT = row_T[0:NE, 0:NT]
        lg = sb("lg", [T, NB, NE])
        oh = sb("oh", [T, NB, NE])
        key = sb("key", [T, NB, NE])
        pre = sb("pre", [T, NB, NE])
        pos = sb("pos", [T, NB, NE])
        r1 = sb("r1", [T, 12, NB])
        slot = sb("slot", [T, NB], i32)
        oscale = sb("oscale", [T, NB, NE])
        ocol = sb("ocol", [T, NB])
        flag = sb("flag", [1, 1], i32)
        xs = carve(0, NB, D, rows=T)
        xg = carve(8 * D, NPAIR, D)
        au = carve(16 * D, 2, F)
        auT = carve(20 * D, 2, FT, 128)
        yb = carve(24 * D, 2, D)
        GU = KT * 2 * F
        wc = sb("wc", [128, 3, KT, D])
        wo = sb("wo", [128, 2, NG, D])
        qT = tT
        kflat = big[:, 0:KT * NT]
        kT = kflat[:, 0:2 * KT * CPAD].rearrange("p (u k c) -> p u k c", u=2, k=KT)
        krT = kflat.rearrange("p (k t) -> p k t", k=KT)
        vpad = carve(0, 2, NJ, NH * 32)
        qbd = carve(2 * NJ * NH * 32, 2, KT, 8 * T)
        den = big[:, 1600:1600 + NG * T]
        attT = big[:, 2000:2000 + 2 * NG * T].rearrange("p (u g t) -> p u g t", u=2, g=NG)
        xgT = big[:, FT * NT:FT * NT + 2 * KT * 128].rearrange("p (u k t) -> p u k t", u=2, k=KT)

        pTq = big[:, 2800:2800 + 8 * NJ * T].rearrange("p (u n) -> p u n", u=8)
        wflat = wgu[:].rearrange("p k w f -> p (k w f)")
        wq2 = wflat[:, 0:W].rearrange("p (k n) -> p k n", k=KT)
        wkvc = wflat[:, W:W + KT * 2 * DC].rearrange("p (k n) -> p k n", k=KT)
        wkv2 = wflat[:, 2 * W:2 * W + 2 * D].rearrange("p (w n) -> p w n", w=2)
        wge = wflat[:, 3 * W:3 * W + KT * (2 + NX)].rearrange("p (k n) -> p k n", k=KT)
        rflat = ring[:].rearrange("p r e n -> p (r e n)")
        w2 = rflat[:, 0:FT * NX * D].rearrange("p (f e d) -> p f e d", f=FT, e=NX)
        wgu2 = rflat[:, FT * NX * D:FT * NX * D + 2 * KT * 2 * F].rearrange("p (s k n) -> p s k n", s=2, k=KT)
        kvcT = big[:, 3600:3600 + NT]
        rot = big[:, 4400:4400 + KT * NT]
        prob4 = prob[:].rearrange("t u n -> t (u n)")[:, 0:2 * 4 * T].rearrange("t (u n) -> t u n", u=2)
        pT4 = big[:, 2800:2800 + 2 * 4 * T].rearrange("p (u n) -> p u n", u=2)
        hid2 = big[:, 0:2 * FT * NT].rearrange("p (s f t) -> p s f t", s=2, f=FT)
        gbias = sb("gbias", [T, 2 + NX])
        gl = sb("gl", [T, NB, 2 + NX])
        ge = sb("ge", [T, NB, 2 + NX])
        we = sb("we", [T, NB, NX])

        PB = [ctx.enter_context(nc.psum_tensor(f"pb{i}", [128, 512], f32)) for i in range(8)]

        def bank3(i, a, n, rows=128):
            return PB[i][0:rows, 0:a * n].rearrange("p (a n) -> p a n", a=a)

        S = {}

        def s(name):
            if name not in S:
                S[name] = sem(name)
            return S[name]

        names = ["ld_x", "ld_const", "ld_small", "ld_w0", "ld_ctxT", "ld_ctxN", "ld_mask", "ld_wb", "ld_wc",
                 "dve_step", "act_step", "pool_step", "set_ones", "set_zero", "set_pads", "stored"]
        for st in "abcd":
            names += [f"{st}_var", f"{st}_std", f"{st}_hN", f"{st}_tp", f"{st}_hT"]
        names += ["a_fold", "a_foldsb", "a_t", "a_tsb", "a_c", "a_csb", "a_mask", "a_s", "a_max", "a_p", "a_pt",
                  "a_ptsb", "a_mix", "a_mixsb", "a_y", "a_res"]
        names += ["ld_ring0", "ld_ring1", "b_zero", "b_lgT", "b_lgTsb", "b_lg", "b_mx", "b_sig", "b_oh", "b_pos", "b_slot",
                  "b_xs", "b_scat", "b_xg0", "b_xg1", "b_xg2", "b_xg3", "b_sgu", "b_sil", "b_hid", "b_xt", "b_xtsb",
                  "b_gu", "b_esil", "b_au", "b_at", "b_atsb", "b_sd", "b_sdres", "b_y", "b_ysb", "b_yst0", "b_yst1",
                  "b_clear", "b_gat", "b_res"]
        names += ["o_count", "o_flag", "o_ld", "o_gu", "o_sil", "o_au", "o_col", "o_at", "o_atsb", "o_y", "o_res"]
        names += ["ld_wd", "c_vones", "c_q", "c_qsb", "c_qbd", "c_pr", "c_prsb", "c_s", "c_max", "c_p", "c_pt", "c_ptsb",
                  "c_av", "c_att", "c_y", "c_res"]
        names += ["d_q", "d_qsb", "d_kvc", "d_kvcsb", "d_k", "d_ksb", "d_rot", "d_qbd", "d_v", "d_vsb", "d_s", "d_shift", "d_p",
                  "d_pt", "d_ptsb", "d_av", "d_att", "d_y", "d_x2", "d_sq", "e_hN", "e_tp", "e_hT", "e_std",
                  "e_gT", "e_gTsb", "e_g", "e_gx", "e_gexp", "e_gu", "e_sil", "e_hid", "e_down", "e_comb", "f_sq", "f_std",
                  "f_out"]
        for n in names:
            s(n)

        xs_dram, y_dram = A["xs_dram"], A["y_dram"]
        block = ctx.enter_context(nc.Block())

        @block.sync
        def _(sp):
            sp.dma_start(x[:], A["x"]).then_inc(s("ld_x"), 16)
            sp.dma_start(consts[:], A["consts"]).then_inc(s("ld_const"), 16)
            for i, n in enumerate(("L0_xattn_Wq", "L0_xattn_Wk", "L0_xattn_WvT")):
                sp.dma_start((wq0, wk0, wv0)[i][:], A[n].rearrange("(k p) n -> p k n", p=128)).then_inc(s("ld_w0"), 16)
            sp.dma_start(bqk[:], A["bqk"]).then_inc(s("ld_w0"), 16)
            for i, n in enumerate(("g_xattn", "g_ffn")):
                sp.dma_start(gates[:, 2 * i:2 * i + 2], A[n].partition_broadcast(128)).then_inc(s("ld_small"), 16)
            for n, w in (("bv", "L0_xattn_bv"), ("bo", "L1_xattn_bo"), ("n1", "L1_ffn_norm1_w"), ("n2", "L1_ffn_norm2_w")):
                sp.dma_start(brow[n][:], A[w].partition_broadcast(T)).then_inc(s("ld_small"), 16)
            sp.dma_start(mask8[:], A["mask"]).then_inc(s("ld_mask"), 16)
            for k in range(KT):
                sp.dma_start(ctxT[:, k, :, 0:CTX], A["ctxT"][128 * k:128 * k + 128]).then_inc(s("ld_ctxT"), 16)
            sp.wait_ge(s("set_pads"), 1)
            for j in range(NJ):
                n = min(KEYS, CTX - KEYS * j)
                sp.dma_start(ctxN[0:n, :, j, :], A["ctx"][:, KEYS * j:KEYS * j + n, :].rearrange("b p d -> p b d")) \
                    .then_inc(s("ld_ctxN"), 16)
            sp.wait_ge(s("set_zero"), 1)
            for i in range(NPAIR):
                sp.dma_start(xs_dram[128 * i:128 * i + 128, :], zero_rows[:]).then_inc(s("b_zero"), 16)
            sp.dma_start(wr[:], A["L0_ffn_w_routerT"].rearrange("(k p) n -> p k n", p=128)).then_inc(s("ld_wb"), 16)
            for i, n in enumerate(("L0_ffn_w_gateT", "L0_ffn_w_upT")):
                sp.dma_start(wgu[:, :, i, :], A[n].rearrange("(k p) n -> p k n", p=128)).then_inc(s("ld_wb"), 16)
            sp.dma_start(wdn[:], A["L0_ffn_w_downT"].rearrange("(k p) n -> p k n", p=128)).then_inc(s("ld_wb"), 16)

            for i, n in enumerate(("L1_xattn_wqT", "L1_xattn_wkT", "L1_xattn_wvT")):
                sp.dma_start(wc[:, i], A[n].rearrange("(k p) n -> p k n", p=128)).then_inc(s("ld_wc"), 16)
            for i, n in enumerate(("L1_xattn_woT", "L1_ffn_Wo")):
                for j in range(4):
                    sp.dma_start(wo[32 * j:32 * j + DH, i], A[n].rearrange("(g j d) n -> j d g n", j=4, d=DH)[j]) \
                        .then_inc(s("ld_wc"), 16)
            sp.dma_start(gbias[:, 0:2], A["L1_ffn_group_bias"].partition_broadcast(T)).then_inc(s("ld_wc"), 16)
            sp.dma_start(gbias[:, 2:], A["L1_ffn_expert_bias"].partition_broadcast(T)).then_inc(s("ld_wc"), 16)

            def load_pair(i):
                for e in range(2):
                    sp.dma_start(ring[:, i % RING, e, 0:GU].rearrange("p (k n) -> p k n", k=KT),
                                 A["L0_ffn_gate_up_proj"][2 * i + e].rearrange("(k p) n -> p k n", p=128)) \
                        .then_inc(s(f"ld_ring{i % RING}"), 16)
                    sp.dma_start(ring[:, i % RING, e, GU:].rearrange("p (k n) -> p k n", k=FT),
                                 A["L0_ffn_down_proj"][2 * i + e].rearrange("(k p) n -> p k n", p=128)) \
                        .then_inc(s(f"ld_ring{i % RING}"), 16)

            for i in range(RING):
                load_pair(i)
            sp.wait_ge(s("b_scat"), 16 * NB)
            for g in range(4):
                sp.dma_start(xg[:, 2 * g:2 * g + 2, :],
                             xs_dram[256 * g:256 * g + 256, :].rearrange("(i p) d -> p i d", p=128)) \
                    .then_inc(s(f"b_xg{g}"), 16)
            for i in range(NPAIR):
                sp.wait_ge(s("b_ysb"), i + 1)
                sp.dma_start(y_dram[128 * i:128 * i + 128, :], yb[:, i % 2, :]).then_inc(s(f"b_yst{i % 2}"), 16)
                if i + RING < NPAIR:
                    load_pair(i + RING)
            sp.wait_ge(s("b_y"), NPAIR)
            sp.wait_ge(s("o_flag"), 1)
            over = sp.value_load(flag[0:1, 0:1], min_val=0, max_val=NT)
            with sp.If(over > 0):
                with sp.Fori(0, NE) as e:
                    sp.wait_ge(s("o_res"), NB * e + 1)
                    sp.dma_start(ring[:, 0, 0, 0:GU].rearrange("p (k n) -> p k n", k=KT),
                                 A["L0_ffn_gate_up_proj"][bass.ds(e, 1)].rearrange("e (k p) n -> p (e k) n", p=128)) \
                        .then_inc(s("o_ld"), 16)
                    sp.dma_start(ring[:, 0, 0, GU:].rearrange("p (k n) -> p k n", k=FT),
                                 A["L0_ffn_down_proj"][bass.ds(e, 1)].rearrange("e (k p) n -> p (e k) n", p=128)) \
                        .then_inc(s("o_ld"), 16)
                sp.wait_ge(s("o_res"), NB * NE + 1)
            sp.wait_ge(s("b_y"), NPAIR)
            sp.wait_ge(s("b_clear"), 2)
            sp.dma_start(wq2, A["L1_ffn_Wq"].rearrange("(k p) n -> p k n", p=128)).then_inc(s("ld_wd"), 16)
            sp.dma_start(wkvc[:, :, 0:DC], A["L1_ffn_Wk_c"].rearrange("(k p) n -> p k n", p=128)).then_inc(s("ld_wd"), 16)
            sp.dma_start(wkvc[:, :, DC:], A["L1_ffn_Wv_c"].rearrange("(k p) n -> p k n", p=128)).then_inc(s("ld_wd"), 16)
            sp.dma_start(wkv2[0:DC, 0], A["L1_ffn_Wk"]).then_inc(s("ld_wd"), 16)
            sp.dma_start(wkv2[DC:, 1], A["L1_ffn_Wv"]).then_inc(s("ld_wd"), 16)
            sp.dma_start(wge[:, :, 0:2], A["L1_ffn_Wg_gate"].rearrange("(k p) n -> p k n", p=128)).then_inc(s("ld_wd"), 16)
            sp.dma_start(wge[:, :, 2:], A["L1_ffn_We_gate"].rearrange("(k p) n -> p k n", p=128)).then_inc(s("ld_wd"), 16)
            for i, n in enumerate(("L1_ffn_W_shared_in", "L1_ffn_W1_shared")):
                sp.dma_start(wgu2[:, i], A[n].rearrange("(k p) n -> p k n", p=128)).then_inc(s("ld_wd"), 16)
            sp.dma_start(wdn[:], A["L1_ffn_W_shared_out"].rearrange("(k p) n -> p k n", p=128)).then_inc(s("ld_wd"), 16)
            for f in range(FT):
                sp.dma_start(w2[:, f], A["L1_ffn_W2_experts"][:, 128 * f:128 * f + 128, :].rearrange("e p d -> p e d")) \
                    .then_inc(s("ld_wd"), 16)
            for b in range(0, NB, 2):
                sp.wait_ge(s("f_out"), b + 2)
                sp.dma_start(out[b:b + 2].rearrange("b t d -> t b d"), x[:, b:b + 2, :]).then_inc(s("stored"), 16)
            sp.wait_ge(s("stored"), 16 * NB // 2)

        @block.gpsimd
        def _(pool):
            nc.gpsimd.memset(ones[:], 1.0)
            nc.gpsimd.memset(eps_ln[:], LN_EPS)
            nc.gpsimd.memset(eps_rms[:], RMS_EPS).then_inc(s("set_ones"), 1)
            nc.gpsimd.memset(ctxN[0:KEYS, :, NJ - 1, :], 0.0)
            nc.gpsimd.memset(ctxT[:, :, :, CTX:CPAD], 0.0)
            nc.gpsimd.memset(prob[:, :, CTX:CPAD], 0.0).then_inc(s("set_pads"), 1)
            nc.gpsimd.memset(wo[:], 0.0)
            nc.gpsimd.memset(zero_rows[:], 0.0).then_inc(s("set_zero"), 1)
            pool.wait_ge(s("ld_mask"), 16)
            for b in range(NB):
                if b >= 2:
                    pool.wait_ge(s("a_max"), b - 1)
                nc.gpsimd.tensor_scalar(keep[:, b % 2, :], mask8[:, b, :], -1.0, 1.0, ALU.mult, ALU.add)
                nc.gpsimd.tensor_scalar(drop[:, b % 2, :], mask8[:, b, :], NEG, 0.0, ALU.mult, ALU.add) \
                    .then_inc(s("a_mask"), 1)
            pool.wait_ge(s("b_zero"), 16 * NPAIR)
            for b in range(NB):
                pool.wait_ge(s("b_xs"), b + 1)
                nc.gpsimd.indirect_dma_start(xs_dram, bass.IndirectOffsetOnAxis(slot[:, b:b + 1], 0), xs[:, b, :], None,
                                             bounds_check=NSLOT - 1, oob_is_err=False).then_inc(s("b_scat"), 16)
            pool.wait_ge(s("b_hT"), NB // 2)
            nc.gpsimd.memset(hN[:], 0.0).then_inc(s("b_clear"), 1)
            pool.wait_ge(s("b_clear"), 1)
            for u in range(2):
                pool.wait_ge(s(f"b_yst{u}"), 16 * NPAIR // 2)
            for b in range(NB):
                nc.gpsimd.indirect_dma_start(hN[:, b, :], None, y_dram, bass.IndirectOffsetOnAxis(slot[:, b:b + 1], 0),
                                             bounds_check=NSLOT - 1, oob_is_err=False).then_inc(s("b_gat"), 16)
            nc.gpsimd.memset(wkv2[0:DC, 1], 0.0)
            nc.gpsimd.memset(wkv2[DC:, 0], 0.0).then_inc(s("b_clear"), 1)
            pool.wait_ge(s("b_clear"), 2)
            for u in range(2):
                for j in range(NJ):
                    last = nc.gpsimd.memset(vpad[:, u, j, :].rearrange("p (h c) -> p h c", c=32)[:, :, DH:], 1.0)
            last.then_inc(s("c_vones"), 1)

            def spread_queries(b, done):
                q = qT[:, :, T * b:T * b + T].unsqueeze(2).to_broadcast([128, KT, 8, T])
                m = consts[:, cs["headmask"]].unsqueeze(1).unsqueeze(3).to_broadcast([128, KT, 8, T])
                nc.gpsimd.tensor_tensor(qbd[:, b % 2].rearrange("p k (h t) -> p k h t", h=8), q, m, ALU.mult) \
                    .then_inc(done, 1)

            pool.wait_ge(s("c_qsb"), 2 * KT)
            for b in range(NB):
                if b >= 2:
                    pool.wait_ge(s("c_s"), NH * (b - 1))
                spread_queries(b, s("c_qbd"))
            pool.wait_ge(s("d_rot"), 2)
            for b in range(NB):
                if b >= 2:
                    pool.wait_ge(s("d_s"), 4 * (b - 1))
                spread_queries(b, s("d_qbd"))

        @block.scalar
        def _(act):
            def ln_act(st):
                act.wait_ge(s(st + "_var"), 1)
                nc.scalar.activation(std[:], mv[:, :, 1], ACT.Sqrt, bias=eps_ln[0:T, :]).then_inc(s(st + "_std"), 1)
                for g in range(NB // 2):
                    act.wait_ge(s(st + "_tp"), g + 1)
                    nc.scalar.activation(hT[:, :, 2 * T * g:2 * T * (g + 1)], bank3(g % 2, KT, 2 * T), ACT.Copy) \
                        .then_inc(s(st + "_hT"), 1)

            act.wait_ge(s("set_ones"), 1)
            act.wait_ge(s("ld_small"), 96)
            nc.scalar.activation(tg[:], gates[:], ACT.Tanh).then_inc(s("act_step"), 1)
            ln_act("a")
            for u in range(2 * KT):
                n, half = u // 2, u % 2
                act.wait_ge(s("a_t"), u + 1)
                if u == 0:
                    act.wait_ge(s("a_foldsb"), 1)
                nc.scalar.activation(tT[:, n, HALF * half:HALF * (half + 1)], PB[4 + u % 2][:, 0:HALF], ACT.Identity,
                                     bias=foldv[:, n:n + 1]).then_inc(s("a_tsb"), 1)
            for half in range(2):
                act.wait_ge(s("a_c"), half + 1)
                nc.scalar.activation(cT[:, HALF * half:HALF * (half + 1)], PB[6 + half][0:1, 0:HALF], ACT.Identity,
                                     bias=fold0[:]).then_inc(s("a_csb"), 1)
            act.wait_ge(s("set_pads"), 1)
            for i in range(NB + 1):
                if i < NB:
                    act.wait_ge(s("a_max"), i + 1)
                    if i >= NP_:
                        act.wait_ge(s("a_pt"), i - NP_ + 1)
                    nc.scalar.activation(prob[:, i % NP_, 0:CTX], sc[:, i % 2, :], ACT.Exp, bias=nmx[:, 0, i:i + 1],
                                         accum_out=rsum[:, i:i + 1]).then_inc(s("a_p"), 1)
                if i >= 1:
                    b = i - 1
                    act.wait_ge(s("a_mix"), b + 1)
                    if b >= 2:
                        act.wait_ge(s("a_y"), b - 1)
                    nc.scalar.activation(mixT[:, b % 2], bank3(4 + b % 2, KT, T), ACT.Copy).then_inc(s("a_mixsb"), 1)
            ln_act("b")
            for half in range(2):
                act.wait_ge(s("b_lgT"), half + 1)
                nc.scalar.activation(lgT[:, HALF * half:HALF * (half + 1)], PB[2 + half][0:NE, 0:HALF], ACT.Copy) \
                    .then_inc(s("b_lgTsb"), 1)
            act.wait_ge(s("b_mx"), 1)
            nc.scalar.activation(r1[:, 1, :], r1[:, 0, :], ACT.Sigmoid).then_inc(s("b_sig"), 1)
            act.wait_ge(s("b_lg"), 1)
            for u in range(2 * FT):
                act.wait_ge(s("b_sgu"), u + 1)
                if u >= 2:
                    act.wait_ge(s("b_hid"), u - 1)
                nc.scalar.activation(sil[:, u % 2, 0:HALF], PB[2 * u % 8][:, 0:HALF], ACT.Silu).then_inc(s("b_sil"), 1)

            def xg_copy(i):
                act.wait_ge(s("b_xt"), i + 1)
                if i >= 2:
                    act.wait_ge(s("b_gu"), i - 1)
                nc.scalar.activation(xgT[:, i % 2], bank3(6, KT, 128), ACT.Copy).then_inc(s("b_xtsb"), 1)

            xg_copy(0)
            for i in range(NPAIR + 1):
                if i < NPAIR:
                    act.wait_ge(s("b_gu"), i + 1)
                    act.wait_ge(s("b_hid"), 2 * FT)
                    if i >= 2:
                        act.wait_ge(s("b_au"), i - 1)
                    nc.scalar.activation(sil[:, i % 2, :], PB[2 * (i % 2)][:, :], ACT.Silu).then_inc(s("b_esil"), 1)
                if i + 1 < NPAIR:
                    xg_copy(i + 1)
                if i >= 1:
                    p = i - 1
                    act.wait_ge(s("b_y"), p + 1)
                    if p >= 2:
                        act.wait_ge(s(f"b_yst{p % 2}"), 16 * (p // 2))
                    nc.scalar.activation(yb[:, p % 2, :], PB[5][:, 0:D], ACT.Copy).then_inc(s("b_ysb"), 1)
            act.wait_ge(s("o_flag"), 1)
            over = act.value_load(flag[0:1, 0:1], min_val=0, max_val=NT)
            with act.If(over > 0):
                with act.Fori(0, NE) as e:
                    for b in range(NB):
                        act.wait_ge(s("o_gu"), NB * e + (b + 1))
                        nc.scalar.activation(sil[0:T, 0, :], PB[0][0:T, :], ACT.Silu, scale=ocol[:, b:b + 1]) \
                            .then_inc(s("o_sil"), 1)
            ln_act("c")

            def q_copy(st):
                for u in range(2 * KT):
                    n, half = u // 2, u % 2
                    act.wait_ge(s(st + "_q"), u + 1)
                    nc.scalar.activation(qT[:, n, HALF * half:HALF * (half + 1)], PB[4 + u % 2][:, 0:HALF], ACT.Copy,
                                         scale=float(DH) ** -0.5).then_inc(s(st + "_qsb"), 1)

            def kv_copy(b, i):
                act.wait_ge(s("c_pr"), 5 * b + i + 1)
                if i < KT:
                    nc.scalar.activation(kT[:, b % 2, i, :], PB[6][:, 0:CPAD], ACT.Copy).then_inc(s("c_prsb"), 1)
                else:
                    nc.scalar.activation(vpad[0:KEYS, b % 2, i - KT, :].rearrange("p (h c) -> p h c", c=32)[:, :, 0:DH],
                                         PB[6][0:KEYS, 0:D].rearrange("p (h c) -> p h c", c=DH), ACT.Copy) \
                        .then_inc(s("c_prsb"), 1)

            q_copy("c")
            act.wait_ge(s("c_vones"), 1)
            for i in range(5):
                kv_copy(0, i)
            for n in range(NB * NH):
                b, h = n // NH, n % NH
                act.wait_ge(s("c_max"), n + 1)
                if n >= 4:
                    act.wait_ge(s("c_pt"), n - 3)
                nc.scalar.activation(prob[:, n % 4, 0:CTX], PB[n % 2][0:T, 0:CTX], ACT.Exp,
                                     bias=nmx[:, n % 4, 0:1]).then_inc(s("c_p"), 1)
                if b + 1 < NB and h in KV_AT:
                    kv_copy(b + 1, KV_AT.index(h))
            ln_act("d")
            q_copy("d")
            for half in range(2):
                act.wait_ge(s("d_kvc"), half + 1)
                nc.scalar.activation(kvcT[:, HALF * half:HALF * (half + 1)], PB[6 + half][:, 0:HALF], ACT.Copy) \
                    .then_inc(s("d_kvcsb"), 1)
            for u in range(2 * KT):
                n, half = u // 2, u % 2
                act.wait_ge(s("d_k"), u + 1)
                nc.scalar.activation(krT[:, n, HALF * half:HALF * (half + 1)], PB[4 + u % 2][:, 0:HALF], ACT.Copy) \
                    .then_inc(s("d_ksb"), 1)

            def v_copy(b):
                act.wait_ge(s("d_v"), b + 1)
                nc.scalar.activation(vpad[0:T, b % 2, 0, :].rearrange("p (h c) -> p h c", c=32)[:, :, 0:DH],
                                     PB[6][0:T, 0:D].rearrange("p (h c) -> p h c", c=DH), ACT.Copy).then_inc(s("d_vsb"), 1)

            v_copy(0)
            for n in range(4 * NB):
                b, g = n // 4, n % 4
                act.wait_ge(s("d_shift"), n + 1)
                nc.scalar.activation(prob4[:, n % 2, :], prob4[:, n % 2, :], ACT.Exp).then_inc(s("d_p"), 1)
                if g == 1 and b + 1 < NB:
                    v_copy(b + 1)
            for b in range(NB):
                act.wait_ge(s("d_x2"), b + 1)
                if b >= 4:
                    act.wait_ge(s("d_sq"), b - 3)
                nc.scalar.activation(row_T[0:T, D * (b % 4):D * (b % 4) + D], hN[:, b, :], ACT.Square, accum_out=rsum[:, b:b + 1]).then_inc(s("d_sq"), 1)
            act.wait_ge(s("d_sq"), NB)
            nc.scalar.activation(std[:], rsum[:], ACT.Sqrt, scale=1.0 / D, bias=eps_rms[0:T, :]).then_inc(s("e_std"), 1)
            for g in range(NB // 2):
                act.wait_ge(s("e_tp"), g + 1)
                nc.scalar.activation(hT[:, :, 2 * T * g:2 * T * (g + 1)], bank3(g % 2, KT, 2 * T), ACT.Copy) \
                    .then_inc(s("e_hT"), 1)
            for half in range(2):
                act.wait_ge(s("e_gT"), half + 1)
                nc.scalar.activation(row_T[0:2 + NX, HALF * half:HALF * (half + 1)], PB[2 + half][0:2 + NX, 0:HALF], ACT.Copy) \
                    .then_inc(s("e_gTsb"), 1)
            act.wait_ge(s("e_gx"), 1)
            nc.scalar.activation(ge[:], gl[:], ACT.Exp).then_inc(s("e_gexp"), 1)
            act.wait_ge(s("e_g"), 1)
            for u in range(4 * FT):
                act.wait_ge(s("e_gu"), u + 1)
                if u >= 2:
                    act.wait_ge(s("e_hid"), u - 1)
                nc.scalar.activation(sil[:, u % 2, 0:HALF], PB[2 * u % 8][:, 0:HALF], ACT.Silu).then_inc(s("e_sil"), 1)
            act.wait_ge(s("e_hid"), 4 * FT)
            for b in range(NB):
                act.wait_ge(s("e_comb"), 5 * b + 5)
                if b >= 4:
                    act.wait_ge(s("f_sq"), b - 3)
                nc.scalar.activation(row_T[0:T, D * (b % 4):D * (b % 4) + D], hN[:, b, :], ACT.Square, accum_out=rsum[:, b:b + 1]).then_inc(s("f_sq"), 1)
                if b % 4 == 3:
                    act.wait_ge(s("f_sq"), b + 1)
                    nc.scalar.activation(std[:, b - 3:b + 1], rsum[:, b - 3:b + 1], ACT.Sqrt, scale=1.0 / D,
                                         bias=eps_rms[0:T, :]).then_inc(s("f_std"), 1)

        @block.vector
        def _(dve):
            steps = [0]

            def link(ins):
                steps[0] += 1
                ins.then_inc(s("dve_step"), 1)
                dve.wait_ge(s("dve_step"), steps[0])

            def bc(ap, n):
                return ap.unsqueeze(2).to_broadcast([ap.shape[0], ap.shape[1], n])

            def ln_dve(st):
                for b in range(NB):
                    last = nc.vector.bn_stats(bn6[:, b, :], x[:, b, :])
                link(last)
                for b in range(NB):
                    last = nc.vector.bn_aggr(mv[:, b, :], bn6[:, b, :])
                last.then_inc(s(st + "_var"), 1)
                dve.wait_ge(s(st + "_std"), 1)
                link(nc.vector.reciprocal(rstd[:], std[:]))
                for b in range(NB):
                    nc.vector.tensor_scalar(hN[:, b, :], x[:, b, :], mv[:, b, 0:1], rstd[:, b:b + 1],
                                            ALU.subtract, ALU.mult).then_inc(s(st + "_hN"), 1)

            dve.wait_ge(s("ld_x"), 16)
            ln_dve("a")
            dve.wait_ge(s("a_fold"), 1)
            nc.vector.tensor_scalar(fold[:], bank3(2, KT, D), 1.0 / 16, None, ALU.mult)
            nc.vector.tensor_scalar(foldv[:], PB[3][:, 0:4], 1.0 / 16, None, ALU.mult)
            nc.vector.tensor_scalar(fold0[:], PB[3][0:1, 4:5], 1.0 / 16, None, ALU.mult).then_inc(s("a_foldsb"), 1)
            dve.wait_ge(s("act_step"), 1)
            dve.wait_ge(s("ld_small"), 96)
            link(nc.vector.tensor_scalar(grow[:], brow["bv"][:], tg[0:T, 0:1], None, ALU.mult))
            link(nc.vector.tensor_tensor(x[:], x[:], grow[:].unsqueeze(1).to_broadcast([T, NB, D]), ALU.add))
            for i in range(NB + 2):
                if i < NB:
                    b = i
                    dve.wait_ge(s("a_s"), b + 1)
                    dve.wait_ge(s("a_mask"), b + 1)
                    if b >= 2:
                        dve.wait_ge(s("a_p"), b - 1)
                    link(nc.vector.tensor_tensor(sc[:, b % 2, :], PB[b % 2][0:T, 0:CTX], keep[:, b % 2, :], ALU.mult))
                    link(nc.vector.tensor_tensor(sc[:, b % 2, :], sc[:, b % 2, :], drop[:, b % 2, :], ALU.add))
                    nc.vector.tensor_reduce(nmx[:, 0, b:b + 1], sc[:, b % 2, :], AX.X, ALU.max, negate=True) \
                        .then_inc(s("a_max"), 1)
                if 1 <= i <= NB:
                    b = i - 1
                    dve.wait_ge(s("a_pt"), b + 1)
                    if b >= 2:
                        dve.wait_ge(s("a_mix"), b - 1)
                    nc.vector.tensor_copy(pT[0:KEYS, b % 2, :], PB[2 + b % 2][0:KEYS, 0:NJ * T]).then_inc(s("a_ptsb"), 1)
                if i >= 2:
                    b = i - 2
                    dve.wait_ge(s("a_p"), b + 1)
                    link(nc.vector.reciprocal(rg[:, b:b + 1], rsum[:, b:b + 1]))
                    link(nc.vector.tensor_scalar(rg[:, b:b + 1], rg[:, b:b + 1], tg[0:T, 0:1], None, ALU.mult))
                    dve.wait_ge(s("a_y"), b + 1)
                    nc.vector.scalar_tensor_tensor(out=x[:, b, :], in0=PB[6 + b % 2][0:T, 0:D], scalar=rg[:, b:b + 1],
                                                   in1=x[:, b, :], op0=ALU.mult, op1=ALU.add).then_inc(s("a_res"), 1)
            dve.wait_ge(s("a_res"), NB)
            ln_dve("b")
            dve.wait_ge(s("b_lg"), 1)
            link(nc.vector.tensor_copy(lg[:], PB[4][0:T, 0:NB * NE].rearrange("p (b e) -> p b e", b=NB)))
            nc.vector.tensor_reduce(r1[:, 0, :], lg[:], AX.X, ALU.max).then_inc(s("b_mx"), 1)
            dve.wait_ge(s("b_mx"), 1)

            def over_b(ap):
                return ap.unsqueeze(1).to_broadcast([T, NB, ap.shape[-1]])

            link(nc.vector.tensor_tensor(key[:], lg[:], bc(r1[:, 0, :], NE), ALU.is_equal))
            link(nc.vector.tensor_tensor(key[:], key[:], over_b(consts[0:T, cs["rev16"]]), ALU.mult))
            link(nc.vector.tensor_reduce(r1[:, 2, :], key[:], AX.X, ALU.max))
            link(nc.vector.tensor_tensor(oh[:], key[:], bc(r1[:, 2, :], NE), ALU.is_equal))
            link(nc.vector.memset(pre[:, 0, :], 0.0))
            for b in range(1, NB):
                link(nc.vector.tensor_tensor(pre[:, b, :], pre[:, b - 1, :], oh[:, b - 1, :], ALU.add))
            nc.vector.tensor_tensor(key[:], oh[:], over_b(consts[0:T, cs["base16"]]), ALU.mult).then_inc(s("b_oh"), 1)
            dve.wait_ge(s("b_oh"), 1)
            link(nc.vector.tensor_reduce(r1[:, 3, :], key[:], AX.X, ALU.add))
            dve.wait_ge(s("b_pos"), 1)
            link(nc.vector.tensor_tensor(pos[:], PB[5][0:T, 0:NB * NE].rearrange("p (b e) -> p b e", b=NB), oh[:], ALU.mult))
            link(nc.vector.tensor_reduce(r1[:, 4, :], pos[:], AX.X, ALU.add))
            link(nc.vector.tensor_scalar(r1[:, 5, :], r1[:, 4, :], float(FULL), None, ALU.is_ge))
            link(nc.vector.tensor_tensor(r1[:, 6, :], r1[:, 4, :], r1[:, 3, :], ALU.add))
            link(nc.vector.scalar_tensor_tensor(out=r1[:, 7, :], in0=r1[:, 5, :], scalar=float(SKIP), in1=r1[:, 6, :],
                                                op0=ALU.mult, op1=ALU.add))
            nc.vector.tensor_copy(slot[:], r1[:, 7, :]).then_inc(s("b_slot"), 1)
            dve.wait_ge(s("b_sig"), 1)
            link(nc.vector.tensor_tensor(r1[:, 8, :], r1[:, 5, :], r1[:, 1, :], ALU.mult))
            link(nc.vector.tensor_tensor(oscale[:], oh[:], bc(r1[:, 8, :], NE), ALU.mult))
            for b in range(NB):
                nc.vector.tensor_scalar(xs[:, b, :], hN[:, b, :], r1[:, 1, b:b + 1], None, ALU.mult).then_inc(s("b_xs"), 1)
            dve.wait_ge(s("o_count"), 1)
            link(nc.vector.tensor_reduce(r1[0:1, 9, 0:1], PB[5][0:1, 0:NB], AX.X, ALU.add))
            nc.vector.tensor_copy(flag[:], r1[0:1, 9, 0:1]).then_inc(s("o_flag"), 1)
            for u in range(2 * FT):
                f, half = u // 2, u % 2
                dve.wait_ge(s("b_sil"), u + 1)
                nc.vector.tensor_tensor(hid[:, f, HALF * half:HALF * (half + 1)], sil[:, u % 2, 0:HALF],
                                        PB[(2 * u + 1) % 8][:, 0:HALF], ALU.mult).then_inc(s("b_hid"), 1)
            for i in range(NPAIR + 1):
                if i >= 1:
                    p = i - 1
                    dve.wait_ge(s("b_at"), p + 1)
                    if p >= 2:
                        dve.wait_ge(s("b_y"), p - 1)
                    nc.vector.tensor_copy(auT[:, p % 2], bank3(4, FT, 128)).then_inc(s("b_atsb"), 1)
                    dve.wait_ge(s("b_sd"), p + 1)
                    nc.vector.scalar_tensor_tensor(out=x[:, p, :], in0=PB[7][0:T, 0:D], scalar=tg[0:T, 2:3],
                                                   in1=x[:, p, :], op0=ALU.mult, op1=ALU.add).then_inc(s("b_sdres"), 1)
                if i < NPAIR:
                    dve.wait_ge(s("b_esil"), i + 1)
                    if i >= 2:
                        dve.wait_ge(s("b_at"), i - 1)
                    nc.vector.tensor_tensor(au[:, i % 2, :], sil[:, i % 2, :], PB[2 * (i % 2) + 1][:, :], ALU.mult) \
                        .then_inc(s("b_au"), 1)
            dve.wait_ge(s("b_gat"), 16 * NB)
            dve.wait_ge(s("b_sdres"), NB)
            nc.vector.scalar_tensor_tensor(out=x[:], in0=hN[:], scalar=tg[0:T, 2:3], in1=x[:],
                                           op0=ALU.mult, op1=ALU.add).then_inc(s("b_res"), 1)
            dve.wait_ge(s("b_res"), 1)
            over = dve.value_load(flag[0:1, 0:1], min_val=0, max_val=NT)
            with dve.If(over > 0):
                nc.vector.memset(ocol[:], 0.0).then_inc(s("o_res"), 1)
                with dve.Fori(0, NE) as e:
                    dve.wait_ge(s("o_res"), NB * e + 1)
                    nc.vector.tensor_copy(ocol[:], oscale[:, :, bass.ds(e, 1)].rearrange("t b e -> t (b e)")) \
                        .then_inc(s("o_col"), 1)
                    dve.wait_ge(s("o_col"), e + 1)
                    for b in range(NB):
                        dve.wait_ge(s("o_sil"), NB * e + (b + 1))
                        nc.vector.scalar_tensor_tensor(out=au[0:T, 0, :], in0=PB[1][0:T, :], scalar=ocol[:, b:b + 1],
                                                       in1=sil[0:T, 0, :], op0=ALU.mult, op1=ALU.mult).then_inc(s("o_au"), 1)
                        dve.wait_ge(s("o_at"), NB * e + (b + 1))
                        nc.vector.tensor_copy(auT[:, 0, :, 0:T], bank3(4, FT, T)).then_inc(s("o_atsb"), 1)
                        dve.wait_ge(s("o_y"), NB * e + (b + 1))
                        nc.vector.scalar_tensor_tensor(out=x[:, b, :], in0=PB[5][0:T, 0:D], scalar=tg[0:T, 2:3],
                                                       in1=x[:, b, :], op0=ALU.mult, op1=ALU.add).then_inc(s("o_res"), 1)
                dve.wait_ge(s("o_res"), NB * NE + 1)
            ln_dve("c")
            link(nc.vector.tensor_scalar(grow[:], brow["bo"][:], tg[0:T, 1:2], None, ALU.mult))
            link(nc.vector.tensor_tensor(x[:], x[:], grow[:].unsqueeze(1).to_broadcast([T, NB, D]), ALU.add))

            def normalise(b, bank, st):
                dve.wait_ge(s(st + "_av"), 4 * b + 4)
                if b >= 2:
                    dve.wait_ge(s(st + "_y"), b - 1)
                link(nc.vector.stream_shuffle(den, PB[bank][:, 0:NG * T], UPPER_HALF))
                link(nc.vector.reciprocal(den, den))
                nc.vector.tensor_tensor(attT[:, b % 2].rearrange("p g t -> p (g t)"), PB[bank][:, 0:NG * T], den, ALU.mult) \
                    .then_inc(s(st + "_att"), 1)

            def c_residual(b):
                dve.wait_ge(s("c_y"), b + 1)
                nc.vector.scalar_tensor_tensor(out=x[:, b, :], in0=PB[7][0:T, 0:D], scalar=tg[0:T, 1:2],
                                               in1=x[:, b, :], op0=ALU.mult, op1=ALU.add).then_inc(s("c_res"), 1)

            for n in range(NB * NH + 1):
                b, h = n // NH, n % NH
                if n < NB * NH:
                    dve.wait_ge(s("c_s"), n + 1)
                    if n >= 4:
                        dve.wait_ge(s("c_p"), n - 3)
                    nc.vector.tensor_reduce(nmx[:, n % 4, 0:1], PB[n % 2][0:T, 0:CTX], AX.X, ALU.max, negate=True) \
                        .then_inc(s("c_max"), 1)
                if n >= 1:
                    m = n - 1
                    dve.wait_ge(s("c_pt"), m + 1)
                    if m >= 8:
                        dve.wait_ge(s("c_av"), m // 4 - 1)
                    nc.vector.tensor_copy(pTq[0:KEYS, m % 8, :], PB[2 + m % 2][0:KEYS, 0:NJ * T]).then_inc(s("c_ptsb"), 1)
                if b >= 1 and h == 2:
                    normalise(b - 1, 4 + (b - 1) % 2, "c")
                if b >= 1 and h == 7:
                    c_residual(b - 1)
            normalise(NB - 1, 4 + (NB - 1) % 2, "c")
            c_residual(NB - 1)
            dve.wait_ge(s("c_res"), NB)
            ln_dve("d")

            def rotate(t, st):
                flat = t.rearrange("p k t -> p (k t)")
                tab = lambda n: consts[:, cs[n]].unsqueeze(1).to_broadcast([128, KT * NB, T])
                w3 = lambda ap: ap.rearrange("p (m t) -> p m t", t=T)
                link(nc.vector.stream_shuffle(rot, flat, SWAP_PAIRS))
                link(nc.vector.tensor_tensor(w3(flat), w3(flat), tab("cos"), ALU.mult))
                link(nc.vector.tensor_tensor(w3(rot), w3(rot), tab("sin"), ALU.mult))
                nc.vector.tensor_tensor(flat, flat, rot, ALU.add).then_inc(s("d_rot"), 1)

            dve.wait_ge(s("d_qsb"), 2 * KT)
            rotate(qT, "q")
            dve.wait_ge(s("d_ksb"), 2 * KT)
            dve.wait_ge(s("d_rot"), 1)
            rotate(krT, "k")

            def d_residual(b):
                dve.wait_ge(s("d_y"), b + 1)
                nc.vector.tensor_tensor(hN[:, b, :], PB[7][0:T, 0:D], hN[:, b, :], ALU.add).then_inc(s("d_x2"), 1)

            for n in range(4 * NB + 1):
                b, g = n // 4, n % 4
                if n < 4 * NB:
                    dve.wait_ge(s("d_s"), n + 1)
                    if n >= 2:
                        dve.wait_ge(s("d_pt"), n - 1)
                    sc4 = PB[n % 2][0:T, 0:4 * T].rearrange("p (h t) -> p h t", h=4)
                    link(nc.vector.tensor_reduce(nmx[:, n % 4, 0:4], sc4, AX.X, ALU.max))
                    nc.vector.tensor_tensor(prob4[:, n % 2, :].rearrange("p (h t) -> p h t", h=4), sc4,
                                            bc(nmx[:, n % 4, 0:4], T), ALU.subtract).then_inc(s("d_shift"), 1)
                if n >= 1:
                    m = n - 1
                    dve.wait_ge(s("d_pt"), m + 1)
                    if m >= 2:
                        dve.wait_ge(s("d_av"), m - 1)
                    nc.vector.tensor_copy(pT4[0:T, m % 2, :], PB[2 + m % 2][0:T, 0:4 * T]).then_inc(s("d_ptsb"), 1)
                if b >= 1 and g == 1:
                    normalise(b - 1, 4 + (b - 1) % 2, "d")
                if b >= 1 and g == 3:
                    d_residual(b - 1)
            normalise(NB - 1, 4 + (NB - 1) % 2, "d")
            d_residual(NB - 1)
            dve.wait_ge(s("e_std"), 1)
            link(nc.vector.reciprocal(rstd[:], std[:]))
            for b in range(NB):
                nc.vector.scalar_tensor_tensor(out=hN[:, b, :], in0=hN[:, b, :], scalar=rstd[:, b:b + 1], in1=brow["n1"][:],
                                               op0=ALU.mult, op1=ALU.mult).then_inc(s("e_hN"), 1)
            link(nc.vector.tensor_scalar(grow[:], brow["n2"][:], tg[0:T, 3:4], None, ALU.mult))
            dve.wait_ge(s("e_g"), 1)
            dve.wait_ge(s("ld_wc"), 16 * 13)
            link(nc.vector.tensor_tensor(gl[:], PB[4][0:T, 0:NB * (2 + NX)].rearrange("p (b e) -> p b e", b=NB),
                                         gbias[:].unsqueeze(1).to_broadcast([T, NB, 2 + NX]), ALU.add))
            link(nc.vector.tensor_reduce(r1[:, 0, :], gl[:, :, 0:2], AX.X, ALU.max))
            nc.vector.tensor_reduce(r1[:, 1, :], gl[:, :, 2:2 + EPG], AX.X, ALU.max)
            link(nc.vector.tensor_reduce(r1[:, 2, :], gl[:, :, 2 + EPG:], AX.X, ALU.max))
            link(nc.vector.tensor_tensor(gl[:, :, 0:2], gl[:, :, 0:2], bc(r1[:, 0, :], 2), ALU.subtract))
            nc.vector.tensor_tensor(gl[:, :, 2:2 + EPG], gl[:, :, 2:2 + EPG], bc(r1[:, 1, :], EPG), ALU.subtract)
            nc.vector.tensor_tensor(gl[:, :, 2 + EPG:], gl[:, :, 2 + EPG:], bc(r1[:, 2, :], EPG), ALU.subtract) \
                .then_inc(s("e_gx"), 1)
            dve.wait_ge(s("e_gexp"), 1)
            for i, (a, z) in enumerate(((0, 2), (2, 2 + EPG), (2 + EPG, 2 + NX))):
                last = nc.vector.tensor_reduce(r1[:, 3 + i, :], ge[:, :, a:z], AX.X, ALU.add)
            link(last)
            link(nc.vector.reciprocal(r1[:, 3:6, :], r1[:, 3:6, :]))
            for i, (a, z) in enumerate(((0, 2), (2, 2 + EPG), (2 + EPG, 2 + NX))):
                last = nc.vector.tensor_tensor(ge[:, :, a:z], ge[:, :, a:z], bc(r1[:, 3 + i, :], z - a), ALU.mult)
            link(last)
            link(nc.vector.tensor_tensor(r1[:, 6, :], ge[:, :, 0], ge[:, :, 1], ALU.is_ge))
            link(nc.vector.tensor_tensor(r1[:, 7, :], ge[:, :, 0], ge[:, :, 1], ALU.max))
            link(nc.vector.tensor_tensor(r1[:, 8, :], r1[:, 6, :], r1[:, 7, :], ALU.mult))
            link(nc.vector.tensor_tensor(r1[:, 9, :], r1[:, 7, :], r1[:, 8, :], ALU.subtract))
            nc.vector.tensor_tensor(ge[:, :, 2:2 + EPG], ge[:, :, 2:2 + EPG], bc(r1[:, 8, :], EPG), ALU.mult)
            link(nc.vector.tensor_tensor(ge[:, :, 2 + EPG:], ge[:, :, 2 + EPG:], bc(r1[:, 9, :], EPG), ALU.mult))
            pe_ = ge[:, :, 2:]
            o8, k8, s8 = oh[:, :, 0:NX], key[:, :, 0:NX], pos[:, :, 0:NX]
            rev8 = consts[0:T, cs["rev8"]].unsqueeze(1).to_broadcast([T, NB, NX])
            link(nc.vector.tensor_copy(s8, pe_))
            for r in range(2):
                link(nc.vector.tensor_reduce(r1[:, 0, :], s8, AX.X, ALU.max))
                link(nc.vector.tensor_tensor(k8, s8, bc(r1[:, 0, :], NX), ALU.is_equal))
                link(nc.vector.tensor_tensor(k8, k8, rev8, ALU.mult))
                link(nc.vector.tensor_reduce(r1[:, 1, :], k8, AX.X, ALU.max))
                link(nc.vector.tensor_tensor(o8, k8, bc(r1[:, 1, :], NX), ALU.is_equal))
                if r == 0:
                    link(nc.vector.tensor_tensor(we[:], o8, pe_, ALU.mult))
                    link(nc.vector.tensor_tensor(s8, s8, o8, ALU.subtract))
                    link(nc.vector.tensor_tensor(s8, s8, o8, ALU.subtract))
                else:
                    link(nc.vector.tensor_tensor(o8, o8, pe_, ALU.mult))
                    link(nc.vector.tensor_tensor(we[:], we[:], o8, ALU.add))
            for u in range(4 * FT):
                which, f, half = u // (2 * FT), u // 2 % FT, u % 2
                dve.wait_ge(s("e_sil"), u + 1)
                nc.vector.tensor_tensor(hid2[:, which, f, HALF * half:HALF * (half + 1)], sil[:, u % 2, 0:HALF],
                                        PB[(2 * u + 1) % 8][:, 0:HALF], ALU.mult).then_inc(s("e_hid"), 1)
            for b in range(NB):
                for i in range(5):
                    v = 5 * b + i
                    dve.wait_ge(s("e_down"), v + 1)
                    if i == 0:
                        nc.vector.tensor_tensor(hN[:, b, :], PB[v % 8][0:T, 0:D], hN[:, b, :], ALU.add) \
                            .then_inc(s("e_comb"), 1)
                    else:
                        for q in range(2):
                            e = 2 * (i - 1) + q
                            last = nc.vector.scalar_tensor_tensor(
                                out=hN[:, b, :], in0=PB[v % 8][0:T, D * q:D * q + D], scalar=we[:, b, e:e + 1],
                                in1=hN[:, b, :], op0=ALU.mult, op1=ALU.add)
                            if q == 0:
                                link(last)
                        last.then_inc(s("e_comb"), 1)
                    dve.wait_ge(s("e_comb"), v + 1)
                if b % 4 == 3:
                    dve.wait_ge(s("f_std"), b // 4 + 1)
                    link(nc.vector.reciprocal(rstd[:, b - 3:b + 1], std[:, b - 3:b + 1]))
                    for c in range(b - 3, b + 1):
                        link(nc.vector.scalar_tensor_tensor(out=hN[:, c, :], in0=hN[:, c, :], scalar=rstd[:, c:c + 1],
                                                            in1=grow[:], op0=ALU.mult, op1=ALU.mult))
                        nc.vector.tensor_tensor(x[:, c, :], x[:, c, :], hN[:, c, :], ALU.add).then_inc(s("f_out"), 1)

        @block.tensor
        def _(pe):
            def mm(o, l, r, start, stop):
                return nc.tensor.matmul(o, l, r, start=start, stop=stop)

            def ln_pe(st):
                for g in range(NB // 2):
                    pe.wait_ge(s(st + "_hN"), 2 * g + 2)
                    if g >= 2:
                        pe.wait_ge(s(st + "_hT"), g - 1)
                    for k in range(KT):
                        for bb in range(2):
                            at = (2 * k + bb) * T
                            last = nc.tensor.transpose(PB[g % 2][:, at:at + T], hN[:, 2 * g + bb, 128 * k:128 * k + 128],
                                                       ident[0:T, 0:T])
                    last.then_inc(s(st + "_tp"), 1)

            pe.wait_ge(s("ld_w0"), 64)
            pe.wait_ge(s("ld_const"), 16)
            for m in range(KT):
                for k in range(KT):
                    mm(PB[2][:, m * D:(m + 1) * D], wq0[:, k, 128 * m:128 * m + 128], wk0[:, k, :], k == 0, k == KT - 1)
            for v, (w, bias) in enumerate(((wk0, 0), (wq0, 1))):
                for m in range(KT):
                    for k in range(KT):
                        mm(PB[3][:, 2 * v + m:2 * v + m + 1], w[:, k, 128 * m:128 * m + 128], bqk[:, bias, k:k + 1],
                           k == 0, k == KT - 1)
            for k in range(KT):
                last = mm(PB[3][0:1, 4:5], bqk[:, 1, k:k + 1], bqk[:, 0, k:k + 1], k == 0, k == KT - 1)
            last.then_inc(s("a_fold"), 1)
            ln_pe("a")
            pe.wait_ge(s("a_foldsb"), 1)
            pe.wait_ge(s("a_hT"), NB // 2)
            for u in range(2 * KT):
                n, half = u // 2, u % 2
                if u >= 2:
                    pe.wait_ge(s("a_tsb"), u - 1)
                for m in range(KT):
                    last = mm(PB[4 + u % 2][:, 0:HALF], fold[:, m, 128 * n:128 * n + 128],
                              hT[:, m, HALF * half:HALF * (half + 1)], m == 0, m == KT - 1)
                last.then_inc(s("a_t"), 1)
            for half in range(2):
                for m in range(KT):
                    last = mm(PB[6 + half][0:1, 0:HALF], foldv[:, 2 + m:3 + m], hT[:, m, HALF * half:HALF * (half + 1)],
                              m == 0, m == KT - 1)
                last.then_inc(s("a_c"), 1)
            pe.wait_ge(s("a_tsb"), 2 * KT)
            pe.wait_ge(s("a_csb"), 2)
            pe.wait_ge(s("ld_ctxT"), 16 * KT)
            pe.wait_ge(s("ld_ctxN"), 16 * NJ)
            pe.wait_ge(s("set_ones"), 1)
            for i in range(NB + 2):
                if i < NB:
                    b = i
                    if b >= 2:
                        pe.wait_ge(s("a_max"), b - 1)
                    for n in range(KT):
                        mm(PB[b % 2][0:T, 0:CTX], tT[:, n, T * b:T * b + T], ctxT[:, n, b, 0:CTX], n == 0, False)
                    mm(PB[b % 2][0:T, 0:CTX], cT[0:1, T * b:T * b + T], ones[0:1, 0:CTX], False, True) \
                        .then_inc(s("a_s"), 1)
                if 1 <= i <= NB:
                    b = i - 1
                    pe.wait_ge(s("a_p"), b + 1)
                    if b >= 2:
                        pe.wait_ge(s("a_ptsb"), b - 1)
                    for j in range(NJ):
                        last = nc.tensor.transpose(PB[2 + b % 2][0:KEYS, T * j:T * j + T],
                                                   prob[:, b % NP_, KEYS * j:KEYS * j + KEYS], ident[0:T, 0:T])
                    last.then_inc(s("a_pt"), 1)
                    pe.wait_ge(s("a_ptsb"), b + 1)
                    if b >= 2:
                        pe.wait_ge(s("a_mixsb"), b - 1)
                    for d in range(KT):
                        for j in range(NJ):
                            last = mm(PB[4 + b % 2][:, T * d:T * d + T], ctxN[0:KEYS, b, j, 128 * d:128 * d + 128],
                                      pT[0:KEYS, b % 2, T * j:T * j + T], j == 0, j == NJ - 1)
                    last.then_inc(s("a_mix"), 1)
                if i >= 2:
                    b = i - 2
                    pe.wait_ge(s("a_mixsb"), b + 1)
                    if b >= 2:
                        pe.wait_ge(s("a_res"), b - 1)
                    for d in range(KT):
                        last = mm(PB[6 + b % 2][0:T, 0:D], mixT[:, b % 2, d, :], wv0[:, d, :], d == 0, d == KT - 1)
                    last.then_inc(s("a_y"), 1)
            ln_pe("b")
            pe.wait_ge(s("ld_wb"), 64)
            pe.wait_ge(s("b_hT"), NB // 2)
            for half in range(2):
                for k in range(KT):
                    last = mm(PB[2 + half][0:NE, 0:HALF], wr[:, k, :], hT[:, k, HALF * half:HALF * (half + 1)],
                              k == 0, k == KT - 1)
                last.then_inc(s("b_lgT"), 1)
            pe.wait_ge(s("b_lgTsb"), 2)
            for b in range(NB):
                last = nc.tensor.transpose(PB[4][0:T, NE * b:NE * b + NE], lgT[:, T * b:T * b + T], ident[0:NE, 0:NE])
            last.then_inc(s("b_lg"), 1)

            def shared_gu(u):
                f, half = u // 2, u % 2
                if u >= 4:
                    pe.wait_ge(s("b_hid"), u - 3)
                for w in range(2):
                    for k in range(KT):
                        last = mm(PB[(2 * u + w) % 8][:, 0:HALF], wgu[:, k, w, 128 * f:128 * f + 128],
                                  hT[:, k, HALF * half:HALF * (half + 1)], k == 0, k == KT - 1)
                last.then_inc(s("b_sgu"), 1)

            shared_gu(0)
            shared_gu(1)
            pe.wait_ge(s("b_oh"), 1)
            mm(PB[5][0:T, 0:NB * NE], consts[0:T, cs["lower"]], oh[:].rearrange("p b e -> p (b e)"), True, False)
            mm(PB[5][0:T, 0:NB * NE], ones[0:T, 0:T], pre[:].rearrange("p b e -> p (b e)"), False, True) \
                .then_inc(s("b_pos"), 1)
            pe.wait_ge(s("b_slot"), 1)
            mm(PB[5][0:1, 0:NB], ones[0:T, 0:1], r1[:, 5, :], True, True).then_inc(s("o_count"), 1)
            pe.wait_ge(s("o_flag"), 1)
            for u in range(2, 2 * FT):
                shared_gu(u)
            pe.wait_ge(s("b_hid"), 2 * FT)

            def slots_T(i):
                pe.wait_ge(s(f"b_xg{i // 2}"), 16)
                if i >= 1:
                    pe.wait_ge(s("b_xtsb"), i)
                for k in range(KT):
                    last = nc.tensor.transpose(PB[6][:, 128 * k:128 * k + 128], xg[:, i, 128 * k:128 * k + 128], ident)
                last.then_inc(s("b_xt"), 1)

            slots_T(0)
            for i in range(NPAIR + 1):
                if i < NPAIR:
                    pe.wait_ge(s("b_xtsb"), i + 1)
                    pe.wait_ge(s(f"ld_ring{i % RING}"), 64 * (i // RING + 1))
                    if i >= 2:
                        pe.wait_ge(s("b_au"), i - 1)
                    for w in range(2):
                        for k in range(KT):
                            for e in range(2):
                                at = (2 * k + w) * F
                                last = mm(PB[2 * (i % 2) + w][CAP * e:CAP * e + CAP, :], xgT[:, i % 2, k, CAP * e:CAP * e + CAP],
                                          ring[:, i % RING, e, at:at + F], k == 0, k == KT - 1)
                    last.then_inc(s("b_gu"), 1)
                if i + 1 < NPAIR:
                    slots_T(i + 1)
                if i >= 1:
                    p = i - 1
                    pe.wait_ge(s("b_au"), p + 1)
                    if p >= 1:
                        pe.wait_ge(s("b_atsb"), p)
                    for f in range(FT):
                        last = nc.tensor.transpose(PB[4][:, 128 * f:128 * f + 128], au[:, p % 2, 128 * f:128 * f + 128], ident)
                    last.then_inc(s("b_at"), 1)
                    if p >= 1:
                        pe.wait_ge(s("b_sdres"), p)
                    for f in range(FT):
                        last = mm(PB[7][0:T, 0:D], hid[:, f, T * p:T * p + T], wdn[:, f, :], f == 0, f == FT - 1)
                    last.then_inc(s("b_sd"), 1)
                    pe.wait_ge(s("b_atsb"), p + 1)
                    if p >= 1:
                        pe.wait_ge(s("b_ysb"), p)
                    for f in range(FT):
                        for e in range(2):
                            last = mm(PB[5][CAP * e:CAP * e + CAP, 0:D], auT[:, p % 2, f, CAP * e:CAP * e + CAP],
                                      ring[:, p % RING, e, GU + D * f:GU + D * f + D], f == 0, f == FT - 1)
                    last.then_inc(s("b_y"), 1)
            over = pe.value_load(flag[0:1, 0:1], min_val=0, max_val=NT)
            with pe.If(over > 0):
                pe.wait_ge(s("b_ysb"), NPAIR)
                with pe.Fori(0, NE) as e:
                    pe.wait_ge(s("o_ld"), 32 * e + 32)
                    pe.wait_ge(s("o_col"), e + 1)
                    for b in range(NB):
                        pe.wait_ge(s("o_res"), NB * e + (b + 1))
                        for w in range(2):
                            for k in range(KT):
                                at = (2 * k + w) * F
                                last = mm(PB[w][0:T, :], hT[:, k, T * b:T * b + T], ring[:, 0, 0, at:at + F],
                                          k == 0, k == KT - 1)
                        last.then_inc(s("o_gu"), 1)
                        pe.wait_ge(s("o_au"), NB * e + (b + 1))
                        for f in range(FT):
                            last = nc.tensor.transpose(PB[4][:, T * f:T * f + T], au[0:T, 0, 128 * f:128 * f + 128],
                                                       ident[0:T, 0:T])
                        last.then_inc(s("o_at"), 1)
                        pe.wait_ge(s("o_atsb"), NB * e + (b + 1))
                        for f in range(FT):
                            last = mm(PB[5][0:T, 0:D], auT[:, 0, f, 0:T], ring[:, 0, 0, GU + D * f:GU + D * f + D],
                                      f == 0, f == FT - 1)
                        last.then_inc(s("o_y"), 1)
            ln_pe("c")
            pe.wait_ge(s("ld_wc"), 16 * 13)

            def queries(st, w):
                pe.wait_ge(s(st + "_hT"), NB // 2)
                for u in range(2 * KT):
                    n, half = u // 2, u % 2
                    if u >= 2:
                        pe.wait_ge(s(st + "_qsb"), u - 1)
                    for m in range(KT):
                        last = mm(PB[4 + u % 2][:, 0:HALF], w[:, m, 128 * n:128 * n + 128],
                                  hT[:, m, HALF * half:HALF * (half + 1)], m == 0, m == KT - 1)
                    last.then_inc(s(st + "_q"), 1)

            def kv_part(b, i):
                if 5 * b + i >= 1:
                    pe.wait_ge(s("c_prsb"), 5 * b + i)
                for k in range(KT):
                    if i < KT:
                        last = mm(PB[6][:, 0:CPAD], wc[:, 1, k, 128 * i:128 * i + 128], ctxT[:, k, b, :], k == 0, k == KT - 1)
                    else:
                        j = i - KT
                        last = mm(PB[6][0:KEYS, 0:D], ctxT[:, k, b, KEYS * j:KEYS * j + KEYS], wc[:, 2, k, :],
                                  k == 0, k == KT - 1)
                last.then_inc(s("c_pr"), 1)

            def out_projection(b, st, w):
                pe.wait_ge(s(st + "_att"), b + 1)
                if b >= 1:
                    pe.wait_ge(s("c_res" if st == "c" else "d_x2"), b)
                for g in range(NG):
                    last = mm(PB[7][0:T, 0:D], attT[:, b % 2, g, :], w[:, g, :], g == 0, g == NG - 1)
                last.then_inc(s(st + "_y"), 1)

            queries("c", wc[:, 0])
            for i in range(5):
                kv_part(0, i)
            pe.wait_ge(s("c_qsb"), 2 * KT)
            for n in range(NB * NH + 2):
                b, h = n // NH, n % NH
                if n < NB * NH:
                    if h == 0:
                        pe.wait_ge(s("c_qbd"), b + 1)
                        pe.wait_ge(s("c_prsb"), 5 * b + 5)
                    if n >= 2:
                        pe.wait_ge(s("c_p"), n - 1)
                    mm(PB[n % 2][0:T, 0:CTX], qbd[:, b % 2, h // 8, T * (h % 8):T * (h % 8) + T], kT[:, b % 2, h // 8, 0:CTX],
                       True, True).then_inc(s("c_s"), 1)
                if 1 <= n <= NB * NH:
                    m = n - 1
                    pe.wait_ge(s("c_p"), m + 1)
                    if m >= 2:
                        pe.wait_ge(s("c_ptsb"), m - 1)
                    for j in range(NJ):
                        last = nc.tensor.transpose(PB[2 + m % 2][0:KEYS, T * j:T * j + T],
                                                   prob[:, m % 4, KEYS * j:KEYS * j + KEYS], ident[0:T, 0:T])
                    last.then_inc(s("c_pt"), 1)
                if n >= 2 and (n - 2) % 4 == 3:
                    quad = (n - 2) // 4
                    bq, g = quad // NG, quad % NG
                    pe.wait_ge(s("c_ptsb"), 4 * quad + 4)
                    if g == 0 and bq >= 2:
                        pe.wait_ge(s("c_att"), bq - 1)
                    for j in range(NJ):
                        for q in range(4):
                            hh = 4 * g + q
                            last = mm(PB[4 + bq % 2][32 * q:32 * q + 32, T * g:T * g + T],
                                      vpad[0:KEYS, bq % 2, j, 32 * hh:32 * hh + 32],
                                      pTq[0:KEYS, (4 * quad + q) % 8, T * j:T * j + T], j == 0, j == NJ - 1)
                    last.then_inc(s("c_av"), 1)
                if b + 1 < NB and h in KV_AT:
                    kv_part(b + 1, KV_AT.index(h))
                if 1 <= b < NB and h == 4:
                    out_projection(b - 1, "c", wo[:, 0])
            out_projection(NB - 1, "c", wo[:, 0])
            ln_pe("d")
            pe.wait_ge(s("ld_wd"), 16 * 14)
            queries("d", wq2)
            for half in range(2):
                for k in range(KT):
                    last = mm(PB[6 + half][:, 0:HALF], wkvc[:, k, :], hT[:, k, HALF * half:HALF * (half + 1)],
                              k == 0, k == KT - 1)
                last.then_inc(s("d_kvc"), 1)
            pe.wait_ge(s("d_kvcsb"), 2)
            pe.wait_ge(s("d_qsb"), 2 * KT)
            for u in range(2 * KT):
                n, half = u // 2, u % 2
                if u >= 2:
                    pe.wait_ge(s("d_ksb"), u - 1)
                mm(PB[4 + u % 2][:, 0:HALF], wkv2[:, 0, 128 * n:128 * n + 128], kvcT[:, HALF * half:HALF * (half + 1)],
                   True, True).then_inc(s("d_k"), 1)

            def values(b):
                if b >= 1:
                    pe.wait_ge(s("d_vsb"), b)
                mm(PB[6][0:T, 0:D], kvcT[:, T * b:T * b + T], wkv2[:, 1, :], True, True).then_inc(s("d_v"), 1)

            values(0)
            pe.wait_ge(s("d_rot"), 2)
            for n in range(4 * NB + 2):
                b, g = n // 4, n % 4
                if n < 4 * NB:
                    if g == 0:
                        pe.wait_ge(s("d_qbd"), b + 1)
                    if n >= 2:
                        pe.wait_ge(s("d_shift"), n - 1)
                    for q in range(4):
                        h = 4 * g + q
                        last = mm(PB[n % 2][0:T, T * q:T * q + T], qbd[:, b % 2, h // 8, T * (h % 8):T * (h % 8) + T],
                                  krT[:, h // 8, T * b:T * b + T], True, True)
                    last.then_inc(s("d_s"), 1)
                if 1 <= n <= 4 * NB:
                    m = n - 1
                    pe.wait_ge(s("d_p"), m + 1)
                    if m >= 2:
                        pe.wait_ge(s("d_ptsb"), m - 1)
                    for q in range(4):
                        last = nc.tensor.transpose(PB[2 + m % 2][0:T, T * q:T * q + T], prob4[:, m % 2, T * q:T * q + T],
                                                   ident[0:T, 0:T])
                    last.then_inc(s("d_pt"), 1)
                if n >= 2:
                    m = n - 2
                    bq, g2 = m // 4, m % 4
                    pe.wait_ge(s("d_ptsb"), m + 1)
                    if g2 == 0:
                        pe.wait_ge(s("d_vsb"), bq + 1)
                        if bq >= 2:
                            pe.wait_ge(s("d_att"), bq - 1)
                    for q in range(4):
                        hh = 4 * g2 + q
                        last = mm(PB[4 + bq % 2][32 * q:32 * q + 32, T * g2:T * g2 + T],
                                  vpad[0:T, bq % 2, 0, 32 * hh:32 * hh + 32], pT4[0:T, m % 2, T * q:T * q + T], True, True)
                    last.then_inc(s("d_av"), 1)
                if g == 1 and b + 1 < NB:
                    values(b + 1)
                if 1 <= b < NB and g == 2:
                    out_projection(b - 1, "d", wo[:, 1])
            out_projection(NB - 1, "d", wo[:, 1])
            for g in range(NB // 2):
                pe.wait_ge(s("e_hN"), 2 * g + 2)
                if g >= 2:
                    pe.wait_ge(s("e_hT"), g - 1)
                for k in range(KT):
                    for bb in range(2):
                        at = (2 * k + bb) * T
                        last = nc.tensor.transpose(PB[g % 2][:, at:at + T], hN[:, 2 * g + bb, 128 * k:128 * k + 128],
                                                   ident[0:T, 0:T])
                last.then_inc(s("e_tp"), 1)
            pe.wait_ge(s("e_hT"), NB // 2)
            for half in range(2):
                for k in range(KT):
                    last = mm(PB[2 + half][0:2 + NX, 0:HALF], wge[:, k, :], hT[:, k, HALF * half:HALF * (half + 1)],
                              k == 0, k == KT - 1)
                last.then_inc(s("e_gT"), 1)
            pe.wait_ge(s("e_gTsb"), 2)
            for b in range(NB):
                n = 2 + NX
                last = nc.tensor.transpose(PB[4][0:T, n * b:n * b + n], row_T[0:n, T * b:T * b + T], ident[0:n, 0:n])
            last.then_inc(s("e_g"), 1)
            for u in range(4 * FT):
                which, f, half = u // (2 * FT), u // 2 % FT, u % 2
                if u == 2:
                    pe.wait_ge(s("e_gx"), 1)
                if u >= 4:
                    pe.wait_ge(s("e_hid"), u - 3)
                for w in range(2):
                    for k in range(KT):
                        last = mm(PB[(2 * u + w) % 8][:, 0:HALF], wgu2[:, which, k, F * w + 128 * f:F * w + 128 * f + 128],
                                  hT[:, k, HALF * half:HALF * (half + 1)], k == 0, k == KT - 1)
                last.then_inc(s("e_gu"), 1)
            pe.wait_ge(s("e_hid"), 4 * FT)
            for b in range(NB):
                for i in range(5):
                    v = 5 * b + i
                    if v >= 8:
                        pe.wait_ge(s("e_comb"), v - 7)
                    for f in range(FT):
                        if i == 0:
                            last = mm(PB[v % 8][0:T, 0:D], hid2[:, 0, f, T * b:T * b + T], wdn[:, f, :], f == 0, f == FT - 1)
                        else:
                            last = mm(PB[v % 8][0:T, :], hid2[:, 1, f, T * b:T * b + T],
                                      w2[:, f, 2 * (i - 1):2 * i, :].rearrange("p e d -> p (e d)"), f == 0, f == FT - 1)
                    last.then_inc(s("e_down"), 1)


def kernel(**inputs):
    import concourse.bacc as bacc
    from concourse.bass_utils import run_bass_kernel_spmd
    nc = bacc.Bacc("TRN2", target_bir_lowering=False, num_devices=1)
    arrays = {n: np.ascontiguousarray(v) for n, v in inputs.items()}
    arrays["x"] = np.ascontiguousarray(arrays["x"].transpose(1, 0, 2))
    context = arrays.pop("ctx_1024")
    arrays["ctx"] = context
    arrays["ctxT"] = np.ascontiguousarray(context.transpose(2, 0, 1))
    arrays["mask"] = np.ascontiguousarray(arrays.pop("mask_BxSxS2_bk1").transpose(1, 0, 2))
    for n in ("L0_xattn_Wv", "L0_ffn_w_router", "L0_ffn_w_gate", "L0_ffn_w_up", "L0_ffn_w_down",
              "L1_xattn_wq", "L1_xattn_wk", "L1_xattn_wv", "L1_xattn_wo"):
        arrays[n + "T"] = np.ascontiguousarray(arrays.pop(n).T)

    arrays["bqk"] = np.ascontiguousarray(
        np.stack([arrays.pop("L0_xattn_bq"), arrays.pop("L0_xattn_bk")]).reshape(2, KT, 128).transpose(2, 0, 1))

    cs, ncols = const_slices()
    c = np.zeros((128, ncols), np.float32)
    c[:, cs["ident"]] = np.eye(128)
    c[:, cs["headmask"]] = np.arange(128)[:, None] // DH == np.arange(8)[None, :]
    c[:T, cs["lower"]] = np.arange(T)[:, None] < np.arange(T)[None, :]
    freq = (1.0 / 10000.0 ** (np.arange(0, DH, 2, dtype=np.float32) / DH)).astype(np.float32)
    angle = (np.arange(T, dtype=np.float32)[None, :] * freq[:, None]).astype(np.float32)
    row = np.arange(128) % DH // 2
    c[:, cs["cos"]] = np.cos(angle)[row]
    c[:, cs["sin"]] = np.sin(angle)[row] * np.where(np.arange(128) % 2 == 0, -1.0, 1.0)[:, None]
    c[:, cs["rev16"]] = NE - np.arange(NE)
    c[:, cs["base16"]] = CAP * np.arange(NE)
    c[:, cs["rev8"]] = NX - np.arange(NX)
    arrays["consts"] = c

    A = {}
    for n, a in arrays.items():
        A[n] = nc.dram_tensor("in_" + n, a.shape, mybir.dt.from_np(a.dtype), kind="ExternalInput").ap()
    A["xs_dram"] = nc.dram_tensor("xs_dram", (NSLOT, D), mybir.dt.float32).ap()
    A["y_dram"] = nc.dram_tensor("y_dram", (NSLOT, D), mybir.dt.float32).ap()
    out = nc.dram_tensor("out", (NB, T, D), mybir.dt.float32, kind="ExternalOutput").ap()
    build(nc, A, out)
    r = run_bass_kernel_spmd(nc, [{"in_" + n: a for n, a in arrays.items()}], core_ids=[0])
    return r.results[0]["out"]
```

```python
import numpy as np
import concourse.bass as bass
from concourse import mybir
from contextlib import ExitStack

NB, T, D = 8, 100, 256
CTX = 361
KT = D // 128
KEYS = 121
NJ = 3
CPAD = KEYS * NJ
NT = NB * T
HALF = NT // 2
NH, DH = 16, 16
NG = NH // 4
F = 512
FT = F // 128
NE, CAP = 16, 64
NPAIR = NE // 2
NSLOT = NE * CAP
FULL = CAP
SKIP = 1 << 20
NX, EPG = 8, 4
DC = 64
LN_EPS, RMS_EPS = 1e-5, 1e-6
NEG = -1000000000.0
RING = 3
LAST_IN_CTX = max(i for i in range(NPAIR) if i % RING == RING - 1)
SB = [0, 1, 7]
KV_AT = [1, 4, 8, 11, 14]
SWAP_PAIRS = [i ^ 1 for i in range(32)]
UPPER_HALF = [16 + i % 16 for i in range(32)]

CONSTS = dict(ident=128, headmask=8, lower=T, cos=T, sin=T, rev16=NE, base16=NE, rev8=NX)


def const_slices():
    at, out = 0, {}
    for name, width in CONSTS.items():
        out[name] = slice(at, at + width)
        at += width
    return out, at


def build(nc, A, out):
    f32, i32, u8 = mybir.dt.float32, mybir.dt.int32, mybir.dt.uint8
    ALU, ACT, AX = mybir.AluOpType, mybir.ActivationFunctionType, mybir.AxisListType

    ctx = ExitStack()
    with ctx:
        def sb(name, shape, dt=f32):
            return ctx.enter_context(nc.sbuf_tensor(name, shape, dt))

        def sem(name):
            return ctx.enter_context(nc.semaphore(name))

        cs, ncols = const_slices()
        consts = sb("consts", [128, ncols])
        ident = consts[:, cs["ident"]]
        ones = sb("ones", [128, CPAD])
        zero_rows = sb("zero_rows", [128, D])
        minus_half = sb("minus_half", [T, NB])
        gates = sb("gates", [128, 4])
        tg = sb("tg", [128, 4])
        x = sb("x", [T, NB, D])
        hN = sb("hN", [T, NB, D])
        hT = sb("hT", [128, KT, NT])
        bn6 = sb("bn6", [T, NB, 6])
        mv = sb("mv", [T, NB, 2])
        std = sb("std", [T, NB])
        rstd = sb("rstd", [T, NB])
        GU = KT * 2 * F
        EW = GU + FT * D
        ctxbuf = sb("ctxbuf", [128, 2 * EW])
        ctxT = ctxbuf[:, 0:KT * NB * CPAD].rearrange("p (k b c) -> p k b c", k=KT, b=NB)
        brow = {n: sb("row_" + n, [T, D]) for n in ("bv", "bo", "n1", "n2")}
        grow = sb("grow", [T, D])
        big = sb("big", [128, NB * NJ * D + 256])
        ctxN = big[:, 0:NB * NJ * D].rearrange("p (b j d) -> p b j d", b=NB, j=NJ)
        arena = sb("arena", [128, 6656 + 320])

        def carve(start, *dims, rows=128):
            n = int(np.prod(dims))
            names = "abcd"[:len(dims)]
            part = arena[0:rows, start:start + n]
            if len(dims) == 1:
                return part
            return part.rearrange(f"p ({' '.join(names)}) -> p {' '.join(names)}",
                                  **dict(zip(names[:-1], dims[:-1])))

        W = KT * D
        wq0 = carve(0, KT, D)
        wk0 = carve(W, KT, D)
        wv0 = carve(2 * W, KT, D)
        fold = carve(3 * W, KT, D)
        keep = carve(4 * W, 2, CTX, rows=T)
        drop = carve(4 * W + 2 * CTX, 2, CTX, rows=T)
        sc = carve(4 * W + 4 * CTX, 2, CTX, rows=T)
        bqk = sb("bqk", [128, 2, KT])
        foldv = sb("foldv", [128, 4])
        fold0 = sb("fold0", [1, 1])
        tT = sb("tT", [128, KT, NT])
        sil = sb("sil", [128, 2, F])
        row_T = sil[:].rearrange("p a b -> p (a b)")
        cT = row_T[0:1, 0:NT]
        ccol = sb("ccol", [T, NB])
        mask8 = sb("mask8", [T, NB, CTX], u8)
        NP_ = 4
        prob = sb("prob", [T, NP_, CPAD])
        nmx = sb("nmx", [T, 4, NB])
        rsum = sb("rsum", [T, NB])
        rg = sb("rg", [T, NB])
        pT = carve(4 * W + 6 * CTX, 2, NJ * T)
        mixT = carve(4 * W + 6 * CTX + 2 * NJ * T, 2, KT, T)
        mix = carve(4 * W + 6 * CTX + 2 * NJ * T + 2 * D, 2, D, rows=T)
        ring = sb("ring", [128, RING - 1, 2, EW])
        pairs = [ring[:, i] for i in range(RING - 1)] + [ctxbuf[:].rearrange("p (e n) -> p e n", e=2)]
        wr = sb("wr", [128, KT, NE])
        wgu = sb("wgu", [128, KT, 2, F])
        wdn = sb("wdn", [128, FT, D])
        hid = big[:, 0:FT * NT].rearrange("p (f t) -> p f t", f=FT)
        lgT = row_T[0:NE, 0:NT]
        lg = sb("lg", [T, NB, NE])
        oh = sb("oh", [T, NB, NE])
        key = sb("key", [T, NB, NE])
        pre = sb("pre", [T, NB, NE])
        pos = sb("pos", [T, NB, NE])
        r1 = sb("r1", [T, 12, NB])
        slot = sb("slot", [T, NB], i32)
        oscale = sb("oscale", [T, NB, NE])
        ocol = sb("ocol", [T, NB])
        flag = sb("flag", [1, 1], i32)
        xs = carve(0, NB, D, rows=T)
        xg = carve(8 * D, NPAIR, D)
        au = carve(16 * D, 2, F)
        auT = carve(20 * D, 2, FT, 128)
        yb = carve(24 * D, 2, D)
        wc = sb("wc", [128, 3, KT, D])
        wo = sb("wo", [128, 2, NG, D])
        qT = tT
        kflat = big[:, 0:KT * NT]
        kT = kflat[:, 0:2 * KT * CPAD].rearrange("p (u k c) -> p u k c", u=2, k=KT)
        krT = kflat.rearrange("p (k t) -> p k t", k=KT)
        vpad = carve(0, 2, NJ, NH * 32)
        qbd = carve(2 * NJ * NH * 32, 2, KT, 8 * T)
        den = big[:, 1600:1600 + NG * T]
        attT = big[:, 2000:2000 + 2 * NG * T].rearrange("p (u g t) -> p u g t", u=2, g=NG)
        xgT = big[:, FT * NT:FT * NT + 2 * KT * 128].rearrange("p (u k t) -> p u k t", u=2, k=KT)

        pTq = big[:, 2800:2800 + 8 * NJ * T].rearrange("p (u n) -> p u n", u=8)
        wflat = wgu[:].rearrange("p k w f -> p (k w f)")
        wq2 = wflat[:, 0:W].rearrange("p (k n) -> p k n", k=KT)
        wkvc = wflat[:, W:W + KT * 2 * DC].rearrange("p (k n) -> p k n", k=KT)
        wkv2 = wflat[:, 2 * W:2 * W + 2 * D].rearrange("p (w n) -> p w n", w=2)
        wge = wflat[:, 3 * W:3 * W + KT * (2 + NX)].rearrange("p (k n) -> p k n", k=KT)
        rflat = ring[:].rearrange("p r e n -> p (r e n)")
        w2 = rflat[:, 0:FT * NX * D].rearrange("p (f e d) -> p f e d", f=FT, e=NX)
        wgu2 = rflat[:, FT * NX * D:FT * NX * D + 2 * KT * 2 * F].rearrange("p (s k n) -> p s k n", s=2, k=KT)
        kvcT = big[:, 3600:3600 + NT]
        rot = big[:, 4400:4400 + KT * NT]
        prob4 = prob[:].rearrange("t u n -> t (u n)")[:, 0:3 * 4 * T].rearrange("t (u n) -> t u n", u=3)
        pT4 = big[:, 2800:2800 + 2 * 4 * T].rearrange("p (u n) -> p u n", u=2)
        hid2 = big[:, 0:2 * FT * NT].rearrange("p (s f t) -> p s f t", s=2, f=FT)
        gbias = sb("gbias", [T, 2 + NX])
        gl = sb("gl", [T, NB, 2 + NX])
        ge = sb("ge", [T, NB, 2 + NX])
        we = sb("we", [T, NB, NX])

        PB = [ctx.enter_context(nc.psum_tensor(f"pb{i}", [128, 512], f32)) for i in range(8)]

        def bank3(i, a, n, rows=128):
            return PB[i][0:rows, 0:a * n].rearrange("p (a n) -> p a n", a=a)

        S = {}

        def s(name):
            if name not in S:
                S[name] = sem(name)
            return S[name]

        names = ["ld_x", "ld_const", "ld_small", "ld_w0", "ld_ctxT", "ld_ctxN", "ld_mask", "ld_wb", "ld_wc",
                 "dve_step", "act_step", "stats", "set_ones", "set_zero", "set_pads", "stored"]
        names += ["n_var", "n_std", "n_hN", "n_tp", "n_hT"]
        turn = "abcdef".index
        names += ["a_fold", "a_foldsb", "a_t", "a_tsb", "a_c", "a_csb", "a_mask", "a_s", "a_max", "a_p", "a_cc", "a_ccsb", "a_pt",
                  "a_ptsb", "a_mix", "a_mixsb", "a_mt", "a_mtsb", "a_y", "a_res"]
        names += ["ld_ring0", "ld_ring1", "ld_ring2", "b_zero", "b_lgT", "b_lgTsb", "b_lg", "b_mx", "b_sig", "b_oh", "b_pos", "b_slot",
                  "b_xs", "b_scat", "b_xg0", "b_xg1", "b_xg2", "b_xg3", "b_sgu", "b_sil", "b_hid", "b_xt", "b_xtsb",
                  "b_gu", "b_esil", "b_au", "b_at", "b_atsb", "b_sd", "b_sdres", "b_y", "b_ysb", "b_yst0", "b_yst1",
                  "b_clear", "b_gat0", "b_gat1", "b_res"]
        names += ["o_count", "o_flag", "o_ld", "o_gu", "o_sil", "o_au", "o_col", "o_at", "o_atsb", "o_y", "o_res"]
        names += ["ld_wd", "c_vones", "c_q", "c_qsb", "c_qbd", "c_pr", "c_prsb", "c_s", "c_max", "c_p", "c_pt", "c_ptsb",
                  "c_av", "c_att", "c_y", "c_res"]
        names += ["d_q", "d_qsb", "d_kvc", "d_kvcsb", "d_k", "d_ksb", "d_swap", "d_cos", "d_rot", "d_qbd", "d_v", "d_vsb", "d_s", "d_shift", "d_p",
                  "d_pt", "d_ptsb", "d_av", "d_att", "d_y", "d_x2", "d_sq", 
                  "e_gT", "e_gTsb", "e_g", "e_gx", "e_gexp", "e_gu", "e_sil", "e_hid", "e_down", "e_comb", "f_sq",
                  "f_out"]
        for n in names:
            s(n)

        xs_dram, y_dram = A["xs_dram"], A["y_dram"]
        block = ctx.enter_context(nc.Block())

        @block.sync
        def _(sp):
            sp.dma_start(x[:], A["x"]).then_inc(s("ld_x"), 16)
            sp.dma_start(consts[:], A["consts"]).then_inc(s("ld_const"), 16)
            for i, n in enumerate(("L0_xattn_Wq", "L0_xattn_Wk", "L0_xattn_WvT")):
                sp.dma_start((wq0, wk0, wv0)[i][:], A[n].rearrange("(k p) n -> p k n", p=128)).then_inc(s("ld_w0"), 16)
            sp.dma_start(bqk[:], A["bqk"]).then_inc(s("ld_w0"), 16)
            for i, n in enumerate(("g_xattn", "g_ffn")):
                sp.dma_start(gates[:, 2 * i:2 * i + 2], A[n].partition_broadcast(128)).then_inc(s("ld_small"), 16)
            for n, w in (("bv", "L0_xattn_bv"), ("bo", "L1_xattn_bo"), ("n1", "L1_ffn_norm1_w"), ("n2", "L1_ffn_norm2_w")):
                sp.dma_start(brow[n][:], A[w].partition_broadcast(T)).then_inc(s("ld_small"), 16)
            sp.dma_start(mask8[:], A["mask"]).then_inc(s("ld_mask"), 16)
            for k in range(KT):
                sp.dma_start(ctxT[:, k, :, 0:CTX], A["ctxT"][128 * k:128 * k + 128]).then_inc(s("ld_ctxT"), 16)
            sp.wait_ge(s("set_pads"), 1)
            for j in range(NJ):
                n = min(KEYS, CTX - KEYS * j)
                sp.dma_start(ctxN[0:n, :, j, :], A["ctx"][:, KEYS * j:KEYS * j + n, :].rearrange("b p d -> p b d")) \
                    .then_inc(s("ld_ctxN"), 16)
            sp.wait_ge(s("set_zero"), 1)
            for i in range(NPAIR):
                sp.dma_start(xs_dram[128 * i:128 * i + 128, :], zero_rows[:]).then_inc(s("b_zero"), 16)
            sp.dma_start(wr[:], A["L0_ffn_w_routerT"].rearrange("(k p) n -> p k n", p=128)).then_inc(s("ld_wb"), 16)
            for i, n in enumerate(("L0_ffn_w_gateT", "L0_ffn_w_upT")):
                sp.dma_start(wgu[:, :, i, :], A[n].rearrange("(k p) n -> p k n", p=128)).then_inc(s("ld_wb"), 16)
            sp.dma_start(wdn[:], A["L0_ffn_w_downT"].rearrange("(k p) n -> p k n", p=128)).then_inc(s("ld_wb"), 16)

            for i, n in enumerate(("L1_xattn_wqT", "L1_xattn_wkT", "L1_xattn_wvT")):
                sp.dma_start(wc[:, i], A[n].rearrange("(k p) n -> p k n", p=128)).then_inc(s("ld_wc"), 16)
            for i, n in enumerate(("L1_xattn_woT", "L1_ffn_Wo")):
                for j in range(4):
                    sp.dma_start(wo[32 * j:32 * j + DH, i], A[n].rearrange("(g j d) n -> j d g n", j=4, d=DH)[j]) \
                        .then_inc(s("ld_wc"), 16)
            sp.dma_start(gbias[:, 0:2], A["L1_ffn_group_bias"].partition_broadcast(T)).then_inc(s("ld_wc"), 16)
            sp.dma_start(gbias[:, 2:], A["L1_ffn_expert_bias"].partition_broadcast(T)).then_inc(s("ld_wc"), 16)

            def load_pair(i):
                for e in range(2):
                    sp.dma_start(pairs[i % RING][:, e, 0:GU].rearrange("p (k n) -> p k n", k=KT),
                                 A["L0_ffn_gate_up_proj"][2 * i + e].rearrange("(k p) n -> p k n", p=128)) \
                        .then_inc(s(f"ld_ring{i % RING}"), 16)
                    sp.dma_start(pairs[i % RING][:, e, GU:].rearrange("p (k n) -> p k n", k=FT),
                                 A["L0_ffn_down_proj"][2 * i + e].rearrange("(k p) n -> p k n", p=128)) \
                        .then_inc(s(f"ld_ring{i % RING}"), 16)

            for i in range(RING - 1):
                load_pair(i)
            sp.wait_ge(s("a_s"), NB)
            load_pair(RING - 1)
            sp.wait_ge(s("b_scat"), 16 * NB)
            for g in range(4):
                sp.dma_start(xg[:, 2 * g:2 * g + 2, :],
                             xs_dram[256 * g:256 * g + 256, :].rearrange("(i p) d -> p i d", p=128)) \
                    .then_inc(s(f"b_xg{g}"), 16)
            for i in range(NPAIR):
                sp.wait_ge(s("b_ysb"), i + 1)
                sp.dma_start(y_dram[128 * i:128 * i + 128, :], yb[:, i % 2, :]).then_inc(s(f"b_yst{i % 2}"), 16)
                if i + RING < NPAIR:
                    load_pair(i + RING)
                if i == LAST_IN_CTX:
                    sp.wait_ge(s("set_pads"), 2)
                    for k in range(KT):
                        sp.dma_start(ctxT[:, k, :, 0:CTX], A["ctxT"][128 * k:128 * k + 128]).then_inc(s("ld_ctxT"), 16)
            sp.wait_ge(s("b_y"), NPAIR)
            sp.wait_ge(s("o_flag"), 1)
            over = sp.value_load(flag[0:1, 0:1], min_val=0, max_val=NT)
            with sp.If(over > 0):
                with sp.Fori(0, NE) as e:
                    sp.wait_ge(s("o_res"), NB * e + 1)
                    sp.dma_start(ring[:, 0, 0, 0:GU].rearrange("p (k n) -> p k n", k=KT),
                                 A["L0_ffn_gate_up_proj"][bass.ds(e, 1)].rearrange("e (k p) n -> p (e k) n", p=128)) \
                        .then_inc(s("o_ld"), 16)
                    sp.dma_start(ring[:, 0, 0, GU:].rearrange("p (k n) -> p k n", k=FT),
                                 A["L0_ffn_down_proj"][bass.ds(e, 1)].rearrange("e (k p) n -> p (e k) n", p=128)) \
                        .then_inc(s("o_ld"), 16)
                sp.wait_ge(s("o_res"), NB * NE + 1)
            sp.wait_ge(s("b_y"), NPAIR)
            sp.wait_ge(s("b_clear"), 2)
            sp.dma_start(wq2, A["L1_ffn_Wq"].rearrange("(k p) n -> p k n", p=128)).then_inc(s("ld_wd"), 16)
            sp.dma_start(wkvc[:, :, 0:DC], A["L1_ffn_Wk_c"].rearrange("(k p) n -> p k n", p=128)).then_inc(s("ld_wd"), 16)
            sp.dma_start(wkvc[:, :, DC:], A["L1_ffn_Wv_c"].rearrange("(k p) n -> p k n", p=128)).then_inc(s("ld_wd"), 16)
            sp.dma_start(wkv2[0:DC, 0], A["L1_ffn_Wk"]).then_inc(s("ld_wd"), 16)
            sp.dma_start(wkv2[DC:, 1], A["L1_ffn_Wv"]).then_inc(s("ld_wd"), 16)
            sp.dma_start(wge[:, :, 0:2], A["L1_ffn_Wg_gate"].rearrange("(k p) n -> p k n", p=128)).then_inc(s("ld_wd"), 16)
            sp.dma_start(wge[:, :, 2:], A["L1_ffn_We_gate"].rearrange("(k p) n -> p k n", p=128)).then_inc(s("ld_wd"), 16)
            for i, n in enumerate(("L1_ffn_W_shared_in", "L1_ffn_W1_shared")):
                sp.dma_start(wgu2[:, i], A[n].rearrange("(k p) n -> p k n", p=128)).then_inc(s("ld_wd"), 16)
            sp.dma_start(wdn[:], A["L1_ffn_W_shared_out"].rearrange("(k p) n -> p k n", p=128)).then_inc(s("ld_wd"), 16)
            for f in range(FT):
                sp.dma_start(w2[:, f], A["L1_ffn_W2_experts"][:, 128 * f:128 * f + 128, :].rearrange("e p d -> p e d")) \
                    .then_inc(s("ld_wd"), 16)
            for b in range(0, NB, 2):
                sp.wait_ge(s("f_out"), b + 2)
                sp.dma_start(out[b:b + 2].rearrange("b t d -> t b d"), x[:, b:b + 2, :]).then_inc(s("stored"), 16)
            sp.wait_ge(s("stored"), 16 * NB // 2)

        @block.gpsimd
        def _(pool):
            nc.gpsimd.memset(ones[:], 1.0)
            nc.gpsimd.memset(minus_half[:], -0.5).then_inc(s("set_ones"), 1)
            nc.gpsimd.memset(ctxN[0:KEYS, :, NJ - 1, :], 0.0)
            nc.gpsimd.memset(ctxT[:, :, :, CTX:CPAD], 0.0)
            nc.gpsimd.memset(prob[:, :, CTX:CPAD], 0.0).then_inc(s("set_pads"), 1)
            nc.gpsimd.memset(wo[:], 0.0)
            nc.gpsimd.memset(zero_rows[:], 0.0).then_inc(s("set_zero"), 1)

            def inverse_root(st, a=0, z=NB, part=0):
                pool.wait_ge(s("n_var"), turn(st) + part + 1)
                nc.gpsimd.tensor_tensor(rstd[:, a:z], std[:, a:z], minus_half[:, a:z], ALU.pow) \
                    .then_inc(s("n_std"), 1)

            pool.wait_ge(s("set_ones"), 1)
            inverse_root("a")
            pool.wait_ge(s("ld_mask"), 16)
            for b in range(NB):
                if b >= 2:
                    pool.wait_ge(s("a_max"), b - 1)
                nc.gpsimd.tensor_scalar(keep[:, b % 2, :], mask8[:, b, :], -1.0, 1.0, ALU.mult, ALU.add)
                nc.gpsimd.tensor_scalar(drop[:, b % 2, :], mask8[:, b, :], NEG, 0.0, ALU.mult, ALU.add) \
                    .then_inc(s("a_mask"), 1)
            inverse_root("b")
            pool.wait_ge(s("b_zero"), 16 * NPAIR)
            for b in range(NB):
                pool.wait_ge(s("b_xs"), b + 1)
                nc.gpsimd.indirect_dma_start(xs_dram, bass.IndirectOffsetOnAxis(slot[:, b:b + 1], 0), xs[:, b, :], None,
                                             bounds_check=NSLOT - 1, oob_is_err=False).then_inc(s("b_scat"), 16)
            pool.wait_ge(s("n_hT"), NB // 2 * (turn("b") + 1))
            nc.gpsimd.memset(hN[:], 0.0).then_inc(s("b_clear"), 1)
            pool.wait_ge(s("b_y"), LAST_IN_CTX + 1)
            nc.gpsimd.memset(ctxT[:, :, :, CTX:CPAD], 0.0).then_inc(s("set_pads"), 1)
            pool.wait_ge(s("b_clear"), 1)
            for u in range(2):
                pool.wait_ge(s(f"b_yst{u}"), 16 * NPAIR // 2)
            for b in range(NB):
                nc.gpsimd.indirect_dma_start(hN[:, b, :], None, y_dram, bass.IndirectOffsetOnAxis(slot[:, b:b + 1], 0),
                                             bounds_check=NSLOT - 1, oob_is_err=False).then_inc(s(f"b_gat{b // 4}"), 16)
            nc.gpsimd.memset(wkv2[0:DC, 1], 0.0)
            nc.gpsimd.memset(wkv2[DC:, 0], 0.0).then_inc(s("b_clear"), 1)
            pool.wait_ge(s("b_clear"), 2)
            for u in range(2):
                for j in range(NJ):
                    last = nc.gpsimd.memset(vpad[:, u, j, :].rearrange("p (h c) -> p h c", c=32)[:, :, DH:], 1.0)
            last.then_inc(s("c_vones"), 1)

            def spread_queries(b, done):
                q = qT[:, :, T * b:T * b + T].unsqueeze(2).to_broadcast([128, KT, 8, T])
                m = consts[:, cs["headmask"]].unsqueeze(1).unsqueeze(3).to_broadcast([128, KT, 8, T])
                nc.gpsimd.tensor_tensor(qbd[:, b % 2].rearrange("p k (h t) -> p k h t", h=8), q, m, ALU.mult) \
                    .then_inc(done, 1)

            inverse_root("c")
            pool.wait_ge(s("c_qsb"), 2 * KT)
            for b in range(NB):
                if b >= 2:
                    pool.wait_ge(s("c_s"), NH * (b - 1))
                spread_queries(b, s("c_qbd"))
            inverse_root("d")
            for i, t in enumerate((qT, krT)):
                pool.wait_ge(s("d_swap"), i + 1)
                w3 = t.rearrange("p k (b t) -> p (k b) t", t=T)
                nc.gpsimd.tensor_tensor(w3, w3, consts[:, cs["cos"]].unsqueeze(1).to_broadcast([128, KT * NB, T]), ALU.mult) \
                    .then_inc(s("d_cos"), 1)
            pool.wait_ge(s("d_rot"), 2)
            for b in range(NB):
                if b >= 2:
                    pool.wait_ge(s("d_s"), 4 * (b - 1))
                spread_queries(b, s("d_qbd"))
            inverse_root("e")
            for half in range(2):
                inverse_root("f", 4 * half, 4 * half + 4, half)

        @block.scalar
        def _(act):
            def ln_act(st):
                for g in range(NB // 2):
                    act.wait_ge(s("n_tp"), NB // 2 * turn(st) + g + 1)
                    nc.scalar.activation(hT[:, :, 2 * T * g:2 * T * (g + 1)], bank3(g % 2, KT, 2 * T), ACT.Copy) \
                        .then_inc(s("n_hT"), 1)

            act.wait_ge(s("set_ones"), 1)
            act.wait_ge(s("ld_small"), 96)
            nc.scalar.activation(tg[:], gates[:], ACT.Tanh).then_inc(s("act_step"), 1)
            ln_act("a")
            for u in range(2 * KT):
                n, half = u // 2, u % 2
                act.wait_ge(s("a_t"), u + 1)
                if u == 0:
                    act.wait_ge(s("a_foldsb"), 1)
                nc.scalar.activation(tT[:, n, HALF * half:HALF * (half + 1)], PB[4 + u % 2][:, 0:HALF], ACT.Identity,
                                     bias=foldv[:, n:n + 1]).then_inc(s("a_tsb"), 1)
            for half in range(2):
                act.wait_ge(s("a_c"), half + 1)
                nc.scalar.activation(cT[:, HALF * half:HALF * (half + 1)], PB[6 + half][0:1, 0:HALF], ACT.Identity,
                                     bias=fold0[:]).then_inc(s("a_csb"), 1)
            act.wait_ge(s("set_pads"), 1)
            for i in range(NB + 4):
                if 2 <= i < NB + 2:
                    b = i - 2
                    act.wait_ge(s("a_pt"), b + 1)
                    if b >= 2:
                        act.wait_ge(s("a_mix"), b - 1)
                    nc.scalar.activation(pT[0:KEYS, b % 2, :], PB[2 + b % 2][0:KEYS, 0:NJ * T], ACT.Copy) \
                        .then_inc(s("a_ptsb"), 1)
                if i < NB:
                    act.wait_ge(s("a_max"), i + 1)
                    if i >= NP_:
                        act.wait_ge(s("a_pt"), i - NP_ + 1)
                    nc.scalar.activation(prob[:, i % NP_, 0:CTX], sc[:, i % 2, :], ACT.Exp, bias=nmx[:, 0, i:i + 1],
                                         accum_out=rsum[:, i:i + 1]).then_inc(s("a_p"), 1)
                if 2 <= i < NB + 2:
                    b = i - 2
                    act.wait_ge(s("a_mix"), b + 1)
                    if b >= 2:
                        act.wait_ge(s("a_mt"), b - 1)
                    nc.scalar.activation(mix[:, b % 2, :], PB[4][0:T, 0:D], ACT.Copy).then_inc(s("a_mixsb"), 1)
                if 3 <= i < NB + 3:
                    b = i - 3
                    act.wait_ge(s("a_mt"), b + 1)
                    if b >= 2:
                        act.wait_ge(s("a_y"), b - 1)
                    nc.scalar.activation(mixT[:, b % 2], bank3(5, KT, T), ACT.Copy).then_inc(s("a_mtsb"), 1)
            ln_act("b")
            for half in range(2):
                act.wait_ge(s("b_lgT"), half + 1)
                nc.scalar.activation(lgT[:, HALF * half:HALF * (half + 1)], PB[2 + half][0:NE, 0:HALF], ACT.Copy) \
                    .then_inc(s("b_lgTsb"), 1)
            act.wait_ge(s("b_mx"), 1)
            nc.scalar.activation(r1[:, 1, :], r1[:, 0, :], ACT.Sigmoid).then_inc(s("b_sig"), 1)
            act.wait_ge(s("b_lg"), 1)
            for u in range(2 * FT):
                act.wait_ge(s("b_sgu"), u + 1)
                if u >= 2:
                    act.wait_ge(s("b_hid"), u - 1)
                nc.scalar.activation(sil[:, u % 2, 0:HALF], PB[2 * u % 8][:, 0:HALF], ACT.Silu).then_inc(s("b_sil"), 1)

            def xg_copy(i):
                act.wait_ge(s("b_xt"), i + 1)
                if i >= 2:
                    act.wait_ge(s("b_gu"), i - 1)
                nc.scalar.activation(xgT[:, i % 2], bank3(6, KT, 128), ACT.Copy).then_inc(s("b_xtsb"), 1)

            xg_copy(0)
            for i in range(NPAIR + 1):
                if i < NPAIR:
                    act.wait_ge(s("b_gu"), i + 1)
                    act.wait_ge(s("b_hid"), 2 * FT)
                    if i >= 2:
                        act.wait_ge(s("b_au"), i - 1)
                    nc.scalar.activation(sil[:, i % 2, :], PB[2 * (i % 2)][:, :], ACT.Silu).then_inc(s("b_esil"), 1)
                if i + 1 < NPAIR:
                    xg_copy(i + 1)
                if i >= 1:
                    p = i - 1
                    act.wait_ge(s("b_y"), p + 1)
                    if p >= 2:
                        act.wait_ge(s(f"b_yst{p % 2}"), 16 * (p // 2))
                    nc.scalar.activation(yb[:, p % 2, :], PB[5][:, 0:D], ACT.Copy).then_inc(s("b_ysb"), 1)
            act.wait_ge(s("o_flag"), 1)
            over = act.value_load(flag[0:1, 0:1], min_val=0, max_val=NT)
            with act.If(over > 0):
                with act.Fori(0, NE) as e:
                    for b in range(NB):
                        act.wait_ge(s("o_gu"), NB * e + (b + 1))
                        nc.scalar.activation(sil[0:T, 0, :], PB[0][0:T, :], ACT.Silu, scale=ocol[:, b:b + 1]) \
                            .then_inc(s("o_sil"), 1)

            def q_copy(st):
                for u in range(2 * KT):
                    n, half = u // 2, u % 2
                    act.wait_ge(s(st + "_q"), u + 1)
                    nc.scalar.activation(qT[:, n, HALF * half:HALF * (half + 1)], PB[4 + u % 2][:, 0:HALF], ACT.Copy,
                                         scale=float(DH) ** -0.5).then_inc(s(st + "_qsb"), 1)

            def kv_copy(b, i):
                act.wait_ge(s("c_pr"), 5 * b + i + 1)
                if i < KT:
                    nc.scalar.activation(kT[:, b % 2, i, :], PB[6][:, 0:CPAD], ACT.Copy).then_inc(s("c_prsb"), 1)
                else:
                    nc.scalar.activation(vpad[0:KEYS, b % 2, i - KT, :].rearrange("p (h c) -> p h c", c=32)[:, :, 0:DH],
                                         PB[6][0:KEYS, 0:D].rearrange("p (h c) -> p h c", c=DH), ACT.Copy) \
                        .then_inc(s("c_prsb"), 1)

            for b in range(2):
                for i in range(5):
                    kv_copy(b, i)
            ln_act("c")
            q_copy("c")
            for n in range(NB * NH):
                b, h = n // NH, n % NH
                act.wait_ge(s("c_max"), n + 1)
                if n >= 4:
                    act.wait_ge(s("c_pt"), n - 3)
                nc.scalar.activation(prob[:, n % 4, 0:CTX], PB[SB[n % 3]][0:T, 0:CTX], ACT.Exp,
                                     bias=nmx[:, n % 4, 0:1]).then_inc(s("c_p"), 1)
                if 1 <= b < NB - 1 and h in KV_AT:
                    kv_copy(b + 1, KV_AT.index(h))
            ln_act("d")
            q_copy("d")
            for half in range(2):
                act.wait_ge(s("d_kvc"), half + 1)
                nc.scalar.activation(kvcT[:, HALF * half:HALF * (half + 1)], PB[6 + half][:, 0:HALF], ACT.Copy) \
                    .then_inc(s("d_kvcsb"), 1)
            for u in range(2 * KT):
                n, half = u // 2, u % 2
                act.wait_ge(s("d_k"), u + 1)
                nc.scalar.activation(krT[:, n, HALF * half:HALF * (half + 1)], PB[4 + u % 2][:, 0:HALF], ACT.Copy) \
                    .then_inc(s("d_ksb"), 1)

            def v_copy(b):
                act.wait_ge(s("d_v"), b + 1)
                nc.scalar.activation(vpad[0:T, b % 2, 0, :].rearrange("p (h c) -> p h c", c=32)[:, :, 0:DH],
                                     PB[6][0:T, 0:D].rearrange("p (h c) -> p h c", c=DH), ACT.Copy).then_inc(s("d_vsb"), 1)

            def d_probs_copy(m):
                act.wait_ge(s("d_pt"), m + 1)
                if m >= 2:
                    act.wait_ge(s("d_av"), m - 1)
                nc.scalar.activation(pT4[0:T, m % 2, :], PB[2 + m % 2][0:T, 0:4 * T], ACT.Copy).then_inc(s("d_ptsb"), 1)

            v_copy(0)
            for n in range(4 * NB):
                b, g = n // 4, n % 4
                if n >= 2:
                    d_probs_copy(n - 2)
                act.wait_ge(s("d_shift"), n + 1)
                nc.scalar.activation(prob4[:, n % 3, :], prob4[:, n % 3, :], ACT.Exp).then_inc(s("d_p"), 1)
                if g == 0 and b >= 1:
                    v_copy(b)
            for m in range(4 * NB - 2, 4 * NB):
                d_probs_copy(m)
            for b in range(NB):
                act.wait_ge(s("d_x2"), b + 1)
                if b >= 4:
                    act.wait_ge(s("d_sq"), b - 3)
                nc.scalar.activation(row_T[0:T, D * (b % 4):D * (b % 4) + D], hN[:, b, :], ACT.Square, accum_out=rsum[:, b:b + 1]).then_inc(s("d_sq"), 1)
            for g in range(NB // 2):
                act.wait_ge(s("n_tp"), NB // 2 * turn("e") + g + 1)
                nc.scalar.activation(hT[:, :, 2 * T * g:2 * T * (g + 1)], bank3(g % 2, KT, 2 * T), ACT.Copy) \
                    .then_inc(s("n_hT"), 1)
            for half in range(2):
                act.wait_ge(s("e_gT"), half + 1)
                nc.scalar.activation(row_T[0:2 + NX, HALF * half:HALF * (half + 1)], PB[2 + half][0:2 + NX, 0:HALF], ACT.Copy) \
                    .then_inc(s("e_gTsb"), 1)
            act.wait_ge(s("e_gx"), 1)
            nc.scalar.activation(ge[:], gl[:], ACT.Exp).then_inc(s("e_gexp"), 1)
            act.wait_ge(s("e_g"), 1)
            for u in range(4 * FT):
                act.wait_ge(s("e_gu"), u + 1)
                if u >= 2:
                    act.wait_ge(s("e_hid"), u - 1)
                nc.scalar.activation(sil[:, u % 2, 0:HALF], PB[2 * u % 8][:, 0:HALF], ACT.Silu).then_inc(s("e_sil"), 1)
            act.wait_ge(s("e_hid"), 4 * FT)
            for b in range(NB):
                act.wait_ge(s("e_comb"), 5 * b + 5)
                if b >= 4:
                    act.wait_ge(s("f_sq"), b - 3)
                nc.scalar.activation(row_T[0:T, D * (b % 4):D * (b % 4) + D], hN[:, b, :], ACT.Square, accum_out=rsum[:, b:b + 1]).then_inc(s("f_sq"), 1)

        @block.vector
        def _(dve):
            steps = [0]

            def link(ins):
                steps[0] += 1
                ins.then_inc(s("dve_step"), 1)
                dve.wait_ge(s("dve_step"), steps[0])

            def bc(ap, n):
                return ap.unsqueeze(2).to_broadcast([ap.shape[0], ap.shape[1], n])

            def batch_stats(b, done):
                dve.wait_ge(done, b + 1)
                nc.vector.bn_stats(bn6[:, b, :], x[:, b, :]).then_inc(s("stats"), 1)

            def ln_dve(st):
                dve.wait_ge(s("stats"), NB * (turn(st) + 1))
                for b in range(NB):
                    last = nc.vector.bn_aggr(mv[:, b, :], bn6[:, b, :])
                link(last)
                nc.vector.tensor_scalar(std[:], mv[:, :, 1], LN_EPS, None, ALU.add).then_inc(s("n_var"), 1)
                dve.wait_ge(s("n_std"), turn(st) + 1)
                for b in range(NB):
                    nc.vector.tensor_scalar(hN[:, b, :], x[:, b, :], mv[:, b, 0:1], rstd[:, b:b + 1],
                                            ALU.subtract, ALU.mult).then_inc(s("n_hN"), 1)

            dve.wait_ge(s("ld_x"), 16)
            for b in range(NB):
                nc.vector.bn_stats(bn6[:, b, :], x[:, b, :]).then_inc(s("stats"), 1)
            ln_dve("a")
            dve.wait_ge(s("a_fold"), 1)
            nc.vector.tensor_scalar(fold[:], bank3(2, KT, D), 1.0 / 16, None, ALU.mult)
            nc.vector.tensor_scalar(foldv[:], PB[3][:, 0:4], 1.0 / 16, None, ALU.mult)
            nc.vector.tensor_scalar(fold0[:], PB[3][0:1, 4:5], 1.0 / 16, None, ALU.mult).then_inc(s("a_foldsb"), 1)
            dve.wait_ge(s("act_step"), 1)
            dve.wait_ge(s("ld_small"), 96)
            link(nc.vector.tensor_scalar(grow[:], brow["bv"][:], tg[0:T, 0:1], None, ALU.mult))
            link(nc.vector.tensor_tensor(x[:], x[:], grow[:].unsqueeze(1).to_broadcast([T, NB, D]), ALU.add))
            dve.wait_ge(s("a_cc"), 1)
            nc.vector.tensor_copy(ccol[:], PB[3][0:T, 0:NB]).then_inc(s("a_ccsb"), 1)
            dve.wait_ge(s("a_ccsb"), 1)
            for i in range(NB + 4):
                if i < NB:
                    b = i
                    dve.wait_ge(s("a_s"), b + 1)
                    dve.wait_ge(s("a_mask"), b + 1)
                    if b >= 2:
                        dve.wait_ge(s("a_p"), b - 1)
                    link(nc.vector.scalar_tensor_tensor(out=sc[:, b % 2, :], in0=PB[SB[b % 3]][0:T, 0:CTX],
                                                        scalar=ccol[:, b:b + 1], in1=keep[:, b % 2, :],
                                                        op0=ALU.add, op1=ALU.mult))
                    link(nc.vector.tensor_tensor(sc[:, b % 2, :], sc[:, b % 2, :], drop[:, b % 2, :], ALU.add))
                    nc.vector.tensor_reduce(nmx[:, 0, b:b + 1], sc[:, b % 2, :], AX.X, ALU.max, negate=True) \
                        .then_inc(s("a_max"), 1)
                if i >= 4:
                    b = i - 4
                    dve.wait_ge(s("a_p"), b + 1)
                    link(nc.vector.reciprocal(rg[:, b:b + 1], rsum[:, b:b + 1]))
                    link(nc.vector.tensor_scalar(rg[:, b:b + 1], rg[:, b:b + 1], tg[0:T, 0:1], None, ALU.mult))
                    dve.wait_ge(s("a_y"), b + 1)
                    nc.vector.scalar_tensor_tensor(out=x[:, b, :], in0=PB[6][0:T, 0:D], scalar=rg[:, b:b + 1],
                                                   in1=x[:, b, :], op0=ALU.mult, op1=ALU.add).then_inc(s("a_res"), 1)
                    batch_stats(b, s("a_res"))
            ln_dve("b")
            dve.wait_ge(s("b_lg"), 1)
            link(nc.vector.tensor_copy(lg[:], PB[4][0:T, 0:NB * NE].rearrange("p (b e) -> p b e", b=NB)))
            nc.vector.tensor_reduce(r1[:, 0, :], lg[:], AX.X, ALU.max).then_inc(s("b_mx"), 1)
            dve.wait_ge(s("b_mx"), 1)

            def over_b(ap):
                return ap.unsqueeze(1).to_broadcast([T, NB, ap.shape[-1]])

            link(nc.vector.tensor_tensor(key[:], lg[:], bc(r1[:, 0, :], NE), ALU.is_equal))
            link(nc.vector.tensor_tensor(key[:], key[:], over_b(consts[0:T, cs["rev16"]]), ALU.mult))
            link(nc.vector.tensor_reduce(r1[:, 2, :], key[:], AX.X, ALU.max))
            link(nc.vector.tensor_tensor(oh[:], key[:], bc(r1[:, 2, :], NE), ALU.is_equal))
            link(nc.vector.memset(pre[:, 0, :], 0.0))
            for b in range(1, NB):
                link(nc.vector.tensor_tensor(pre[:, b, :], pre[:, b - 1, :], oh[:, b - 1, :], ALU.add))
            nc.vector.tensor_tensor(key[:], oh[:], over_b(consts[0:T, cs["base16"]]), ALU.mult).then_inc(s("b_oh"), 1)
            dve.wait_ge(s("b_oh"), 1)
            link(nc.vector.tensor_reduce(r1[:, 3, :], key[:], AX.X, ALU.add))
            dve.wait_ge(s("b_pos"), 1)
            link(nc.vector.tensor_tensor(pos[:], PB[5][0:T, 0:NB * NE].rearrange("p (b e) -> p b e", b=NB), oh[:], ALU.mult))
            link(nc.vector.tensor_reduce(r1[:, 4, :], pos[:], AX.X, ALU.add))
            link(nc.vector.tensor_scalar(r1[:, 5, :], r1[:, 4, :], float(FULL), None, ALU.is_ge))
            link(nc.vector.tensor_tensor(r1[:, 6, :], r1[:, 4, :], r1[:, 3, :], ALU.add))
            link(nc.vector.scalar_tensor_tensor(out=r1[:, 7, :], in0=r1[:, 5, :], scalar=float(SKIP), in1=r1[:, 6, :],
                                                op0=ALU.mult, op1=ALU.add))
            nc.vector.tensor_copy(slot[:], r1[:, 7, :]).then_inc(s("b_slot"), 1)
            dve.wait_ge(s("b_sig"), 1)
            link(nc.vector.tensor_tensor(r1[:, 8, :], r1[:, 5, :], r1[:, 1, :], ALU.mult))
            link(nc.vector.tensor_tensor(oscale[:], oh[:], bc(r1[:, 8, :], NE), ALU.mult))
            for b in range(NB):
                nc.vector.tensor_scalar(xs[:, b, :], hN[:, b, :], r1[:, 1, b:b + 1], None, ALU.mult).then_inc(s("b_xs"), 1)
            dve.wait_ge(s("o_count"), 1)
            link(nc.vector.tensor_reduce(r1[0:1, 9, 0:1], PB[5][0:1, 0:NB], AX.X, ALU.add))
            nc.vector.tensor_copy(flag[:], r1[0:1, 9, 0:1]).then_inc(s("o_flag"), 1)
            for u in range(2 * FT):
                f, half = u // 2, u % 2
                dve.wait_ge(s("b_sil"), u + 1)
                nc.vector.tensor_tensor(hid[:, f, HALF * half:HALF * (half + 1)], sil[:, u % 2, 0:HALF],
                                        PB[(2 * u + 1) % 8][:, 0:HALF], ALU.mult).then_inc(s("b_hid"), 1)
            for i in range(NPAIR + 1):
                if i >= 1:
                    p = i - 1
                    dve.wait_ge(s("b_at"), p + 1)
                    if p >= 2:
                        dve.wait_ge(s("b_y"), p - 1)
                    nc.vector.tensor_copy(auT[:, p % 2], bank3(4, FT, 128)).then_inc(s("b_atsb"), 1)
                    dve.wait_ge(s("b_sd"), p + 1)
                    nc.vector.scalar_tensor_tensor(out=x[:, p, :], in0=PB[7][0:T, 0:D], scalar=tg[0:T, 2:3],
                                                   in1=x[:, p, :], op0=ALU.mult, op1=ALU.add).then_inc(s("b_sdres"), 1)
                if i < NPAIR:
                    dve.wait_ge(s("b_esil"), i + 1)
                    if i >= 2:
                        dve.wait_ge(s("b_at"), i - 1)
                    nc.vector.tensor_tensor(au[:, i % 2, :], sil[:, i % 2, :], PB[2 * (i % 2) + 1][:, :], ALU.mult) \
                        .then_inc(s("b_au"), 1)
            dve.wait_ge(s("b_sdres"), NB)
            for b in range(NB):
                dve.wait_ge(s(f"b_gat{b // 4}"), 64)
                nc.vector.scalar_tensor_tensor(out=x[:, b, :], in0=hN[:, b, :], scalar=tg[0:T, 2:3], in1=x[:, b, :],
                                               op0=ALU.mult, op1=ALU.add).then_inc(s("b_res"), 1)
            dve.wait_ge(s("b_res"), NB)
            over = dve.value_load(flag[0:1, 0:1], min_val=0, max_val=NT)
            with dve.If(over > 0):
                nc.vector.memset(ocol[:], 0.0).then_inc(s("o_res"), 1)
                with dve.Fori(0, NE) as e:
                    dve.wait_ge(s("o_res"), NB * e + 1)
                    nc.vector.tensor_copy(ocol[:], oscale[:, :, bass.ds(e, 1)].rearrange("t b e -> t (b e)")) \
                        .then_inc(s("o_col"), 1)
                    dve.wait_ge(s("o_col"), e + 1)
                    for b in range(NB):
                        dve.wait_ge(s("o_sil"), NB * e + (b + 1))
                        nc.vector.scalar_tensor_tensor(out=au[0:T, 0, :], in0=PB[1][0:T, :], scalar=ocol[:, b:b + 1],
                                                       in1=sil[0:T, 0, :], op0=ALU.mult, op1=ALU.mult).then_inc(s("o_au"), 1)
                        dve.wait_ge(s("o_at"), NB * e + (b + 1))
                        nc.vector.tensor_copy(auT[:, 0, :, 0:T], bank3(4, FT, T)).then_inc(s("o_atsb"), 1)
                        dve.wait_ge(s("o_y"), NB * e + (b + 1))
                        nc.vector.scalar_tensor_tensor(out=x[:, b, :], in0=PB[5][0:T, 0:D], scalar=tg[0:T, 2:3],
                                                       in1=x[:, b, :], op0=ALU.mult, op1=ALU.add).then_inc(s("o_res"), 1)
                dve.wait_ge(s("o_res"), NB * NE + 1)
            for b in range(NB):
                batch_stats(b, s("b_res"))
            ln_dve("c")
            link(nc.vector.tensor_scalar(grow[:], brow["bo"][:], tg[0:T, 1:2], None, ALU.mult))
            link(nc.vector.tensor_tensor(x[:], x[:], grow[:].unsqueeze(1).to_broadcast([T, NB, D]), ALU.add))

            def normalise(b, bank, st):
                dve.wait_ge(s(st + "_av"), 4 * b + 4)
                if b >= 2:
                    dve.wait_ge(s(st + "_y"), b - 1)
                link(nc.vector.stream_shuffle(den, PB[bank][:, 0:NG * T], UPPER_HALF))
                link(nc.vector.reciprocal(den, den))
                nc.vector.tensor_tensor(attT[:, b % 2].rearrange("p g t -> p (g t)"), PB[bank][:, 0:NG * T], den, ALU.mult) \
                    .then_inc(s(st + "_att"), 1)

            def c_residual(b):
                dve.wait_ge(s("c_y"), b + 1)
                nc.vector.scalar_tensor_tensor(out=x[:, b, :], in0=PB[6][0:T, 0:D], scalar=tg[0:T, 1:2],
                                               in1=x[:, b, :], op0=ALU.mult, op1=ALU.add).then_inc(s("c_res"), 1)
                batch_stats(b, s("c_res"))

            for n in range(NB * NH + 2):
                b, h = n // NH, n % NH
                if n < NB * NH:
                    dve.wait_ge(s("c_s"), n + 1)
                    if n >= 4:
                        dve.wait_ge(s("c_p"), n - 3)
                    nc.vector.tensor_reduce(nmx[:, n % 4, 0:1], PB[SB[n % 3]][0:T, 0:CTX], AX.X, ALU.max, negate=True) \
                        .then_inc(s("c_max"), 1)
                if n >= 2:
                    m = n - 2
                    dve.wait_ge(s("c_pt"), m + 1)
                    if m >= 8:
                        dve.wait_ge(s("c_av"), m // 4 - 1)
                    nc.vector.tensor_copy(pTq[0:KEYS, m % 8, :], PB[2 + m % 2][0:KEYS, 0:NJ * T]).then_inc(s("c_ptsb"), 1)
                if 1 <= b < NB and h == 3:
                    normalise(b - 1, 4 + (b - 1) % 2, "c")
                if 1 <= b < NB and h == 8:
                    c_residual(b - 1)
            normalise(NB - 1, 4 + (NB - 1) % 2, "c")
            c_residual(NB - 1)
            ln_dve("d")

            def rotate(t, st):
                flat = t.rearrange("p k t -> p (k t)")
                tab = lambda n: consts[:, cs[n]].unsqueeze(1).to_broadcast([128, KT * NB, T])
                w3 = lambda ap: ap.rearrange("p (m t) -> p m t", t=T)
                nc.vector.stream_shuffle(rot, flat, SWAP_PAIRS).then_inc(s("d_swap"), 1)
                dve.wait_ge(s("d_swap"), 1 if st == "q" else 2)
                link(nc.vector.tensor_tensor(w3(rot), w3(rot), tab("sin"), ALU.mult))
                dve.wait_ge(s("d_cos"), 1 if st == "q" else 2)
                nc.vector.tensor_tensor(flat, flat, rot, ALU.add).then_inc(s("d_rot"), 1)

            dve.wait_ge(s("d_qsb"), 2 * KT)
            rotate(qT, "q")
            dve.wait_ge(s("d_ksb"), 2 * KT)
            dve.wait_ge(s("d_rot"), 1)
            rotate(krT, "k")

            def d_residual(b):
                dve.wait_ge(s("d_y"), b + 1)
                nc.vector.tensor_tensor(hN[:, b, :], PB[6][0:T, 0:D], hN[:, b, :], ALU.add).then_inc(s("d_x2"), 1)

            for n in range(4 * NB):
                b, g = n // 4, n % 4
                if b >= 3 and g == 0:
                    d_residual(b - 3)
                dve.wait_ge(s("d_s"), n + 1)
                if n >= 3:
                    dve.wait_ge(s("d_pt"), n - 2)
                sc4 = PB[SB[n % 3]][0:T, 0:4 * T].rearrange("p (h t) -> p h t", h=4)
                link(nc.vector.tensor_reduce(nmx[:, n % 4, 0:4], sc4, AX.X, ALU.max))
                nc.vector.tensor_tensor(prob4[:, n % 3, :].rearrange("p (h t) -> p h t", h=4), sc4,
                                        bc(nmx[:, n % 4, 0:4], T), ALU.subtract).then_inc(s("d_shift"), 1)
                if b >= 1 and g == 2:
                    normalise(b - 1, 4 + (b - 1) % 2, "d")
            d_residual(NB - 3)
            d_residual(NB - 2)
            normalise(NB - 1, 4 + (NB - 1) % 2, "d")
            d_residual(NB - 1)
            dve.wait_ge(s("d_sq"), NB)
            nc.vector.tensor_scalar(std[:], rsum[:], 1.0 / D, RMS_EPS, ALU.mult, ALU.add).then_inc(s("n_var"), 1)
            dve.wait_ge(s("n_std"), turn("e") + 1)
            for b in range(NB):
                nc.vector.scalar_tensor_tensor(out=hN[:, b, :], in0=hN[:, b, :], scalar=rstd[:, b:b + 1], in1=brow["n1"][:],
                                               op0=ALU.mult, op1=ALU.mult).then_inc(s("n_hN"), 1)
            link(nc.vector.tensor_scalar(grow[:], brow["n2"][:], tg[0:T, 3:4], None, ALU.mult))
            dve.wait_ge(s("e_g"), 1)
            dve.wait_ge(s("ld_wc"), 16 * 13)
            link(nc.vector.tensor_tensor(gl[:], PB[4][0:T, 0:NB * (2 + NX)].rearrange("p (b e) -> p b e", b=NB),
                                         gbias[:].unsqueeze(1).to_broadcast([T, NB, 2 + NX]), ALU.add))
            link(nc.vector.tensor_reduce(r1[:, 0, :], gl[:, :, 0:2], AX.X, ALU.max))
            nc.vector.tensor_reduce(r1[:, 1, :], gl[:, :, 2:2 + EPG], AX.X, ALU.max)
            link(nc.vector.tensor_reduce(r1[:, 2, :], gl[:, :, 2 + EPG:], AX.X, ALU.max))
            link(nc.vector.tensor_tensor(gl[:, :, 0:2], gl[:, :, 0:2], bc(r1[:, 0, :], 2), ALU.subtract))
            nc.vector.tensor_tensor(gl[:, :, 2:2 + EPG], gl[:, :, 2:2 + EPG], bc(r1[:, 1, :], EPG), ALU.subtract)
            nc.vector.tensor_tensor(gl[:, :, 2 + EPG:], gl[:, :, 2 + EPG:], bc(r1[:, 2, :], EPG), ALU.subtract) \
                .then_inc(s("e_gx"), 1)
            dve.wait_ge(s("e_gexp"), 1)
            for i, (a, z) in enumerate(((0, 2), (2, 2 + EPG), (2 + EPG, 2 + NX))):
                last = nc.vector.tensor_reduce(r1[:, 3 + i, :], ge[:, :, a:z], AX.X, ALU.add)
            link(last)
            link(nc.vector.reciprocal(r1[:, 3:6, :], r1[:, 3:6, :]))
            for i, (a, z) in enumerate(((0, 2), (2, 2 + EPG), (2 + EPG, 2 + NX))):
                last = nc.vector.tensor_tensor(ge[:, :, a:z], ge[:, :, a:z], bc(r1[:, 3 + i, :], z - a), ALU.mult)
            link(last)
            link(nc.vector.tensor_tensor(r1[:, 6, :], ge[:, :, 0], ge[:, :, 1], ALU.is_ge))
            link(nc.vector.tensor_tensor(r1[:, 7, :], ge[:, :, 0], ge[:, :, 1], ALU.max))
            link(nc.vector.tensor_tensor(r1[:, 8, :], r1[:, 6, :], r1[:, 7, :], ALU.mult))
            link(nc.vector.tensor_tensor(r1[:, 9, :], r1[:, 7, :], r1[:, 8, :], ALU.subtract))
            nc.vector.tensor_tensor(ge[:, :, 2:2 + EPG], ge[:, :, 2:2 + EPG], bc(r1[:, 8, :], EPG), ALU.mult)
            link(nc.vector.tensor_tensor(ge[:, :, 2 + EPG:], ge[:, :, 2 + EPG:], bc(r1[:, 9, :], EPG), ALU.mult))
            pe_ = ge[:, :, 2:]
            o8, k8, s8 = oh[:, :, 0:NX], key[:, :, 0:NX], pos[:, :, 0:NX]
            rev8 = consts[0:T, cs["rev8"]].unsqueeze(1).to_broadcast([T, NB, NX])
            link(nc.vector.tensor_copy(s8, pe_))
            for r in range(2):
                link(nc.vector.tensor_reduce(r1[:, 0, :], s8, AX.X, ALU.max))
                link(nc.vector.tensor_tensor(k8, s8, bc(r1[:, 0, :], NX), ALU.is_equal))
                link(nc.vector.tensor_tensor(k8, k8, rev8, ALU.mult))
                link(nc.vector.tensor_reduce(r1[:, 1, :], k8, AX.X, ALU.max))
                link(nc.vector.tensor_tensor(o8, k8, bc(r1[:, 1, :], NX), ALU.is_equal))
                if r == 0:
                    link(nc.vector.tensor_tensor(we[:], o8, pe_, ALU.mult))
                    link(nc.vector.tensor_tensor(s8, s8, o8, ALU.subtract))
                    link(nc.vector.tensor_tensor(s8, s8, o8, ALU.subtract))
                else:
                    link(nc.vector.tensor_tensor(o8, o8, pe_, ALU.mult))
                    link(nc.vector.tensor_tensor(we[:], we[:], o8, ALU.add))
            for u in range(4 * FT):
                which, f, half = u // (2 * FT), u // 2 % FT, u % 2
                dve.wait_ge(s("e_sil"), u + 1)
                nc.vector.tensor_tensor(hid2[:, which, f, HALF * half:HALF * (half + 1)], sil[:, u % 2, 0:HALF],
                                        PB[(2 * u + 1) % 8][:, 0:HALF], ALU.mult).then_inc(s("e_hid"), 1)
            for b in range(NB):
                for i in range(5):
                    v = 5 * b + i
                    dve.wait_ge(s("e_down"), v + 1)
                    if i == 0:
                        nc.vector.tensor_tensor(hN[:, b, :], PB[v % 8][0:T, 0:D], hN[:, b, :], ALU.add) \
                            .then_inc(s("e_comb"), 1)
                    else:
                        for q in range(2):
                            e = 2 * (i - 1) + q
                            last = nc.vector.scalar_tensor_tensor(
                                out=hN[:, b, :], in0=PB[v % 8][0:T, D * q:D * q + D], scalar=we[:, b, e:e + 1],
                                in1=hN[:, b, :], op0=ALU.mult, op1=ALU.add)
                            if q == 0:
                                link(last)
                        last.then_inc(s("e_comb"), 1)
                    dve.wait_ge(s("e_comb"), v + 1)
                if b % 4 == 3:
                    dve.wait_ge(s("f_sq"), b + 1)
                    nc.vector.tensor_scalar(std[:, b - 3:b + 1], rsum[:, b - 3:b + 1], 1.0 / D, RMS_EPS,
                                            ALU.mult, ALU.add).then_inc(s("n_var"), 1)
                    dve.wait_ge(s("n_std"), turn("f") + b // 4 + 1)
                    for c in range(b - 3, b + 1):
                        link(nc.vector.scalar_tensor_tensor(out=hN[:, c, :], in0=hN[:, c, :], scalar=rstd[:, c:c + 1],
                                                            in1=grow[:], op0=ALU.mult, op1=ALU.mult))
                        nc.vector.tensor_tensor(x[:, c, :], x[:, c, :], hN[:, c, :], ALU.add).then_inc(s("f_out"), 1)

        @block.tensor
        def _(pe):
            def mm(o, l, r, start, stop):
                return nc.tensor.matmul(o, l, r, start=start, stop=stop)

            def ln_pe(st):
                for g in range(NB // 2):
                    pe.wait_ge(s("n_hN"), NB * turn(st) + 2 * g + 2)
                    if g >= 2:
                        pe.wait_ge(s("n_hT"), NB // 2 * turn(st) + g - 1)
                    for k in range(KT):
                        for bb in range(2):
                            at = (2 * k + bb) * T
                            last = nc.tensor.transpose(PB[g % 2][:, at:at + T], hN[:, 2 * g + bb, 128 * k:128 * k + 128],
                                                       ident[0:T, 0:T])
                    last.then_inc(s("n_tp"), 1)

            pe.wait_ge(s("ld_w0"), 64)
            pe.wait_ge(s("ld_const"), 16)
            for m in range(KT):
                for k in range(KT):
                    mm(PB[2][:, m * D:(m + 1) * D], wq0[:, k, 128 * m:128 * m + 128], wk0[:, k, :], k == 0, k == KT - 1)
            for v, (w, bias) in enumerate(((wk0, 0), (wq0, 1))):
                for m in range(KT):
                    for k in range(KT):
                        mm(PB[3][:, 2 * v + m:2 * v + m + 1], w[:, k, 128 * m:128 * m + 128], bqk[:, bias, k:k + 1],
                           k == 0, k == KT - 1)
            for k in range(KT):
                last = mm(PB[3][0:1, 4:5], bqk[:, 1, k:k + 1], bqk[:, 0, k:k + 1], k == 0, k == KT - 1)
            last.then_inc(s("a_fold"), 1)
            ln_pe("a")
            pe.wait_ge(s("a_foldsb"), 1)
            pe.wait_ge(s("n_hT"), NB // 2 * (turn("a") + 1))
            for u in range(2 * KT):
                n, half = u // 2, u % 2
                if u >= 2:
                    pe.wait_ge(s("a_tsb"), u - 1)
                for m in range(KT):
                    last = mm(PB[4 + u % 2][:, 0:HALF], fold[:, m, 128 * n:128 * n + 128],
                              hT[:, m, HALF * half:HALF * (half + 1)], m == 0, m == KT - 1)
                last.then_inc(s("a_t"), 1)
            for half in range(2):
                for m in range(KT):
                    last = mm(PB[6 + half][0:1, 0:HALF], foldv[:, 2 + m:3 + m], hT[:, m, HALF * half:HALF * (half + 1)],
                              m == 0, m == KT - 1)
                last.then_inc(s("a_c"), 1)
            pe.wait_ge(s("a_tsb"), 2 * KT)
            pe.wait_ge(s("a_csb"), 2)
            pe.wait_ge(s("ld_ctxT"), 16 * KT)
            pe.wait_ge(s("ld_ctxN"), 16 * NJ)
            pe.wait_ge(s("set_ones"), 1)
            for b in range(NB):
                last = nc.tensor.transpose(PB[3][0:T, b:b + 1], cT[0:1, T * b:T * b + T], ident[0:1, 0:1])
            last.then_inc(s("a_cc"), 1)
            pe.wait_ge(s("a_ccsb"), 1)
            for i in range(NB + 4):
                if 2 <= i < NB + 2:
                    b = i - 2
                    pe.wait_ge(s("a_p"), b + 1)
                    if b >= 2:
                        pe.wait_ge(s("a_ptsb"), b - 1)
                    for j in range(NJ):
                        last = nc.tensor.transpose(PB[2 + b % 2][0:KEYS, T * j:T * j + T],
                                                   prob[:, b % NP_, KEYS * j:KEYS * j + KEYS], ident[0:T, 0:T])
                    last.then_inc(s("a_pt"), 1)
                if i < NB:
                    b = i
                    if b >= 3:
                        pe.wait_ge(s("a_max"), b - 2)
                    for n in range(KT):
                        last = mm(PB[SB[b % 3]][0:T, 0:CTX], tT[:, n, T * b:T * b + T], ctxT[:, n, b, 0:CTX],
                                  n == 0, n == KT - 1)
                    last.then_inc(s("a_s"), 1)
                if 2 <= i < NB + 2:
                    b = i - 2
                    pe.wait_ge(s("a_ptsb"), b + 1)
                    if b >= 1:
                        pe.wait_ge(s("a_mixsb"), b)
                    for j in range(NJ):
                        last = mm(PB[4][0:T, 0:D], pT[0:KEYS, b % 2, T * j:T * j + T], ctxN[0:KEYS, b, j, :],
                                  j == 0, j == NJ - 1)
                    last.then_inc(s("a_mix"), 1)
                if 3 <= i < NB + 3:
                    b = i - 3
                    pe.wait_ge(s("a_mixsb"), b + 1)
                    if b >= 1:
                        pe.wait_ge(s("a_mtsb"), b)
                    for d in range(KT):
                        last = nc.tensor.transpose(PB[5][:, T * d:T * d + T], mix[:, b % 2, 128 * d:128 * d + 128],
                                                   ident[0:T, 0:T])
                    last.then_inc(s("a_mt"), 1)
                if i >= 4:
                    b = i - 4
                    pe.wait_ge(s("a_mtsb"), b + 1)
                    if b >= 1:
                        pe.wait_ge(s("a_res"), b)
                    for d in range(KT):
                        last = mm(PB[6][0:T, 0:D], mixT[:, b % 2, d, :], wv0[:, d, :], d == 0, d == KT - 1)
                    last.then_inc(s("a_y"), 1)
            ln_pe("b")
            pe.wait_ge(s("ld_wb"), 64)
            pe.wait_ge(s("n_hT"), NB // 2 * (turn("b") + 1))
            for half in range(2):
                for k in range(KT):
                    last = mm(PB[2 + half][0:NE, 0:HALF], wr[:, k, :], hT[:, k, HALF * half:HALF * (half + 1)],
                              k == 0, k == KT - 1)
                last.then_inc(s("b_lgT"), 1)
            pe.wait_ge(s("b_lgTsb"), 2)
            for b in range(NB):
                last = nc.tensor.transpose(PB[4][0:T, NE * b:NE * b + NE], lgT[:, T * b:T * b + T], ident[0:NE, 0:NE])
            last.then_inc(s("b_lg"), 1)

            def shared_gu(u):
                f, half = u // 2, u % 2
                if u >= 4:
                    pe.wait_ge(s("b_hid"), u - 3)
                for w in range(2):
                    for k in range(KT):
                        last = mm(PB[(2 * u + w) % 8][:, 0:HALF], wgu[:, k, w, 128 * f:128 * f + 128],
                                  hT[:, k, HALF * half:HALF * (half + 1)], k == 0, k == KT - 1)
                last.then_inc(s("b_sgu"), 1)

            shared_gu(0)
            shared_gu(1)
            pe.wait_ge(s("b_oh"), 1)
            mm(PB[5][0:T, 0:NB * NE], consts[0:T, cs["lower"]], oh[:].rearrange("p b e -> p (b e)"), True, False)
            mm(PB[5][0:T, 0:NB * NE], ones[0:T, 0:T], pre[:].rearrange("p b e -> p (b e)"), False, True) \
                .then_inc(s("b_pos"), 1)
            pe.wait_ge(s("b_slot"), 1)
            mm(PB[5][0:1, 0:NB], ones[0:T, 0:1], r1[:, 5, :], True, True).then_inc(s("o_count"), 1)
            pe.wait_ge(s("o_flag"), 1)
            for u in range(2, 2 * FT):
                shared_gu(u)
            pe.wait_ge(s("b_hid"), 2 * FT)

            def slots_T(i):
                pe.wait_ge(s(f"b_xg{i // 2}"), 16)
                if i >= 1:
                    pe.wait_ge(s("b_xtsb"), i)
                for k in range(KT):
                    last = nc.tensor.transpose(PB[6][:, 128 * k:128 * k + 128], xg[:, i, 128 * k:128 * k + 128], ident)
                last.then_inc(s("b_xt"), 1)

            slots_T(0)
            for i in range(NPAIR + 1):
                if i < NPAIR:
                    pe.wait_ge(s("b_xtsb"), i + 1)
                    pe.wait_ge(s(f"ld_ring{i % RING}"), 64 * (i // RING + 1))
                    if i >= 2:
                        pe.wait_ge(s("b_au"), i - 1)
                    for w in range(2):
                        for k in range(KT):
                            for e in range(2):
                                at = (2 * k + w) * F
                                last = mm(PB[2 * (i % 2) + w][CAP * e:CAP * e + CAP, :], xgT[:, i % 2, k, CAP * e:CAP * e + CAP],
                                          pairs[i % RING][:, e, at:at + F], k == 0, k == KT - 1)
                    last.then_inc(s("b_gu"), 1)
                if i + 1 < NPAIR:
                    slots_T(i + 1)
                if i >= 1:
                    p = i - 1
                    pe.wait_ge(s("b_au"), p + 1)
                    if p >= 1:
                        pe.wait_ge(s("b_atsb"), p)
                    for f in range(FT):
                        last = nc.tensor.transpose(PB[4][:, 128 * f:128 * f + 128], au[:, p % 2, 128 * f:128 * f + 128], ident)
                    last.then_inc(s("b_at"), 1)
                    if p >= 1:
                        pe.wait_ge(s("b_sdres"), p)
                    for f in range(FT):
                        last = mm(PB[7][0:T, 0:D], hid[:, f, T * p:T * p + T], wdn[:, f, :], f == 0, f == FT - 1)
                    last.then_inc(s("b_sd"), 1)
                    pe.wait_ge(s("b_atsb"), p + 1)
                    if p >= 1:
                        pe.wait_ge(s("b_ysb"), p)
                    for f in range(FT):
                        for e in range(2):
                            last = mm(PB[5][CAP * e:CAP * e + CAP, 0:D], auT[:, p % 2, f, CAP * e:CAP * e + CAP],
                                      pairs[p % RING][:, e, GU + D * f:GU + D * f + D], f == 0, f == FT - 1)
                    last.then_inc(s("b_y"), 1)
            over = pe.value_load(flag[0:1, 0:1], min_val=0, max_val=NT)
            with pe.If(over > 0):
                pe.wait_ge(s("b_ysb"), NPAIR)
                with pe.Fori(0, NE) as e:
                    pe.wait_ge(s("o_ld"), 32 * e + 32)
                    pe.wait_ge(s("o_col"), e + 1)
                    for b in range(NB):
                        pe.wait_ge(s("o_res"), NB * e + (b + 1))
                        for w in range(2):
                            for k in range(KT):
                                at = (2 * k + w) * F
                                last = mm(PB[w][0:T, :], hT[:, k, T * b:T * b + T], ring[:, 0, 0, at:at + F],
                                          k == 0, k == KT - 1)
                        last.then_inc(s("o_gu"), 1)
                        pe.wait_ge(s("o_au"), NB * e + (b + 1))
                        for f in range(FT):
                            last = nc.tensor.transpose(PB[4][:, T * f:T * f + T], au[0:T, 0, 128 * f:128 * f + 128],
                                                       ident[0:T, 0:T])
                        last.then_inc(s("o_at"), 1)
                        pe.wait_ge(s("o_atsb"), NB * e + (b + 1))
                        for f in range(FT):
                            last = mm(PB[5][0:T, 0:D], auT[:, 0, f, 0:T], ring[:, 0, 0, GU + D * f:GU + D * f + D],
                                      f == 0, f == FT - 1)
                        last.then_inc(s("o_y"), 1)
            pe.wait_ge(s("ld_wc"), 16 * 13)
            pe.wait_ge(s("ld_ctxT"), 32 * KT)

            def queries(st, w):
                pe.wait_ge(s("n_hT"), NB // 2 * (turn(st) + 1))
                for u in range(2 * KT):
                    n, half = u // 2, u % 2
                    if u >= 2:
                        pe.wait_ge(s(st + "_qsb"), u - 1)
                    for m in range(KT):
                        last = mm(PB[4 + u % 2][:, 0:HALF], w[:, m, 128 * n:128 * n + 128],
                                  hT[:, m, HALF * half:HALF * (half + 1)], m == 0, m == KT - 1)
                    last.then_inc(s(st + "_q"), 1)

            def kv_part(b, i):
                if 5 * b + i >= 1:
                    pe.wait_ge(s("c_prsb"), 5 * b + i)
                if b >= 2 and i == 2:
                    pe.wait_ge(s("c_res"), b - 1)
                for k in range(KT):
                    if i < KT:
                        last = mm(PB[6][:, 0:CPAD], wc[:, 1, k, 128 * i:128 * i + 128], ctxT[:, k, b, :], k == 0, k == KT - 1)
                    else:
                        j = i - KT
                        last = mm(PB[6][0:KEYS, 0:D], ctxT[:, k, b, KEYS * j:KEYS * j + KEYS], wc[:, 2, k, :],
                                  k == 0, k == KT - 1)
                last.then_inc(s("c_pr"), 1)

            def out_projection(b, st, w):
                pe.wait_ge(s(st + "_att"), b + 1)
                if st == "c":
                    pe.wait_ge(s("c_prsb"), 5 * (b + 2) + 2 if b + 2 < NB else 5 * NB)
                else:
                    pe.wait_ge(s("d_vsb"), min(b + 3, NB))
                if b >= 1:
                    pe.wait_ge(s("c_res" if st == "c" else "d_x2"), b)
                for g in range(NG):
                    last = mm(PB[6][0:T, 0:D], attT[:, b % 2, g, :], w[:, g, :], g == 0, g == NG - 1)
                last.then_inc(s(st + "_y"), 1)

            for b in range(2):
                for i in range(5):
                    kv_part(b, i)
            ln_pe("c")
            queries("c", wc[:, 0])
            pe.wait_ge(s("c_vones"), 1)
            pe.wait_ge(s("c_qsb"), 2 * KT)
            for n in range(NB * NH + 3):
                b, h = n // NH, n % NH
                if n < NB * NH:
                    if h == 0:
                        pe.wait_ge(s("c_qbd"), b + 1)
                        pe.wait_ge(s("c_prsb"), 5 * b + 5)
                    if n >= 3:
                        pe.wait_ge(s("c_p"), n - 2)
                    mm(PB[SB[n % 3]][0:T, 0:CTX], qbd[:, b % 2, h // 8, T * (h % 8):T * (h % 8) + T], kT[:, b % 2, h // 8, 0:CTX],
                       True, True).then_inc(s("c_s"), 1)
                if 2 <= n <= NB * NH + 1:
                    m = n - 2
                    pe.wait_ge(s("c_p"), m + 1)
                    if m >= 2:
                        pe.wait_ge(s("c_ptsb"), m - 1)
                    for j in range(NJ):
                        last = nc.tensor.transpose(PB[2 + m % 2][0:KEYS, T * j:T * j + T],
                                                   prob[:, m % 4, KEYS * j:KEYS * j + KEYS], ident[0:T, 0:T])
                    last.then_inc(s("c_pt"), 1)
                if n >= 3 and (n - 3) % 4 == 3:
                    quad = (n - 3) // 4
                    bq, g = quad // NG, quad % NG
                    pe.wait_ge(s("c_ptsb"), 4 * quad + 4)
                    if g == 0 and bq >= 2:
                        pe.wait_ge(s("c_att"), bq - 1)
                    for j in range(NJ):
                        for q in range(4):
                            hh = 4 * g + q
                            last = mm(PB[4 + bq % 2][32 * q:32 * q + 32, T * g:T * g + T],
                                      vpad[0:KEYS, bq % 2, j, 32 * hh:32 * hh + 32],
                                      pTq[0:KEYS, (4 * quad + q) % 8, T * j:T * j + T], j == 0, j == NJ - 1)
                    last.then_inc(s("c_av"), 1)
                if 1 <= b < NB - 1 and h in KV_AT:
                    kv_part(b + 1, KV_AT.index(h))
                if 1 <= b < NB and h == 6:
                    out_projection(b - 1, "c", wo[:, 0])
            out_projection(NB - 1, "c", wo[:, 0])
            ln_pe("d")
            pe.wait_ge(s("ld_wd"), 16 * 14)
            queries("d", wq2)
            for half in range(2):
                for k in range(KT):
                    last = mm(PB[6 + half][:, 0:HALF], wkvc[:, k, :], hT[:, k, HALF * half:HALF * (half + 1)],
                              k == 0, k == KT - 1)
                last.then_inc(s("d_kvc"), 1)
            pe.wait_ge(s("d_kvcsb"), 2)
            pe.wait_ge(s("d_qsb"), 2 * KT)
            for u in range(2 * KT):
                n, half = u // 2, u % 2
                if u >= 2:
                    pe.wait_ge(s("d_ksb"), u - 1)
                mm(PB[4 + u % 2][:, 0:HALF], wkv2[:, 0, 128 * n:128 * n + 128], kvcT[:, HALF * half:HALF * (half + 1)],
                   True, True).then_inc(s("d_k"), 1)

            def values(b):
                if b >= 1:
                    pe.wait_ge(s("d_vsb"), b)
                if b >= 3:
                    pe.wait_ge(s("d_x2"), b - 2)
                mm(PB[6][0:T, 0:D], kvcT[:, T * b:T * b + T], wkv2[:, 1, :], True, True).then_inc(s("d_v"), 1)

            values(0)
            pe.wait_ge(s("d_rot"), 2)
            for n in range(4 * NB + 3):
                b, g = n // 4, n % 4
                if n < 4 * NB:
                    if g == 0:
                        pe.wait_ge(s("d_qbd"), b + 1)
                    if n >= 3:
                        pe.wait_ge(s("d_shift"), n - 2)
                    for q in range(4):
                        h = 4 * g + q
                        last = mm(PB[SB[n % 3]][0:T, T * q:T * q + T], qbd[:, b % 2, h // 8, T * (h % 8):T * (h % 8) + T],
                                  krT[:, h // 8, T * b:T * b + T], True, True)
                    last.then_inc(s("d_s"), 1)
                if 2 <= n <= 4 * NB + 1:
                    m = n - 2
                    pe.wait_ge(s("d_p"), m + 1)
                    if m >= 2:
                        pe.wait_ge(s("d_ptsb"), m - 1)
                    for q in range(4):
                        last = nc.tensor.transpose(PB[2 + m % 2][0:T, T * q:T * q + T], prob4[:, m % 3, T * q:T * q + T],
                                                   ident[0:T, 0:T])
                    last.then_inc(s("d_pt"), 1)
                if n >= 3:
                    m = n - 3
                    bq, g2 = m // 4, m % 4
                    pe.wait_ge(s("d_ptsb"), m + 1)
                    if g2 == 0:
                        pe.wait_ge(s("d_vsb"), bq + 1)
                        if bq >= 2:
                            pe.wait_ge(s("d_att"), bq - 1)
                    for q in range(4):
                        hh = 4 * g2 + q
                        last = mm(PB[4 + bq % 2][32 * q:32 * q + 32, T * g2:T * g2 + T],
                                  vpad[0:T, bq % 2, 0, 32 * hh:32 * hh + 32], pT4[0:T, m % 2, T * q:T * q + T], True, True)
                    last.then_inc(s("d_av"), 1)
                if g == 0 and 1 <= b < NB:
                    values(b)
                if 2 <= b < NB and g == 2:
                    out_projection(b - 2, "d", wo[:, 1])
            out_projection(NB - 2, "d", wo[:, 1])
            out_projection(NB - 1, "d", wo[:, 1])
            ln_pe("e")
            pe.wait_ge(s("n_hT"), NB // 2 * (turn("e") + 1))
            for half in range(2):
                for k in range(KT):
                    last = mm(PB[2 + half][0:2 + NX, 0:HALF], wge[:, k, :], hT[:, k, HALF * half:HALF * (half + 1)],
                              k == 0, k == KT - 1)
                last.then_inc(s("e_gT"), 1)

            def e_gu(u):
                which, f, half = u // (2 * FT), u // 2 % FT, u % 2
                if u >= 4:
                    pe.wait_ge(s("e_hid"), u - 3)
                for w in range(2):
                    for k in range(KT):
                        last = mm(PB[(2 * u + w) % 8][:, 0:HALF], wgu2[:, which, k, F * w + 128 * f:F * w + 128 * f + 128],
                                  hT[:, k, HALF * half:HALF * (half + 1)], k == 0, k == KT - 1)
                last.then_inc(s("e_gu"), 1)

            e_gu(0)
            pe.wait_ge(s("e_gTsb"), 2)
            for b in range(NB):
                n = 2 + NX
                last = nc.tensor.transpose(PB[4][0:T, n * b:n * b + n], row_T[0:n, T * b:T * b + T], ident[0:n, 0:n])
            last.then_inc(s("e_g"), 1)
            e_gu(1)
            pe.wait_ge(s("e_gx"), 1)
            for u in range(2, 4 * FT):
                e_gu(u)
            pe.wait_ge(s("e_hid"), 4 * FT)
            for b in range(NB):
                for i in range(5):
                    v = 5 * b + i
                    if v >= 8:
                        pe.wait_ge(s("e_comb"), v - 7)
                    for f in range(FT):
                        if i == 0:
                            last = mm(PB[v % 8][0:T, 0:D], hid2[:, 0, f, T * b:T * b + T], wdn[:, f, :], f == 0, f == FT - 1)
                        else:
                            last = mm(PB[v % 8][0:T, :], hid2[:, 1, f, T * b:T * b + T],
                                      w2[:, f, 2 * (i - 1):2 * i, :].rearrange("p e d -> p (e d)"), f == 0, f == FT - 1)
                    last.then_inc(s("e_down"), 1)


def kernel(**inputs):
    import concourse.bacc as bacc
    from concourse.bass_utils import run_bass_kernel_spmd
    nc = bacc.Bacc("TRN2", target_bir_lowering=False, num_devices=1)
    arrays = {n: np.ascontiguousarray(v) for n, v in inputs.items()}
    arrays["x"] = np.ascontiguousarray(arrays["x"].transpose(1, 0, 2))
    context = arrays.pop("ctx_1024")
    arrays["ctx"] = context
    arrays["ctxT"] = np.ascontiguousarray(context.transpose(2, 0, 1))
    arrays["mask"] = np.ascontiguousarray(arrays.pop("mask_BxSxS2_bk1").transpose(1, 0, 2))
    for n in ("L0_xattn_Wv", "L0_ffn_w_router", "L0_ffn_w_gate", "L0_ffn_w_up", "L0_ffn_w_down",
              "L1_xattn_wq", "L1_xattn_wk", "L1_xattn_wv", "L1_xattn_wo"):
        arrays[n + "T"] = np.ascontiguousarray(arrays.pop(n).T)

    arrays["bqk"] = np.ascontiguousarray(
        np.stack([arrays.pop("L0_xattn_bq"), arrays.pop("L0_xattn_bk")]).reshape(2, KT, 128).transpose(2, 0, 1))

    cs, ncols = const_slices()
    c = np.zeros((128, ncols), np.float32)
    c[:, cs["ident"]] = np.eye(128)
    c[:, cs["headmask"]] = np.arange(128)[:, None] // DH == np.arange(8)[None, :]
    c[:T, cs["lower"]] = np.arange(T)[:, None] < np.arange(T)[None, :]
    freq = (1.0 / 10000.0 ** (np.arange(0, DH, 2, dtype=np.float32) / DH)).astype(np.float32)
    angle = (np.arange(T, dtype=np.float32)[None, :] * freq[:, None]).astype(np.float32)
    row = np.arange(128) % DH // 2
    c[:, cs["cos"]] = np.cos(angle)[row]
    c[:, cs["sin"]] = np.sin(angle)[row] * np.where(np.arange(128) % 2 == 0, -1.0, 1.0)[:, None]
    c[:, cs["rev16"]] = NE - np.arange(NE)
    c[:, cs["base16"]] = CAP * np.arange(NE)
    c[:, cs["rev8"]] = NX - np.arange(NX)
    arrays["consts"] = c

    A = {}
    for n, a in arrays.items():
        A[n] = nc.dram_tensor("in_" + n, a.shape, mybir.dt.from_np(a.dtype), kind="ExternalInput").ap()
    A["xs_dram"] = nc.dram_tensor("xs_dram", (NSLOT, D), mybir.dt.float32).ap()
    A["y_dram"] = nc.dram_tensor("y_dram", (NSLOT, D), mybir.dt.float32).ap()
    out = nc.dram_tensor("out", (NB, T, D), mybir.dt.float32, kind="ExternalOutput").ap()
    build(nc, A, out)
    r = run_bass_kernel_spmd(nc, [{"in_" + n: a for n, a in arrays.items()}], core_ids=[0])
    return r.results[0]["out"]
```

```python
import numpy as np
import concourse.bass as bass
from concourse import mybir
from contextlib import ExitStack

NB, T, D = 8, 100, 256
CTX = 361
KT = D // 128
KEYS = 121
NJ = 3
CPAD = KEYS * NJ
CEV = CTX + 1
NT = NB * T
HALF = NT // 2
NH, DH = 16, 16
NG = NH // 4
F = 512
FT = F // 128
NE, CAP = 16, 64
NPAIR = NE // 2
NSLOT = NE * CAP
FULL = CAP
SKIP = 1 << 20
NX, EPG = 8, 4
DC = 64
LN_EPS, RMS_EPS = 1e-5, 1e-6
NEG = -1000000000.0
RING = 3
LAST_IN_CTX = max(i for i in range(NPAIR) if i % RING == RING - 1)
STARTS = [0, 128, 256, 768, 384, 512, 640]
NF = len(STARTS)
TAIL = STARTS.index(NT // 128 * 128)
TAILN = NT % 128
WHOLE = [c for c in range(NF) if c != TAIL]
PARTS = [(0, 4), (4, 6), (6, 7)]
PIECES = [(c, max(a, T * b) - a, b, max(a, T * b) - T * b, min(a + 128, NT, T * b + T) - max(a, T * b))
          for c, a in enumerate(STARTS) for b in range(NB) if max(a, T * b) < min(a + 128, NT, T * b + T)]
SB = [0, 1, 7]
SBC = [0, 1, 7, 5]
KV_AT = [1, 3, 11, 13, 15]
ACT_COPIES = 0
HALVES = [slice(0, NG // 2 * T), slice(NG // 2 * T, NG * T)]
SWAP_PAIRS = [i ^ 1 for i in range(32)]
UPPER_HALF = [16 + i % 16 for i in range(32)]

CONSTS = dict(ident=128, headmask=8, lower=T, cos=T, sin=T, rev16=NE, base16=NE, rev8=NX)


def const_slices():
    at, out = 0, {}
    for name, width in CONSTS.items():
        out[name] = slice(at, at + width)
        at += width
    return out, at


def build(nc, A, out):
    f32, f32r, i32, u8 = mybir.dt.float32, mybir.dt.float32r, mybir.dt.int32, mybir.dt.uint8
    ALU, ACT, AX = mybir.AluOpType, mybir.ActivationFunctionType, mybir.AxisListType

    ctx = ExitStack()
    with ctx:
        def sb(name, shape, dt=f32):
            return ctx.enter_context(nc.sbuf_tensor(name, shape, dt))

        def sem(name):
            return ctx.enter_context(nc.semaphore(name))

        cs, ncols = const_slices()
        consts = sb("consts", [128, ncols])
        ident = consts[:, cs["ident"]]
        ones = sb("ones", [128, CPAD])
        zero_rows = sb("zero_rows", [128, D])
        minus_half = sb("minus_half", [128, NB])
        gates = sb("gates", [128, 4])
        tg = sb("tg", [128, 4])
        x = sb("x", [T, NB, D])
        hN = sb("hN", [T, NB, D])
        hT = sb("hT", [128, KT, NT])
        bn6 = sb("bn6", [T, NB, 6])
        mv = sb("mv", [T, NB, 2])
        std = sb("std", [T, NB])
        rstd = sb("rstd", [T, NB])
        GU = KT * 2 * F
        EW = GU + FT * D
        ctxbuf = sb("ctxbuf", [128, 2 * EW])
        ctxT = ctxbuf[:, 0:KT * NB * CPAD].rearrange("p (k b c) -> p k b c", k=KT, b=NB)
        brow = {n: sb("row_" + n, [128, D]) for n in ("bv", "bo", "n1", "n2")}
        grow = sb("grow", [T, D])
        big = sb("big", [128, NB * NJ * D + 256])
        ctxN = big[:, 0:NB * NJ * D].rearrange("p (b j d) -> p b j d", b=NB, j=NJ)
        arena = sb("arena", [128, 6656 + 320])

        def carve(start, *dims, rows=128):
            n = int(np.prod(dims))
            names = "abcd"[:len(dims)]
            part = arena[0:rows, start:start + n]
            if len(dims) == 1:
                return part
            return part.rearrange(f"p ({' '.join(names)}) -> p {' '.join(names)}",
                                  **dict(zip(names[:-1], dims[:-1])))

        W = KT * D
        wq0 = carve(0, KT, D)
        wk0 = carve(W, KT, D)
        wv0 = carve(2 * W, KT, D)
        fold = carve(3 * W, KT, D)
        keep = carve(4 * W, 2, CTX, rows=T)
        drop = carve(4 * W + 2 * CTX, 2, CTX, rows=T)
        sc = carve(4 * W + 4 * CTX, 2, CTX, rows=T)
        bqk = sb("bqk", [128, 2, KT])
        foldv = sb("foldv", [128, 4])
        fold0 = sb("fold0", [1, 1])
        tT = sb("tT", [128, KT, NT])
        sil = sb("sil", [128, 2, F])
        row_T = sil[:].rearrange("p a b -> p (a b)")
        cT = row_T[0:1, 0:NT]
        ccol = sb("ccol", [T, NB])
        mask8 = sb("mask8", [T, NB, CTX], u8)
        NP_ = 4
        prob = sb("prob", [T, NP_, CPAD])
        nmx = sb("nmx", [T, 4, NB])
        rsum = sb("rsum", [T, NB])
        rg = sb("rg", [T, NB])
        pT = carve(4 * W + 6 * CTX, 2, NJ * T)
        mixT = carve(4 * W + 6 * CTX + 2 * NJ * T, 2, KT, T)
        mix = carve(4 * W + 6 * CTX + 2 * NJ * T + 2 * D, 2, D, rows=T)
        wr = sb("wr", [128, KT, NE])
        wgu = sb("wgu", [128, KT, 2, F])
        wdn = sb("wdn", [128, FT, D])
        hid = big[:, 0:FT * NT].rearrange("p (f t) -> p f t", f=FT)
        lgT = row_T[0:NE, 0:NT]
        lg = sb("lg", [T, NB, NE])
        oh = sb("oh", [T, NB, NE])
        key = sb("key", [T, NB, NE])
        pre = sb("pre", [T, NB, NE])
        pos = sb("pos", [T, NB, NE])
        r1 = sb("r1", [T, 12, NB])
        slot = sb("slot", [T, NB], i32)
        oscale = sb("oscale", [T, NB, NE])
        ocol = sb("ocol", [T, NB])
        flag = sb("flag", [1, 1], i32)
        xs = carve(0, NB, D, rows=T)
        xg = carve(8 * D, NPAIR, D)
        au = carve(16 * D, 2, F)
        auT = carve(20 * D, 2, FT, 128)
        yb = carve(24 * D, 2, D)
        wc = sb("wc", [128, 3, KT, D])
        wo = sb("wo", [128, 2, NG, D])
        qT = tT
        kflat = big[:, 0:KT * NT]
        kraw = kflat[:, 0:2 * KT * CPAD].rearrange("p (u k c) -> p u k c", u=2, k=KT)
        krT = kflat.rearrange("p (k t) -> p k t", k=KT)
        vpad = carve(0, 2, NJ, NH * 32)
        qbd = carve(2 * NJ * NH * 32, 2, KT, 8 * T)
        den = big[:, 1600:1600 + NG * T]
        attT = big[:, 2000:2000 + 2 * NG * T].rearrange("p (u g t) -> p u g t", u=2, g=NG)
        xgT = big[:, FT * NT:FT * NT + 2 * KT * 128].rearrange("p (u k t) -> p u k t", u=2, k=KT)

        pTq = big[:, 2800:2800 + 8 * NJ * T].rearrange("p (u n) -> p u n", u=8)
        wflat = wgu[:].rearrange("p k w f -> p (k w f)")
        wq2 = wflat[:, 0:W].rearrange("p (k n) -> p k n", k=KT)
        wkvc = wflat[:, W:W + KT * 2 * DC].rearrange("p (k n) -> p k n", k=KT)
        wkv2 = wflat[:, 2 * W:2 * W + 2 * D].rearrange("p (w n) -> p w n", w=2)
        wge = wflat[:, 3 * W:3 * W + KT * (2 + NX)].rearrange("p (k n) -> p k n", k=KT)
        avsb = big[:, 5200:5200 + 2 * NG * T].rearrange("p (u g t) -> p u g t", u=2, g=NG)
        kvcT = big[:, 3600:3600 + NT]
        rot = big[:, 4400:4400 + KT * NT].rearrange("p (k t) -> p k t", k=KT)
        prob4 = prob[:].rearrange("t u n -> t (u n)")[:, 0:3 * 4 * T].rearrange("t (u n) -> t u n", u=3)
        pT4 = big[:, 2800:2800 + 2 * 4 * T].rearrange("p (u n) -> p u n", u=2)
        hid2 = big[:, 0:2 * FT * NT].rearrange("p (s f t) -> p s f t", s=2, f=FT)
        gbias = sb("gbias", [128, 2 + NX])
        taken = [0]

        def flat(*dims):
            a, taken[0] = taken[0], taken[0] + int(np.prod(dims))
            piece = ctxbuf[:, a:taken[0]]
            return piece if len(dims) == 1 else piece.rearrange("p (a b) -> p a b", a=dims[0])

        xF, hF = flat(NF, D), flat(NF, D)
        growF, acc = flat(D), flat(D)
        gl, ge, we = flat(NF, 2 + NX), flat(NF, 2 + NX), flat(NF, NX)
        r1F, ohF, keyF, posF = flat(12, NF), flat(NF, NX), flat(NF, NX), flat(NF, NX)
        stdF, rstdF, rsumF, wsel = flat(NF), flat(NF), flat(NF), flat(2)

        with nc.sbuf_tensor("ring", [128, RING - 1, 2, EW], f32) as ring:
            pass
        pairs = [ring[:, i] for i in range(RING - 1)] + [ctxbuf[:].rearrange("p (e n) -> p e n", e=2)]
        rflat = ring[:].rearrange("p r e n -> p (r e n)")
        w2 = rflat[:, 0:FT * NX * D].rearrange("p (f e d) -> p f e d", f=FT, e=NX)
        wgu2 = rflat[:, FT * NX * D:FT * NX * D + 2 * KT * 2 * F].rearrange("p (s k n) -> p s k n", s=2, k=KT)
        split = sb("split", [128, (RING - 1) * 2 * EW], f32r)

        def part(start, *dims):
            names = "abcd"[:len(dims)]
            return split[:, start:start + int(np.prod(dims))].rearrange(
                f"p ({' '.join(names)}) -> p {' '.join(names)}", **dict(zip(names[:-1], dims[:-1])))

        NHP = NH // 2
        K4W, Q4W, KXW, QXW = NHP * CEV, 2 * NHP * 2 * T, 2 * KT * CEV, 2 * KT * NT
        k4 = [part(0, NHP, CEV), part(K4W + Q4W + KXW, NHP, CEV)]
        q4 = part(K4W, 2, NHP, 2 * T)
        kx = part(K4W + Q4W, 2, KT, CEV)
        qx = part((RING - 1) * 2 * EW - QXW, 2, KT, NT)

        PB = [ctx.enter_context(nc.psum_tensor(f"pb{i}", [128, 512], f32)) for i in range(8)]

        def bank3(i, a, n, rows=128):
            return PB[i][0:rows, 0:a * n].rearrange("p (a n) -> p a n", a=a)

        S = {}

        def s(name):
            if name not in S:
                S[name] = sem(name)
            return S[name]

        names = ["ld_x", "ld_const", "ld_small", "ld_w0", "ld_ctxT", "ld_ctxN", "ld_mask", "ld_wb", "ld_wc",
                 "dve_step", "act_step", "stats", "set_ones", "set_zero", "set_pads", "stored"]
        names += ["n_var", "n_std", "n_hN", "n_tp", "n_hT"]
        turn = "abcdef".index
        LN_PARTS = dict(a=[(0, NB)], b=[(0, NB - 2), (NB - 2, NB)], c=[(0, NB)], d=[(0, NB - 1), (NB - 1, NB)],
                        e=[(0, NB - 2), (NB - 2, NB)], f=PARTS)

        def roots(st, part):
            return sum(len(LN_PARTS[t]) for t in "abcdef"[:turn(st)]) + part + 1

        names += ["a_fold", "a_foldsb", "a_t", "a_tsb", "a_c", "a_csb", "a_mask", "a_s", "a_max", "a_p", "a_cc", "a_ccsb", "a_pt",
                  "a_ptsb", "a_mix", "a_mixsb", "a_mt", "a_mtsb", "a_y", "a_res"]
        names += ["ld_ring0", "ld_ring1", "ld_ring2", "ld_down0", "ld_down1", "ld_down2", "b_zero", "lgT", "lgTsb", "lg", "b_mx", "b_sig", "b_oh", "b_pos", "b_slot",
                  "b_xs", "b_scat", "b_xg0", "b_xg1", "b_xg2", "b_xg3", "b_sgu", "b_sil", "b_hid", "b_xt", "b_xtsb",
                  "b_gu", "b_esil", "b_au", "b_at", "b_atsb", "b_sd", "b_sdres", "b_y", "b_ysb", "b_yst0", "b_yst1",
                  "b_clear", "b_gat0", "b_gat1", "b_res"]
        names += ["o_flag", "o_ld", "o_gu", "o_sil", "o_au", "o_col", "o_at", "o_atsb", "o_y", "o_res"]
        names += ["ld_wd", "ld_we", "c_vones", "qry", "qry_sb", "c_kh", "c_kl", "c_kst", "c_k4_0", "c_k4_1",
                  "c_qh", "c_ql", "c_qst", "c_q4_0", "c_q4_1", "c_pr", "c_prsb", "c_s", "c_max", "c_p", "c_pt", "c_ptsb",
                  "c_pta", "c_av", "c_avsb", "c_att", "c_y", "c_res"]
        names += ["d_kvc", "d_kvcsb", "d_k", "d_ksb", "d_swap", "d_cos", "d_rot", "d_qbd", "d_v", "d_vsb", "d_s", "d_max", "d_p",
                  "d_pt", "d_ptsb", "d_av", "d_att", "d_y", "d_x2", "d_sq", 
                  "e_gx", "e_gexp", "e_gu", "e_sil", "e_hid", "e_down", "e_comb", "e_tailx", "e_acc", "e_tail", "ld_F", "f_sq",
                  "f_out"]
        for n in names:
            s(n)

        xs_dram, y_dram, kx_dram, qx_dram = A["xs_dram"], A["y_dram"], A["kx_dram"], A["qx_dram"]
        block = ctx.enter_context(nc.Block())

        @block.sync
        def _(sp):
            sp.dma_start(x[:], A["x"]).then_inc(s("ld_x"), 16)
            sp.dma_start(consts[:], A["consts"]).then_inc(s("ld_const"), 16)
            for i, n in enumerate(("L0_xattn_Wq", "L0_xattn_Wk", "L0_xattn_WvT")):
                sp.dma_start((wq0, wk0, wv0)[i][:], A[n].rearrange("(k p) n -> p k n", p=128)).then_inc(s("ld_w0"), 16)
            sp.dma_start(bqk[:], A["bqk"]).then_inc(s("ld_w0"), 16)
            for i, n in enumerate(("g_xattn", "g_ffn")):
                sp.dma_start(gates[:, 2 * i:2 * i + 2], A[n].partition_broadcast(128)).then_inc(s("ld_small"), 16)
            for n, w in (("bv", "L0_xattn_bv"), ("bo", "L1_xattn_bo"), ("n1", "L1_ffn_norm1_w"), ("n2", "L1_ffn_norm2_w")):
                sp.dma_start(brow[n][:], A[w].partition_broadcast(128)).then_inc(s("ld_small"), 16)
            sp.dma_start(mask8[:], A["mask"]).then_inc(s("ld_mask"), 16)
            for k in range(KT):
                sp.dma_start(ctxT[:, k, :, 0:CTX], A["ctxT"][128 * k:128 * k + 128]).then_inc(s("ld_ctxT"), 16)
            sp.wait_ge(s("set_pads"), 1)
            for j in range(NJ):
                n = min(KEYS, CTX - KEYS * j)
                sp.dma_start(ctxN[0:n, :, j, :], A["ctx"][:, KEYS * j:KEYS * j + n, :].rearrange("b p d -> p b d")) \
                    .then_inc(s("ld_ctxN"), 16)
            sp.wait_ge(s("set_zero"), 1)
            for i in range(NPAIR):
                sp.dma_start(xs_dram[128 * i:128 * i + 128, :], zero_rows[:]).then_inc(s("b_zero"), 16)
            sp.dma_start(wr[:], A["L0_ffn_w_routerT"].rearrange("(k p) n -> p k n", p=128)).then_inc(s("ld_wb"), 16)
            for i, n in enumerate(("L0_ffn_w_gateT", "L0_ffn_w_upT")):
                sp.dma_start(wgu[:, :, i, :], A[n].rearrange("(k p) n -> p k n", p=128)).then_inc(s("ld_wb"), 16)
            sp.dma_start(wdn[:], A["L0_ffn_w_downT"].rearrange("(k p) n -> p k n", p=128)).then_inc(s("ld_wb"), 16)

            for i, n in enumerate(("L1_xattn_wqT", "L1_xattn_wkT", "L1_xattn_wvT")):
                sp.dma_start(wc[:, i], A[n].rearrange("(k p) n -> p k n", p=128)).then_inc(s("ld_wc"), 16)
            for i, n in enumerate(("L1_xattn_woT", "L1_ffn_Wo")):
                for j in range(4):
                    sp.dma_start(wo[32 * j:32 * j + DH, i], A[n].rearrange("(g j d) n -> j d g n", j=4, d=DH)[j]) \
                        .then_inc(s("ld_wc"), 16)
            sp.dma_start(gbias[:, 0:2], A["L1_ffn_group_bias"].partition_broadcast(128)).then_inc(s("ld_wc"), 16)
            sp.dma_start(gbias[:, 2:], A["L1_ffn_expert_bias"].partition_broadcast(128)).then_inc(s("ld_wc"), 16)

            def load_gate_up(i):
                for e in range(2):
                    sp.dma_start(pairs[i % RING][:, e, 0:GU].rearrange("p (k n) -> p k n", k=KT),
                                 A["L0_ffn_gate_up_proj"][2 * i + e].rearrange("(k p) n -> p k n", p=128)) \
                        .then_inc(s(f"ld_ring{i % RING}"), 16)

            def load_down(i):
                for e in range(2):
                    sp.dma_start(pairs[i % RING][:, e, GU:].rearrange("p (k n) -> p k n", k=FT),
                                 A["L0_ffn_down_proj"][2 * i + e].rearrange("(k p) n -> p k n", p=128)) \
                        .then_inc(s(f"ld_down{i % RING}"), 16)

            for i in range(RING - 1):
                load_gate_up(i)
                load_down(i)
            sp.wait_ge(s("a_s"), NB)
            load_gate_up(RING - 1)
            load_down(RING - 1)
            sp.wait_ge(s("b_scat"), 16 * NB)
            for g in range(4):
                sp.dma_start(xg[:, 2 * g:2 * g + 2, :],
                             xs_dram[256 * g:256 * g + 256, :].rearrange("(i p) d -> p i d", p=128)) \
                    .then_inc(s(f"b_xg{g}"), 16)
            for i in range(NPAIR):
                if i + RING < NPAIR:
                    sp.wait_ge(s("b_gu"), i + 1)
                    load_gate_up(i + RING)
                sp.wait_ge(s("b_ysb"), i + 1)
                sp.dma_start(y_dram[128 * i:128 * i + 128, :], yb[:, i % 2, :]).then_inc(s(f"b_yst{i % 2}"), 16)
                if i + RING < NPAIR:
                    load_down(i + RING)
                if i == LAST_IN_CTX:
                    sp.wait_ge(s("set_pads"), 2)
                    for k in range(KT):
                        sp.dma_start(ctxT[:, k, :, 0:CTX], A["ctxT"][128 * k:128 * k + 128]).then_inc(s("ld_ctxT"), 16)
            sp.wait_ge(s("b_y"), NPAIR)
            sp.wait_ge(s("o_flag"), 1)
            over = sp.value_load(flag[0:1, 0:1], min_val=0, max_val=NT)
            with sp.If(over > 0):
                with sp.Fori(0, NE) as e:
                    sp.wait_ge(s("o_res"), NB * e + 1)
                    sp.dma_start(ring[:, 0, 0, 0:GU].rearrange("p (k n) -> p k n", k=KT),
                                 A["L0_ffn_gate_up_proj"][bass.ds(e, 1)].rearrange("e (k p) n -> p (e k) n", p=128)) \
                        .then_inc(s("o_ld"), 16)
                    sp.dma_start(ring[:, 0, 0, GU:].rearrange("p (k n) -> p k n", k=FT),
                                 A["L0_ffn_down_proj"][bass.ds(e, 1)].rearrange("e (k p) n -> p (e k) n", p=128)) \
                        .then_inc(s("o_ld"), 16)
                sp.wait_ge(s("o_res"), NB * NE + 1)
            sp.wait_ge(s("b_y"), NPAIR)
            sp.wait_ge(s("b_clear"), 2)
            sp.dma_start(wq2, A["L1_ffn_Wq"].rearrange("(k p) n -> p k n", p=128)).then_inc(s("ld_wd"), 16)
            sp.dma_start(wkvc[:, :, 0:DC], A["L1_ffn_Wk_c"].rearrange("(k p) n -> p k n", p=128)).then_inc(s("ld_wd"), 16)
            sp.dma_start(wkvc[:, :, DC:], A["L1_ffn_Wv_c"].rearrange("(k p) n -> p k n", p=128)).then_inc(s("ld_wd"), 16)
            sp.dma_start(wkv2[0:DC, 0], A["L1_ffn_Wk"]).then_inc(s("ld_wd"), 16)
            sp.dma_start(wkv2[DC:, 1], A["L1_ffn_Wv"]).then_inc(s("ld_wd"), 16)
            sp.dma_start(wge[:, :, 0:2], A["L1_ffn_Wg_gate"].rearrange("(k p) n -> p k n", p=128)).then_inc(s("ld_wd"), 16)
            sp.dma_start(wge[:, :, 2:], A["L1_ffn_We_gate"].rearrange("(k p) n -> p k n", p=128)).then_inc(s("ld_wd"), 16)
            sp.dma_start(wdn[:], A["L1_ffn_W_shared_out"].rearrange("(k p) n -> p k n", p=128)).then_inc(s("ld_wd"), 16)
            def store_k(b):
                sp.wait_ge(s("c_kl"), b + 1)
                for hl in range(2):
                    sp.dma_start(kx_dram[b, hl].rearrange("(k p) c -> p k c", p=128), kx[:, hl].bitcast(f32)).then_inc(s("c_kst"), 16)

            def load_k(b):
                sp.wait_ge(s("c_kst"), 32 * (b + 1))
                if b >= 2:
                    sp.wait_ge(s("c_s"), NH * (b - 1))
                for odd in range(2):
                    for r in range(4):
                        at = 64 * odd + DH * r
                        sp.dma_start(k4[b % 2][at:at + DH].bitcast(f32),
                                     kx_dram[b, r % 2].rearrange("(h o d) c -> o d h c", o=2, d=DH)[odd]) \
                            .then_inc(s(f"c_k4_{b % 2}"), 16)

            def store_q(half):
                sp.wait_ge(s("c_ql"), half + 1)
                for hl in range(2):
                    sp.dma_start(qx_dram[hl, :, HALF * half:HALF * (half + 1)].rearrange("(k p) c -> p k c", p=128),
                                 qx[:, hl, :, HALF * half:HALF * (half + 1)].bitcast(f32)).then_inc(s("c_qst"), 16)

            def load_q(two):
                if two >= 2:
                    sp.wait_ge(s("c_s"), 2 * NH * (two - 1))
                for odd in range(2):
                    for r in range(4):
                        at = 64 * odd + DH * r
                        sp.dma_start(q4[at:at + DH, two % 2].bitcast(f32),
                                     qx_dram[r // 2, :, 2 * T * two:2 * T * (two + 1)]
                                     .rearrange("(h o d) c -> o d h c", o=2, d=DH)[odd]).then_inc(s(f"c_q4_{two % 2}"), 16)

            store_k(0)
            load_k(0)
            store_q(0)
            sp.wait_ge(s("c_qst"), 32)
            load_q(0)
            load_q(1)
            store_q(1)
            store_k(1)
            sp.wait_ge(s("c_qst"), 64)
            load_k(1)
            for b in range(2, NB):
                store_k(b)
                load_k(b)
                if b >= 4 and b % 2 == 0:
                    load_q(b // 2)
            sp.wait_ge(s("c_s"), NB * NH)
            for i, n in enumerate(("L1_ffn_W_shared_in", "L1_ffn_W1_shared")):
                sp.dma_start(wgu2[:, i], A[n].rearrange("(k p) n -> p k n", p=128)).then_inc(s("ld_we"), 16)
            for f in range(FT):
                sp.dma_start(w2[:, f], A["L1_ffn_W2_experts"][:, 128 * f:128 * f + 128, :].rearrange("e p d -> p e d")) \
                    .then_inc(s("ld_we"), 16)
            for done, count, src, dst in (("c_res", NB, x, xF), ("n_hN", NB * (turn("e") + 1), hN, hF)):
                sp.wait_ge(s(done), count)
                for c, at, b, row, n in PIECES:
                    sp.dma_start(dst[at:at + n, c, :], src[row:row + n, b, :]).then_inc(s("ld_F"), 16)
            flat_out = out.rearrange("b t d -> (b t) d")
            sp.wait_ge(s("f_out"), TAIL)
            sp.dma_start(flat_out[0:128 * TAIL].rearrange("(i p) d -> p i d", p=128), xF[:, 0:TAIL, :]) \
                .then_inc(s("stored"), 16)
            for c in range(TAIL, NF):
                n = TAILN if c == TAIL else 128
                sp.wait_ge(s("f_out"), c + 1)
                sp.dma_start(flat_out[STARTS[c]:STARTS[c] + n], xF[0:n, c, :]).then_inc(s("stored"), 16)
            sp.wait_ge(s("stored"), 16 * (1 + NF - TAIL))

        @block.gpsimd
        def _(pool):
            nc.gpsimd.memset(ones[:], 1.0)
            nc.gpsimd.memset(minus_half[:], -0.5).then_inc(s("set_ones"), 1)
            nc.gpsimd.memset(ctxN[0:KEYS, :, NJ - 1, :], 0.0)
            nc.gpsimd.memset(ctxT[:, :, :, CTX:CPAD], 0.0)
            nc.gpsimd.memset(prob[:, :, CTX:CPAD], 0.0).then_inc(s("set_pads"), 1)
            nc.gpsimd.memset(wo[:], 0.0)
            nc.gpsimd.memset(zero_rows[:], 0.0).then_inc(s("set_zero"), 1)

            def inverse_root(st, var=std[:], to=rstd[:]):
                for part, (a, z) in enumerate(LN_PARTS[st]):
                    pool.wait_ge(s("n_var"), roots(st, part))
                    nc.gpsimd.tensor_tensor(to[:, a:z], var[:, a:z], minus_half[0:var.shape[0], a:z], ALU.pow) \
                        .then_inc(s("n_std"), 1)

            pool.wait_ge(s("set_ones"), 1)
            inverse_root("a")
            pool.wait_ge(s("ld_mask"), 16)
            for b in range(NB):
                if b >= 2:
                    pool.wait_ge(s("a_max"), b - 1)
                nc.gpsimd.tensor_scalar(keep[:, b % 2, :], mask8[:, b, :], -1.0, 1.0, ALU.mult, ALU.add)
                nc.gpsimd.tensor_scalar(drop[:, b % 2, :], mask8[:, b, :], NEG, 0.0, ALU.mult, ALU.add) \
                    .then_inc(s("a_mask"), 1)
            inverse_root("b")
            pool.wait_ge(s("b_zero"), 16 * NPAIR)
            for b in range(NB):
                pool.wait_ge(s("b_xs"), b + 1)
                nc.gpsimd.indirect_dma_start(xs_dram, bass.IndirectOffsetOnAxis(slot[:, b:b + 1], 0), xs[:, b, :], None,
                                             bounds_check=NSLOT - 1, oob_is_err=False).then_inc(s("b_scat"), 16)
            pool.wait_ge(s("n_hT"), NB // 2 * (turn("b") + 1))
            nc.gpsimd.memset(hN[:], 0.0).then_inc(s("b_clear"), 1)
            pool.wait_ge(s("b_y"), LAST_IN_CTX + 1)
            nc.gpsimd.memset(ctxT[:, :, :, CTX:CPAD], 0.0).then_inc(s("set_pads"), 1)
            pool.wait_ge(s("b_clear"), 1)
            for u in range(2):
                pool.wait_ge(s(f"b_yst{u}"), 16 * NPAIR // 2)
            for b in range(NB):
                nc.gpsimd.indirect_dma_start(hN[:, b, :], None, y_dram, bass.IndirectOffsetOnAxis(slot[:, b:b + 1], 0),
                                             bounds_check=NSLOT - 1, oob_is_err=False).then_inc(s(f"b_gat{b // 4}"), 16)
            nc.gpsimd.memset(wkv2[0:DC, 1], 0.0)
            nc.gpsimd.memset(wkv2[DC:, 0], 0.0).then_inc(s("b_clear"), 1)
            pool.wait_ge(s("b_clear"), 2)
            for u in range(2):
                for j in range(NJ):
                    last = nc.gpsimd.memset(vpad[:, u, j, :].rearrange("p (h c) -> p h c", c=32)[:, :, DH:], 1.0)
            last.then_inc(s("c_vones"), 1)

            def spread_queries(b, done):
                q = qT[:, :, T * b:T * b + T].unsqueeze(2).to_broadcast([128, KT, 8, T])
                m = consts[:, cs["headmask"]].unsqueeze(1).unsqueeze(3).to_broadcast([128, KT, 8, T])
                nc.gpsimd.tensor_tensor(qbd[:, b % 2].rearrange("p k (h t) -> p k h t", h=8), q, m, ALU.mult) \
                    .then_inc(done, 1)

            def low_part(dst, whole, high, done):
                nc.gpsimd.tensor_tensor(dst, whole, high.bitcast(f32), ALU.subtract).then_inc(done, 1)

            def k_low(b):
                pool.wait_ge(s("c_kh"), b + 1)
                low_part(kx[:, 1], kraw[:, b % 2, :, 0:CEV], kx[:, 0], s("c_kl"))

            k_low(0)
            inverse_root("c")
            for half in range(2):
                pool.wait_ge(s("c_qh"), half + 1)
                cut = slice(HALF * half, HALF * (half + 1))
                low_part(qx[:, 1, :, cut], qT[:, :, cut], qx[:, 0, :, cut], s("c_ql"))
            for b in range(1, NB):
                k_low(b)
            inverse_root("d")
            nc.gpsimd.memset(rsumF, 0.0).then_inc(s("set_pads"), 1)
            def times_cos(t, half, turn):
                pool.wait_ge(s("d_swap"), turn)
                w4 = t[:, :, HALF * half:HALF * (half + 1)].rearrange("p k (b t) -> p k b t", t=T)
                cos = consts[:, cs["cos"]].unsqueeze(1).unsqueeze(1).to_broadcast([128, KT, NB // 2, T])
                nc.gpsimd.tensor_tensor(w4, w4, cos, ALU.mult).then_inc(s("d_cos"), 1)

            for half in range(2):
                times_cos(qT, half, half + 1)
            pool.wait_ge(s("d_rot"), 1)
            spread_queries(0, s("d_qbd"))
            for half in range(2):
                times_cos(krT, half, half + 3)
            for b in range(1, NB):
                pool.wait_ge(s("d_rot"), 1 if b < NB // 2 else 2)
                if b >= 2:
                    pool.wait_ge(s("d_s"), 4 * (b - 1))
                spread_queries(b, s("d_qbd"))
            inverse_root("e")
            inverse_root("f", stdF, rstdF)

        @block.scalar
        def _(act):
            def ln_act(st):
                for g in range(NB // 2):
                    act.wait_ge(s("n_tp"), NB // 2 * turn(st) + g + 1)
                    nc.scalar.activation(hT[:, :, 2 * T * g:2 * T * (g + 1)], bank3(g % 2, KT, 2 * T), ACT.Copy) \
                        .then_inc(s("n_hT"), 1)

            act.wait_ge(s("set_ones"), 1)
            act.wait_ge(s("ld_small"), 96)
            nc.scalar.activation(tg[:], gates[:], ACT.Tanh).then_inc(s("act_step"), 1)
            ln_act("a")
            for u in range(2 * KT):
                n, half = u // 2, u % 2
                act.wait_ge(s("a_t"), u + 1)
                if u == 0:
                    act.wait_ge(s("a_foldsb"), 1)
                nc.scalar.activation(tT[:, n, HALF * half:HALF * (half + 1)], PB[4 + u % 2][:, 0:HALF], ACT.Identity,
                                     bias=foldv[:, n:n + 1]).then_inc(s("a_tsb"), 1)
            for half in range(2):
                act.wait_ge(s("a_c"), half + 1)
                nc.scalar.activation(cT[:, HALF * half:HALF * (half + 1)], PB[6 + half][0:1, 0:HALF], ACT.Identity,
                                     bias=fold0[:]).then_inc(s("a_csb"), 1)
            act.wait_ge(s("set_pads"), 1)
            for i in range(NB + 4):
                if 2 <= i < NB + 2:
                    b = i - 2
                    act.wait_ge(s("a_pt"), b + 1)
                    if b >= 2:
                        act.wait_ge(s("a_mix"), b - 1)
                    nc.scalar.activation(pT[0:KEYS, b % 2, :], PB[2 + b % 2][0:KEYS, 0:NJ * T], ACT.Copy) \
                        .then_inc(s("a_ptsb"), 1)
                if i < NB:
                    act.wait_ge(s("a_max"), i + 1)
                    if i >= NP_:
                        act.wait_ge(s("a_pt"), i - NP_ + 1)
                    nc.scalar.activation(prob[:, i % NP_, 0:CTX], sc[:, i % 2, :], ACT.Exp, bias=nmx[:, 0, i:i + 1],
                                         accum_out=rsum[:, i:i + 1]).then_inc(s("a_p"), 1)
                if 2 <= i < NB + 2:
                    b = i - 2
                    act.wait_ge(s("a_mix"), b + 1)
                    if b >= 2:
                        act.wait_ge(s("a_mt"), b - 1)
                    nc.scalar.activation(mix[:, b % 2, :], PB[4][0:T, 0:D], ACT.Copy).then_inc(s("a_mixsb"), 1)
                if 3 <= i < NB + 3:
                    b = i - 3
                    act.wait_ge(s("a_mt"), b + 1)
                    if b >= 2:
                        act.wait_ge(s("a_y"), b - 1)
                    nc.scalar.activation(mixT[:, b % 2], bank3(5, KT, T), ACT.Copy).then_inc(s("a_mtsb"), 1)
            ln_act("b")
            for half in range(2):
                act.wait_ge(s("lgT"), half + 1)
                nc.scalar.activation(lgT[:, HALF * half:HALF * (half + 1)], PB[2 + half][0:NE, 0:HALF], ACT.Copy) \
                    .then_inc(s("lgTsb"), 1)
            act.wait_ge(s("b_mx"), 1)
            nc.scalar.activation(r1[:, 1, :], r1[:, 0, :], ACT.Sigmoid).then_inc(s("b_sig"), 1)
            act.wait_ge(s("lg"), 1)
            for u in range(2 * FT):
                act.wait_ge(s("b_sgu"), u + 1)
                if u >= 2:
                    act.wait_ge(s("b_hid"), u - 1)
                nc.scalar.activation(sil[:, u % 2, 0:HALF], PB[2 * u % 8][:, 0:HALF], ACT.Silu).then_inc(s("b_sil"), 1)

            def xg_copy(i):
                act.wait_ge(s("b_xt"), i + 1)
                if i >= 2:
                    act.wait_ge(s("b_gu"), i - 1)
                nc.scalar.activation(xgT[:, i % 2], bank3(6, KT, 128), ACT.Copy).then_inc(s("b_xtsb"), 1)

            xg_copy(0)
            for i in range(NPAIR + 1):
                if i < NPAIR:
                    act.wait_ge(s("b_gu"), i + 1)
                    act.wait_ge(s("b_hid"), 2 * FT)
                    if i >= 2:
                        act.wait_ge(s("b_au"), i - 1)
                    nc.scalar.activation(sil[:, i % 2, :], PB[2 * (i % 2)][:, :], ACT.Silu).then_inc(s("b_esil"), 1)
                if i + 1 < NPAIR:
                    xg_copy(i + 1)
                if i >= 1:
                    p = i - 1
                    act.wait_ge(s("b_y"), p + 1)
                    if p >= 2:
                        act.wait_ge(s(f"b_yst{p % 2}"), 16 * (p // 2))
                    nc.scalar.activation(yb[:, p % 2, :], PB[5][:, 0:D], ACT.Copy).then_inc(s("b_ysb"), 1)
            act.wait_ge(s("o_flag"), 1)
            over = act.value_load(flag[0:1, 0:1], min_val=0, max_val=NT)
            with act.If(over > 0):
                with act.Fori(0, NE) as e:
                    for b in range(NB):
                        act.wait_ge(s("o_gu"), NB * e + (b + 1))
                        nc.scalar.activation(sil[0:T, 0, :], PB[0][0:T, :], ACT.Silu, scale=ocol[:, b:b + 1]) \
                            .then_inc(s("o_sil"), 1)

            def q_copy(st):
                base = 0 if st == "c" else 2 * KT
                for u in range(2 * KT):
                    half, n = u // KT, u % KT
                    cut = slice(HALF * half, HALF * (half + 1))
                    act.wait_ge(s("qry"), base + u + 1)
                    nc.scalar.activation(qT[:, n, cut], PB[4 + u % 2][:, 0:HALF], ACT.Copy,
                                         scale=float(DH) ** -0.5).then_inc(s("qry_sb"), 1)
                    if st == "c" and n == KT - 1:
                        act.wait_ge(s("qry_sb"), u + 1)
                        nc.scalar.activation(qx[:, 0, :, cut], qT[:, :, cut], ACT.Copy).then_inc(s("c_qh"), 1)

            def kv_copy(b, i):
                act.wait_ge(s("c_pr"), 5 * b + i + 1)
                if i < KT:
                    if b >= 2:
                        act.wait_ge(s("c_kl"), b - 1)
                    nc.scalar.activation(kraw[:, b % 2, i, :], PB[6][:, 0:CPAD], ACT.Copy).then_inc(s("c_prsb"), 1)
                else:
                    nc.scalar.activation(vpad[0:KEYS, b % 2, i - KT, :].rearrange("p (h c) -> p h c", c=32)[:, :, 0:DH],
                                         PB[6][0:KEYS, 0:D].rearrange("p (h c) -> p h c", c=DH), ACT.Copy) \
                        .then_inc(s("c_prsb"), 1)

            def k_high(b):
                act.wait_ge(s("c_prsb"), 5 * b + KT)
                if b >= 1:
                    act.wait_ge(s("c_kst"), 32 * b)
                nc.scalar.activation(kx[:, 0], kraw[:, b % 2, :, 0:CEV], ACT.Copy).then_inc(s("c_kh"), 1)

            for b in range(2):
                for i in range(5):
                    kv_copy(b, i)
                    if b == 0 and i == KT - 1:
                        k_high(0)
            ln_act("c")
            q_copy("c")
            k_high(1)
            def sums_copy(quad):
                act.wait_ge(s("c_av"), quad + 1)
                if quad >= 8:
                    act.wait_ge(s("c_att"), 2 * (quad // NG - 1))
                nc.scalar.activation(avsb[:, quad // NG % 2, quad % NG, :], PB[4][:, 0:T], ACT.Copy) \
                    .then_inc(s("c_avsb"), 1)

            for n in range(NB * NH):
                b, h = n // NH, n % NH
                act.wait_ge(s("c_max"), n + 1)
                if n >= 4:
                    act.wait_ge(s("c_pt"), n - 3)
                nc.scalar.activation(prob[:, n % 4, 0:CTX], PB[SBC[n % 4]][0:T, 0:CTX], ACT.Exp,
                                     bias=nmx[:, n % 4, 0:1]).then_inc(s("c_p"), 1)
                if n >= 3 and (n - 3) % 4 == ACT_COPIES:
                    m = n - 3
                    act.wait_ge(s("c_pt"), m + 1)
                    if m >= 8:
                        act.wait_ge(s("c_av"), m // 4 - 1)
                    nc.scalar.activation(pTq[0:KEYS, m % 8, :], PB[2 + m % 2][0:KEYS, 0:NJ * T], ACT.Copy) \
                        .then_inc(s("c_pta"), 1)
                if n % 4 == 1 and n >= 9:
                    sums_copy(n // 4 - 2)
                if 1 <= b < NB - 1 and h in KV_AT:
                    kv_copy(b + 1, KV_AT.index(h))
                    if h == KV_AT[KT - 1]:
                        k_high(b + 1)
            for quad in range(NB * NG - 2, NB * NG):
                sums_copy(quad)
            ln_act("d")
            q_copy("d")
            for half in range(2):
                act.wait_ge(s("d_kvc"), half + 1)
                nc.scalar.activation(kvcT[:, HALF * half:HALF * (half + 1)], PB[6 + half][:, 0:HALF], ACT.Copy) \
                    .then_inc(s("d_kvcsb"), 1)
            for u in range(2 * KT):
                half, n = u // KT, u % KT
                act.wait_ge(s("d_k"), u + 1)
                nc.scalar.activation(krT[:, n, HALF * half:HALF * (half + 1)], PB[4 + u % 2][:, 0:HALF], ACT.Copy) \
                    .then_inc(s("d_ksb"), 1)

            def v_copy(b):
                act.wait_ge(s("d_v"), b + 1)
                nc.scalar.activation(vpad[0:T, b % 2, 0, :].rearrange("p (h c) -> p h c", c=32)[:, :, 0:DH],
                                     PB[6][0:T, 0:D].rearrange("p (h c) -> p h c", c=DH), ACT.Copy).then_inc(s("d_vsb"), 1)

            def d_probs_copy(m):
                act.wait_ge(s("d_pt"), m + 1)
                if m >= 2:
                    act.wait_ge(s("d_av"), m - 1)
                nc.scalar.activation(pT4[0:T, m % 2, :], PB[2 + m % 2][0:T, 0:4 * T], ACT.Copy).then_inc(s("d_ptsb"), 1)

            v_copy(0)
            for n in range(4 * NB):
                b, g = n // 4, n % 4
                if n >= 2:
                    d_probs_copy(n - 2)
                act.wait_ge(s("d_max"), n + 1)
                if n >= 3:
                    act.wait_ge(s("d_pt"), n - 2)
                for q in range(4):
                    last = nc.scalar.activation(prob4[:, n % 3, T * q:T * q + T], PB[SB[n % 3]][0:T, T * q:T * q + T],
                                                ACT.Exp, bias=nmx[:, n % 4, q:q + 1])
                last.then_inc(s("d_p"), 1)
                if g == 0 and b >= 1:
                    v_copy(b)
            for m in range(4 * NB - 2, 4 * NB):
                d_probs_copy(m)
            for b in range(NB):
                act.wait_ge(s("d_x2"), b + 1)
                if b >= 4:
                    act.wait_ge(s("d_sq"), b - 3)
                nc.scalar.activation(row_T[0:T, D * (b % 4):D * (b % 4) + D], hN[:, b, :], ACT.Square, accum_out=rsum[:, b:b + 1]).then_inc(s("d_sq"), 1)
            for g in range(NB // 2):
                act.wait_ge(s("n_tp"), NB // 2 * turn("e") + g + 1)
                nc.scalar.activation(hT[:, :, 2 * T * g:2 * T * (g + 1)], bank3(g % 2, KT, 2 * T), ACT.Copy) \
                    .then_inc(s("n_hT"), 1)
            for half in range(2):
                act.wait_ge(s("lgT"), 2 + half + 1)
                nc.scalar.activation(row_T[0:2 + NX, HALF * half:HALF * (half + 1)], PB[2 + half][0:2 + NX, 0:HALF], ACT.Copy) \
                    .then_inc(s("lgTsb"), 1)
            nc.scalar.activation(row_T[0:2 + NX, NT:NT + 96].rearrange("p (r c) -> p r c", r=3),
                                 PB[3][0:2 + NX, HALF - TAILN:HALF].unsqueeze(1).to_broadcast([2 + NX, 3, TAILN]), ACT.Copy) \
                .then_inc(s("lgTsb"), 1)
            act.wait_ge(s("e_gx"), 1)
            nc.scalar.activation(ge, gl, ACT.Exp).then_inc(s("e_gexp"), 1)
            act.wait_ge(s("lg"), 2)
            for u in range(4 * FT):
                act.wait_ge(s("e_gu"), u + 1)
                if u >= 2:
                    act.wait_ge(s("e_hid"), u - 1)
                nc.scalar.activation(sil[:, u % 2, 0:HALF], PB[2 * u % 8][:, 0:HALF], ACT.Silu).then_inc(s("e_sil"), 1)
            act.wait_ge(s("e_hid"), 4 * FT)
            act.wait_ge(s("set_pads"), 3)
            for i, c in enumerate([0, TAIL] + WHOLE[1:]):
                n = TAILN if c == TAIL else 128
                if c == TAIL:
                    act.wait_ge(s("e_tail"), 2)
                else:
                    act.wait_ge(s("e_comb"), 5 * (WHOLE.index(c) + 1))
                if i >= 4:
                    act.wait_ge(s("f_sq"), i - 3)
                nc.scalar.activation(row_T[0:n, D * (i % 4):D * (i % 4) + D], hF[0:n, c, :], ACT.Square,
                                     accum_out=rsumF[0:n, c:c + 1]).then_inc(s("f_sq"), 1)

        @block.vector
        def _(dve):
            steps = [0]

            def link(ins):
                steps[0] += 1
                ins.then_inc(s("dve_step"), 1)
                dve.wait_ge(s("dve_step"), steps[0])

            def bc(ap, n):
                return ap.unsqueeze(2).to_broadcast([ap.shape[0], ap.shape[1], n])

            def batch_stats(b, done):
                dve.wait_ge(done, b + 1)
                nc.vector.bn_stats(bn6[:, b, :], x[:, b, :]).then_inc(s("stats"), 1)

            def ln_variance(st, part):
                a, z = LN_PARTS[st][part]
                dve.wait_ge(s("stats"), NB * turn(st) + z)
                for b in range(a, z):
                    last = nc.vector.bn_aggr(mv[:, b, :], bn6[:, b, :])
                link(last)
                nc.vector.tensor_scalar(std[:, a:z], mv[:, a:z, 1], LN_EPS, None, ALU.add).then_inc(s("n_var"), 1)

            def ln_rows(st, part):
                dve.wait_ge(s("n_std"), roots(st, part))
                for b in range(*LN_PARTS[st][part]):
                    nc.vector.tensor_scalar(hN[:, b, :], x[:, b, :], mv[:, b, 0:1], rstd[:, b:b + 1],
                                            ALU.subtract, ALU.mult).then_inc(s("n_hN"), 1)

            dve.wait_ge(s("ld_x"), 16)
            for b in range(NB):
                nc.vector.bn_stats(bn6[:, b, :], x[:, b, :]).then_inc(s("stats"), 1)
            ln_variance("a", 0)
            ln_rows("a", 0)
            dve.wait_ge(s("a_fold"), 1)
            nc.vector.tensor_scalar(fold[:], bank3(2, KT, D), 1.0 / 16, None, ALU.mult)
            nc.vector.tensor_scalar(foldv[:], PB[3][:, 0:4], 1.0 / 16, None, ALU.mult)
            nc.vector.tensor_scalar(fold0[:], PB[3][0:1, 4:5], 1.0 / 16, None, ALU.mult).then_inc(s("a_foldsb"), 1)
            dve.wait_ge(s("act_step"), 1)
            dve.wait_ge(s("ld_small"), 96)
            link(nc.vector.tensor_scalar(grow[:], brow["bv"][0:T], tg[0:T, 0:1], None, ALU.mult))
            link(nc.vector.tensor_tensor(x[:], x[:], grow[:].unsqueeze(1).to_broadcast([T, NB, D]), ALU.add))
            dve.wait_ge(s("a_cc"), 1)
            nc.vector.tensor_copy(ccol[:], PB[3][0:T, 0:NB]).then_inc(s("a_ccsb"), 1)
            dve.wait_ge(s("a_ccsb"), 1)
            for i in range(NB + 4):
                if i < NB:
                    b = i
                    dve.wait_ge(s("a_s"), b + 1)
                    dve.wait_ge(s("a_mask"), b + 1)
                    if b >= 2:
                        dve.wait_ge(s("a_p"), b - 1)
                    link(nc.vector.scalar_tensor_tensor(out=sc[:, b % 2, :], in0=PB[SB[b % 3]][0:T, 0:CTX],
                                                        scalar=ccol[:, b:b + 1], in1=keep[:, b % 2, :],
                                                        op0=ALU.add, op1=ALU.mult))
                    link(nc.vector.tensor_tensor(sc[:, b % 2, :], sc[:, b % 2, :], drop[:, b % 2, :], ALU.add))
                    nc.vector.tensor_reduce(nmx[:, 0, b:b + 1], sc[:, b % 2, :], AX.X, ALU.max, negate=True) \
                        .then_inc(s("a_max"), 1)
                if i >= 4:
                    b = i - 4
                    if b == NB - 2:
                        ln_variance("b", 0)
                    dve.wait_ge(s("a_p"), b + 1)
                    link(nc.vector.reciprocal(rg[:, b:b + 1], rsum[:, b:b + 1]))
                    link(nc.vector.tensor_scalar(rg[:, b:b + 1], rg[:, b:b + 1], tg[0:T, 0:1], None, ALU.mult))
                    dve.wait_ge(s("a_y"), b + 1)
                    nc.vector.scalar_tensor_tensor(out=x[:, b, :], in0=PB[6][0:T, 0:D], scalar=rg[:, b:b + 1],
                                                   in1=x[:, b, :], op0=ALU.mult, op1=ALU.add).then_inc(s("a_res"), 1)
                    batch_stats(b, s("a_res"))
                    if b == NB - 2:
                        ln_rows("b", 0)
            ln_variance("b", 1)
            ln_rows("b", 1)
            dve.wait_ge(s("lg"), 1)
            link(nc.vector.tensor_copy(lg[:], PB[4][0:T, 0:NB * NE].rearrange("p (b e) -> p b e", b=NB)))
            nc.vector.tensor_reduce(r1[:, 0, :], lg[:], AX.X, ALU.max).then_inc(s("b_mx"), 1)
            dve.wait_ge(s("b_mx"), 1)

            def over_b(ap):
                return ap.unsqueeze(1).to_broadcast([T, NB, ap.shape[-1]])

            link(nc.vector.tensor_tensor(key[:], lg[:], bc(r1[:, 0, :], NE), ALU.is_equal))
            link(nc.vector.tensor_tensor(key[:], key[:], over_b(consts[0:T, cs["rev16"]]), ALU.mult))
            link(nc.vector.tensor_reduce(r1[:, 2, :], key[:], AX.X, ALU.max))
            link(nc.vector.tensor_tensor(oh[:], key[:], bc(r1[:, 2, :], NE), ALU.is_equal))
            link(nc.vector.memset(pre[:, 0, :], 0.0))
            for b in range(1, NB):
                link(nc.vector.tensor_tensor(pre[:, b, :], pre[:, b - 1, :], oh[:, b - 1, :], ALU.add))
            nc.vector.tensor_tensor(key[:], oh[:], over_b(consts[0:T, cs["base16"]]), ALU.mult).then_inc(s("b_oh"), 1)
            dve.wait_ge(s("b_oh"), 1)
            link(nc.vector.tensor_reduce(r1[:, 3, :], key[:], AX.X, ALU.add))
            dve.wait_ge(s("b_pos"), 1)
            link(nc.vector.tensor_tensor(pos[:], PB[5][0:T, 0:NB * NE].rearrange("p (b e) -> p b e", b=NB), oh[:], ALU.mult))
            link(nc.vector.tensor_reduce(r1[:, 4, :], pos[:], AX.X, ALU.add))
            link(nc.vector.tensor_scalar(r1[:, 5, :], r1[:, 4, :], float(FULL), None, ALU.is_ge))
            link(nc.vector.tensor_tensor(r1[:, 6, :], r1[:, 4, :], r1[:, 3, :], ALU.add))
            link(nc.vector.scalar_tensor_tensor(out=r1[:, 7, :], in0=r1[:, 5, :], scalar=float(SKIP), in1=r1[:, 6, :],
                                                op0=ALU.mult, op1=ALU.add))
            nc.vector.tensor_copy(slot[:], r1[:, 7, :]).then_inc(s("b_slot"), 1)
            dve.wait_ge(s("b_sig"), 1)
            link(nc.vector.tensor_tensor(r1[:, 8, :], r1[:, 5, :], r1[:, 1, :], ALU.mult))
            link(nc.vector.tensor_tensor(oscale[:], oh[:], bc(r1[:, 8, :], NE), ALU.mult))
            for b in range(NB):
                nc.vector.tensor_scalar(xs[:, b, :], hN[:, b, :], r1[:, 1, b:b + 1], None, ALU.mult).then_inc(s("b_xs"), 1)
            dve.wait_ge(s("b_pos"), 2)
            link(nc.vector.tensor_reduce(r1[0:1, 9, 0:1], PB[5][0:1, 0:NB], AX.X, ALU.add))
            nc.vector.tensor_copy(flag[:], r1[0:1, 9, 0:1]).then_inc(s("o_flag"), 1)
            for u in range(2 * FT):
                f, half = u // 2, u % 2
                dve.wait_ge(s("b_sil"), u + 1)
                nc.vector.tensor_tensor(hid[:, f, HALF * half:HALF * (half + 1)], sil[:, u % 2, 0:HALF],
                                        PB[(2 * u + 1) % 8][:, 0:HALF], ALU.mult).then_inc(s("b_hid"), 1)
            for i in range(NPAIR + 1):
                if i >= 1:
                    p = i - 1
                    dve.wait_ge(s("b_at"), p + 1)
                    if p >= 2:
                        dve.wait_ge(s("b_y"), p - 1)
                    nc.vector.tensor_copy(auT[:, p % 2], bank3(4, FT, 128)).then_inc(s("b_atsb"), 1)
                    dve.wait_ge(s("b_sd"), p + 1)
                    nc.vector.scalar_tensor_tensor(out=x[:, p, :], in0=PB[7][0:T, 0:D], scalar=tg[0:T, 2:3],
                                                   in1=x[:, p, :], op0=ALU.mult, op1=ALU.add).then_inc(s("b_sdres"), 1)
                if i < NPAIR:
                    dve.wait_ge(s("b_esil"), i + 1)
                    if i >= 2:
                        dve.wait_ge(s("b_at"), i - 1)
                    nc.vector.tensor_tensor(au[:, i % 2, :], sil[:, i % 2, :], PB[2 * (i % 2) + 1][:, :], ALU.mult) \
                        .then_inc(s("b_au"), 1)
            dve.wait_ge(s("b_sdres"), NB)
            for b in range(NB):
                dve.wait_ge(s(f"b_gat{b // 4}"), 64)
                nc.vector.scalar_tensor_tensor(out=x[:, b, :], in0=hN[:, b, :], scalar=tg[0:T, 2:3], in1=x[:, b, :],
                                               op0=ALU.mult, op1=ALU.add).then_inc(s("b_res"), 1)
            dve.wait_ge(s("b_res"), NB)
            over = dve.value_load(flag[0:1, 0:1], min_val=0, max_val=NT)
            with dve.If(over > 0):
                nc.vector.memset(ocol[:], 0.0).then_inc(s("o_res"), 1)
                with dve.Fori(0, NE) as e:
                    dve.wait_ge(s("o_res"), NB * e + 1)
                    nc.vector.tensor_copy(ocol[:], oscale[:, :, bass.ds(e, 1)].rearrange("t b e -> t (b e)")) \
                        .then_inc(s("o_col"), 1)
                    dve.wait_ge(s("o_col"), e + 1)
                    for b in range(NB):
                        dve.wait_ge(s("o_sil"), NB * e + (b + 1))
                        nc.vector.scalar_tensor_tensor(out=au[0:T, 0, :], in0=PB[1][0:T, :], scalar=ocol[:, b:b + 1],
                                                       in1=sil[0:T, 0, :], op0=ALU.mult, op1=ALU.mult).then_inc(s("o_au"), 1)
                        dve.wait_ge(s("o_at"), NB * e + (b + 1))
                        nc.vector.tensor_copy(auT[:, 0, :, 0:T], bank3(4, FT, T)).then_inc(s("o_atsb"), 1)
                        dve.wait_ge(s("o_y"), NB * e + (b + 1))
                        nc.vector.scalar_tensor_tensor(out=x[:, b, :], in0=PB[5][0:T, 0:D], scalar=tg[0:T, 2:3],
                                                       in1=x[:, b, :], op0=ALU.mult, op1=ALU.add).then_inc(s("o_res"), 1)
                dve.wait_ge(s("o_res"), NB * NE + 1)
            for b in range(NB):
                batch_stats(b, s("b_res"))
            ln_variance("c", 0)
            ln_rows("c", 0)
            link(nc.vector.tensor_scalar(grow[:], brow["bo"][0:T], tg[0:T, 1:2], None, ALU.mult))
            link(nc.vector.tensor_tensor(x[:], x[:], grow[:].unsqueeze(1).to_broadcast([T, NB, D]), ALU.add))

            def normalise(b, bank, st, cols=slice(0, NG * T)):
                dve.wait_ge(s("d_av" if st == "d" else "c_avsb"), 4 * b + cols.stop // T)
                if b >= 2:
                    dve.wait_ge(s(st + "_y"), b - 1)
                sums = bank.rearrange("p g t -> p (g t)")[:, cols]
                link(nc.vector.stream_shuffle(den[:, cols], sums, UPPER_HALF))
                link(nc.vector.reciprocal(den[:, cols], den[:, cols]))
                last = nc.vector.tensor_tensor(attT[:, b % 2].rearrange("p g t -> p (g t)")[:, cols], sums, den[:, cols],
                                               ALU.mult)
                last.then_inc(s(st + "_att"), 1)

            def c_residual(b):
                dve.wait_ge(s("c_y"), b + 1)
                nc.vector.scalar_tensor_tensor(out=x[:, b, :], in0=PB[6][0:T, 0:D], scalar=tg[0:T, 1:2],
                                               in1=x[:, b, :], op0=ALU.mult, op1=ALU.add).then_inc(s("c_res"), 1)
                batch_stats(b, s("c_res"))

            for n in range(NB * NH + 3):
                b, h = n // NH, n % NH
                if n < NB * NH:
                    dve.wait_ge(s("c_s"), n + 1)
                    if n >= 4:
                        dve.wait_ge(s("c_p"), n - 3)
                    nc.vector.tensor_reduce(nmx[:, n % 4, 0:1], PB[SBC[n % 4]][0:T, 0:CTX], AX.X, ALU.max, negate=True) \
                        .then_inc(s("c_max"), 1)
                if n >= 3 and (n - 3) % 4 != ACT_COPIES:
                    m = n - 3
                    dve.wait_ge(s("c_pt"), m + 1)
                    if m >= 8:
                        dve.wait_ge(s("c_av"), m // 4 - 1)
                    nc.vector.tensor_copy(pTq[0:KEYS, m % 8, :], PB[2 + m % 2][0:KEYS, 0:NJ * T]).then_inc(s("c_ptsb"), 1)
                if n == NB * NH:
                    normalise(NB - 1, avsb[:, (NB - 1) % 2], "c", HALVES[0])
                if 1 <= b < NB and h in (6, 8):
                    normalise(b - 1, avsb[:, (b - 1) % 2], "c", HALVES[h // 2 - 3])
                if 1 <= b < NB and h == 11:
                    c_residual(b - 1)
            ln_variance("d", 0)
            normalise(NB - 1, avsb[:, (NB - 1) % 2], "c", HALVES[1])
            ln_rows("d", 0)
            c_residual(NB - 1)
            ln_variance("d", 1)
            ln_rows("d", 1)

            def rotate(t, half, turn):
                cut = slice(HALF * half, HALF * (half + 1))
                w4 = lambda ap: ap.rearrange("p k (b t) -> p k b t", t=T)
                sin = consts[:, cs["sin"]].unsqueeze(1).unsqueeze(1).to_broadcast([128, KT, NB // 2, T])
                nc.vector.stream_shuffle(rot[:, :, cut], t[:, :, cut], SWAP_PAIRS).then_inc(s("d_swap"), 1)
                dve.wait_ge(s("d_swap"), turn)
                link(nc.vector.tensor_tensor(w4(rot[:, :, cut]), w4(rot[:, :, cut]), sin, ALU.mult))
                dve.wait_ge(s("d_cos"), turn)
                nc.vector.tensor_tensor(t[:, :, cut], t[:, :, cut], rot[:, :, cut], ALU.add).then_inc(s("d_rot"), 1)

            for half in range(2):
                dve.wait_ge(s("qry_sb"), 2 * KT + KT * (half + 1))
                rotate(qT, half, half + 1)
            for half in range(2):
                dve.wait_ge(s("d_ksb"), KT * (half + 1))
                dve.wait_ge(s("d_rot"), half + 1)
                rotate(krT, half, half + 3)

            def d_residual(b):
                dve.wait_ge(s("d_y"), b + 1)
                nc.vector.tensor_tensor(hN[:, b, :], PB[6][0:T, 0:D], hN[:, b, :], ALU.add).then_inc(s("d_x2"), 1)

            for n in range(4 * NB):
                b, g = n // 4, n % 4
                if b >= 3 and g == 0:
                    d_residual(b - 3)
                dve.wait_ge(s("d_s"), n + 1)
                sc4 = PB[SB[n % 3]][0:T, 0:4 * T].rearrange("p (h t) -> p h t", h=4)
                nc.vector.tensor_reduce(nmx[:, n % 4, 0:4], sc4, AX.X, ALU.max, negate=True).then_inc(s("d_max"), 1)
                if b >= 1 and g == 2:
                    normalise(b - 1, bank3(4 + (b - 1) % 2, NG, T), "d")
            d_residual(NB - 3)

            def rms_variance(part):
                a, z = LN_PARTS["e"][part]
                dve.wait_ge(s("d_sq"), z)
                nc.vector.tensor_scalar(std[:, a:z], rsum[:, a:z], 1.0 / D, RMS_EPS, ALU.mult, ALU.add).then_inc(s("n_var"), 1)

            def rms_rows(part):
                dve.wait_ge(s("n_std"), roots("e", part))
                for b in range(*LN_PARTS["e"][part]):
                    nc.vector.scalar_tensor_tensor(out=hN[:, b, :], in0=hN[:, b, :], scalar=rstd[:, b:b + 1],
                                                   in1=brow["n1"][0:T], op0=ALU.mult, op1=ALU.mult).then_inc(s("n_hN"), 1)

            rms_variance(0)
            normalise(NB - 1, bank3(4 + (NB - 1) % 2, NG, T), "d")
            d_residual(NB - 2)
            rms_rows(0)
            d_residual(NB - 1)
            rms_variance(1)
            rms_rows(1)
            link(nc.vector.tensor_scalar(growF, brow["n2"][:], tg[:, 3:4], None, ALU.mult))
            dve.wait_ge(s("lg"), 2)
            dve.wait_ge(s("ld_wc"), 16 * 13)
            link(nc.vector.tensor_tensor(gl, PB[4][:, 0:NF * (2 + NX)].rearrange("p (b e) -> p b e", b=NF),
                                         gbias[:].unsqueeze(1).to_broadcast([128, NF, 2 + NX]), ALU.add))
            link(nc.vector.tensor_reduce(r1F[:, 0, :], gl[:, :, 0:2], AX.X, ALU.max))
            nc.vector.tensor_reduce(r1F[:, 1, :], gl[:, :, 2:2 + EPG], AX.X, ALU.max)
            link(nc.vector.tensor_reduce(r1F[:, 2, :], gl[:, :, 2 + EPG:], AX.X, ALU.max))
            link(nc.vector.tensor_tensor(gl[:, :, 0:2], gl[:, :, 0:2], bc(r1F[:, 0, :], 2), ALU.subtract))
            nc.vector.tensor_tensor(gl[:, :, 2:2 + EPG], gl[:, :, 2:2 + EPG], bc(r1F[:, 1, :], EPG), ALU.subtract)
            nc.vector.tensor_tensor(gl[:, :, 2 + EPG:], gl[:, :, 2 + EPG:], bc(r1F[:, 2, :], EPG), ALU.subtract) \
                .then_inc(s("e_gx"), 1)
            dve.wait_ge(s("e_gexp"), 1)
            for i, (a, z) in enumerate(((0, 2), (2, 2 + EPG), (2 + EPG, 2 + NX))):
                last = nc.vector.tensor_reduce(r1F[:, 3 + i, :], ge[:, :, a:z], AX.X, ALU.add)
            link(last)
            link(nc.vector.reciprocal(r1F[:, 3:6, :], r1F[:, 3:6, :]))
            for i, (a, z) in enumerate(((0, 2), (2, 2 + EPG), (2 + EPG, 2 + NX))):
                last = nc.vector.tensor_tensor(ge[:, :, a:z], ge[:, :, a:z], bc(r1F[:, 3 + i, :], z - a), ALU.mult)
            link(last)
            link(nc.vector.tensor_tensor(r1F[:, 6, :], ge[:, :, 0], ge[:, :, 1], ALU.is_ge))
            link(nc.vector.tensor_tensor(r1F[:, 7, :], ge[:, :, 0], ge[:, :, 1], ALU.max))
            link(nc.vector.tensor_tensor(r1F[:, 8, :], r1F[:, 6, :], r1F[:, 7, :], ALU.mult))
            link(nc.vector.tensor_tensor(r1F[:, 9, :], r1F[:, 7, :], r1F[:, 8, :], ALU.subtract))
            nc.vector.tensor_tensor(ge[:, :, 2:2 + EPG], ge[:, :, 2:2 + EPG], bc(r1F[:, 8, :], EPG), ALU.mult)
            link(nc.vector.tensor_tensor(ge[:, :, 2 + EPG:], ge[:, :, 2 + EPG:], bc(r1F[:, 9, :], EPG), ALU.mult))
            pe_ = ge[:, :, 2:]
            o8, k8, s8 = ohF, keyF, posF
            rev8 = consts[:, cs["rev8"]].unsqueeze(1).to_broadcast([128, NF, NX])
            link(nc.vector.tensor_copy(s8, pe_))
            for r in range(2):
                link(nc.vector.tensor_reduce(r1F[:, 0, :], s8, AX.X, ALU.max))
                link(nc.vector.tensor_tensor(k8, s8, bc(r1F[:, 0, :], NX), ALU.is_equal))
                link(nc.vector.tensor_tensor(k8, k8, rev8, ALU.mult))
                link(nc.vector.tensor_reduce(r1F[:, 1, :], k8, AX.X, ALU.max))
                link(nc.vector.tensor_tensor(o8, k8, bc(r1F[:, 1, :], NX), ALU.is_equal))
                if r == 0:
                    link(nc.vector.tensor_tensor(we, o8, pe_, ALU.mult))
                    link(nc.vector.tensor_tensor(s8, s8, o8, ALU.subtract))
                    link(nc.vector.tensor_tensor(s8, s8, o8, ALU.subtract))
                else:
                    link(nc.vector.tensor_tensor(o8, o8, pe_, ALU.mult))
                    link(nc.vector.tensor_tensor(we, we, o8, ALU.add))
            for u in range(4 * FT):
                which, f, half = u // (2 * FT), u // 2 % FT, u % 2
                dve.wait_ge(s("e_sil"), u + 1)
                nc.vector.tensor_tensor(hid2[:, which, f, HALF * half:HALF * (half + 1)], sil[:, u % 2, 0:HALF],
                                        PB[(2 * u + 1) % 8][:, 0:HALF], ALU.mult).then_inc(s("e_hid"), 1)
            dve.wait_ge(s("ld_F"), 32 * len(PIECES))
            for q in range(4):
                last = nc.vector.tensor_copy(wsel[32 * q:32 * q + 32], we[32 * q:32 * q + 32, TAIL, 2 * q:2 * q + 2])
            link(last)
            dve.wait_ge(s("e_tailx"), 1)
            link(nc.vector.tensor_scalar(acc, PB[1][:, 0:D], wsel[:, 0:1], None, ALU.mult))
            nc.vector.scalar_tensor_tensor(out=acc, in0=PB[1][:, D:2 * D], scalar=wsel[:, 1:2], in1=acc,
                                           op0=ALU.mult, op1=ALU.add).then_inc(s("e_acc"), 1)
            for w, c in enumerate(WHOLE):
                for i in range(5):
                    v = 5 * w + i
                    bank = PB[2 + v % 6]
                    dve.wait_ge(s("e_down"), v + 1)
                    if i == 0:
                        nc.vector.tensor_tensor(hF[:, c, :], bank[:, 0:D], hF[:, c, :], ALU.add).then_inc(s("e_comb"), 1)
                    else:
                        for q in range(2):
                            e = 2 * (i - 1) + q
                            last = nc.vector.scalar_tensor_tensor(
                                out=hF[:, c, :], in0=bank[:, D * q:D * q + D], scalar=we[:, c, e:e + 1],
                                in1=hF[:, c, :], op0=ALU.mult, op1=ALU.add)
                            if q == 0:
                                link(last)
                        last.then_inc(s("e_comb"), 1)
                    dve.wait_ge(s("e_comb"), v + 1)
                if w == 0:
                    dve.wait_ge(s("e_tail"), 1)
                    nc.vector.tensor_tensor(hF[0:TAILN, TAIL, :], PB[0][0:TAILN, 0:D], hF[0:TAILN, TAIL, :], ALU.add) \
                        .then_inc(s("e_tail"), 1)
                for a, z in PARTS:
                    if c != z - 1 and not (c == TAIL - 1 and z - 1 == TAIL):
                        continue
                    dve.wait_ge(s("f_sq"), z)
                    nc.vector.tensor_scalar(stdF[:, a:z], rsumF[:, a:z], 1.0 / D, RMS_EPS, ALU.mult, ALU.add) \
                        .then_inc(s("n_var"), 1)
                    dve.wait_ge(s("n_std"), roots("f", PARTS.index((a, z))))
                    for k in range(a, z):
                        n = TAILN if k == TAIL else 128
                        link(nc.vector.scalar_tensor_tensor(out=hF[0:n, k, :], in0=hF[0:n, k, :], scalar=rstdF[0:n, k:k + 1],
                                                            in1=growF[0:n], op0=ALU.mult, op1=ALU.mult))
                        nc.vector.tensor_tensor(xF[0:n, k, :], xF[0:n, k, :], hF[0:n, k, :], ALU.add).then_inc(s("f_out"), 1)

        @block.tensor
        def _(pe):
            def mm(o, l, r, start, stop):
                return nc.tensor.matmul(o, l, r, start=start, stop=stop)

            def ln_pe(st):
                for g in range(NB // 2):
                    pe.wait_ge(s("n_hN"), NB * turn(st) + 2 * g + 2)
                    if g >= 2:
                        pe.wait_ge(s("n_hT"), NB // 2 * turn(st) + g - 1)
                    for k in range(KT):
                        for bb in range(2):
                            at = (2 * k + bb) * T
                            last = nc.tensor.transpose(PB[g % 2][:, at:at + T], hN[:, 2 * g + bb, 128 * k:128 * k + 128],
                                                       ident[0:T, 0:T])
                    last.then_inc(s("n_tp"), 1)

            pe.wait_ge(s("ld_w0"), 64)
            pe.wait_ge(s("ld_const"), 16)
            for m in range(KT):
                for k in range(KT):
                    mm(PB[2][:, m * D:(m + 1) * D], wq0[:, k, 128 * m:128 * m + 128], wk0[:, k, :], k == 0, k == KT - 1)
            for v, (w, bias) in enumerate(((wk0, 0), (wq0, 1))):
                for m in range(KT):
                    for k in range(KT):
                        mm(PB[3][:, 2 * v + m:2 * v + m + 1], w[:, k, 128 * m:128 * m + 128], bqk[:, bias, k:k + 1],
                           k == 0, k == KT - 1)
            for k in range(KT):
                last = mm(PB[3][0:1, 4:5], bqk[:, 1, k:k + 1], bqk[:, 0, k:k + 1], k == 0, k == KT - 1)
            last.then_inc(s("a_fold"), 1)
            ln_pe("a")
            pe.wait_ge(s("a_foldsb"), 1)
            pe.wait_ge(s("n_hT"), NB // 2 * (turn("a") + 1))
            for u in range(2 * KT):
                n, half = u // 2, u % 2
                if u >= 2:
                    pe.wait_ge(s("a_tsb"), u - 1)
                for m in range(KT):
                    last = mm(PB[4 + u % 2][:, 0:HALF], fold[:, m, 128 * n:128 * n + 128],
                              hT[:, m, HALF * half:HALF * (half + 1)], m == 0, m == KT - 1)
                last.then_inc(s("a_t"), 1)
            for half in range(2):
                for m in range(KT):
                    last = mm(PB[6 + half][0:1, 0:HALF], foldv[:, 2 + m:3 + m], hT[:, m, HALF * half:HALF * (half + 1)],
                              m == 0, m == KT - 1)
                last.then_inc(s("a_c"), 1)
            pe.wait_ge(s("a_tsb"), 2 * KT)
            pe.wait_ge(s("a_csb"), 2)
            pe.wait_ge(s("ld_ctxT"), 16 * KT)
            pe.wait_ge(s("ld_ctxN"), 16 * NJ)
            pe.wait_ge(s("set_ones"), 1)
            for b in range(NB):
                last = nc.tensor.transpose(PB[3][0:T, b:b + 1], cT[0:1, T * b:T * b + T], ident[0:1, 0:1])
            last.then_inc(s("a_cc"), 1)
            pe.wait_ge(s("a_ccsb"), 1)
            for i in range(NB + 4):
                if 2 <= i < NB + 2:
                    b = i - 2
                    pe.wait_ge(s("a_p"), b + 1)
                    if b >= 2:
                        pe.wait_ge(s("a_ptsb"), b - 1)
                    for j in range(NJ):
                        last = nc.tensor.transpose(PB[2 + b % 2][0:KEYS, T * j:T * j + T],
                                                   prob[:, b % NP_, KEYS * j:KEYS * j + KEYS], ident[0:T, 0:T])
                    last.then_inc(s("a_pt"), 1)
                if i < NB:
                    b = i
                    if b >= 3:
                        pe.wait_ge(s("a_max"), b - 2)
                    for n in range(KT):
                        last = mm(PB[SB[b % 3]][0:T, 0:CTX], tT[:, n, T * b:T * b + T], ctxT[:, n, b, 0:CTX],
                                  n == 0, n == KT - 1)
                    last.then_inc(s("a_s"), 1)
                if 2 <= i < NB + 2:
                    b = i - 2
                    pe.wait_ge(s("a_ptsb"), b + 1)
                    if b >= 1:
                        pe.wait_ge(s("a_mixsb"), b)
                    for j in range(NJ):
                        last = mm(PB[4][0:T, 0:D], pT[0:KEYS, b % 2, T * j:T * j + T], ctxN[0:KEYS, b, j, :],
                                  j == 0, j == NJ - 1)
                    last.then_inc(s("a_mix"), 1)
                if 3 <= i < NB + 3:
                    b = i - 3
                    pe.wait_ge(s("a_mixsb"), b + 1)
                    if b >= 1:
                        pe.wait_ge(s("a_mtsb"), b)
                    for d in range(KT):
                        last = nc.tensor.transpose(PB[5][:, T * d:T * d + T], mix[:, b % 2, 128 * d:128 * d + 128],
                                                   ident[0:T, 0:T])
                    last.then_inc(s("a_mt"), 1)
                if i >= 4:
                    b = i - 4
                    pe.wait_ge(s("a_mtsb"), b + 1)
                    if b >= 1:
                        pe.wait_ge(s("a_res"), b)
                    for d in range(KT):
                        last = mm(PB[6][0:T, 0:D], mixT[:, b % 2, d, :], wv0[:, d, :], d == 0, d == KT - 1)
                    last.then_inc(s("a_y"), 1)
            ln_pe("b")
            pe.wait_ge(s("ld_wb"), 64)
            pe.wait_ge(s("n_hT"), NB // 2 * (turn("b") + 1))
            for half in range(2):
                for k in range(KT):
                    last = mm(PB[2 + half][0:NE, 0:HALF], wr[:, k, :], hT[:, k, HALF * half:HALF * (half + 1)],
                              k == 0, k == KT - 1)
                last.then_inc(s("lgT"), 1)
            pe.wait_ge(s("lgTsb"), 2)
            for b in range(NB):
                last = nc.tensor.transpose(PB[4][0:T, NE * b:NE * b + NE], lgT[:, T * b:T * b + T], ident[0:NE, 0:NE])
            last.then_inc(s("lg"), 1)

            def shared_gu(u):
                f, half = u // 2, u % 2
                if u >= 4:
                    pe.wait_ge(s("b_hid"), u - 3)
                for w in range(2):
                    for k in range(KT):
                        last = mm(PB[(2 * u + w) % 8][:, 0:HALF], wgu[:, k, w, 128 * f:128 * f + 128],
                                  hT[:, k, HALF * half:HALF * (half + 1)], k == 0, k == KT - 1)
                last.then_inc(s("b_sgu"), 1)

            shared_gu(0)
            shared_gu(1)
            pe.wait_ge(s("b_oh"), 1)
            mm(PB[5][0:T, 0:NB * NE], consts[0:T, cs["lower"]], oh[:].rearrange("p b e -> p (b e)"), True, False)
            mm(PB[5][0:T, 0:NB * NE], ones[0:T, 0:T], pre[:].rearrange("p b e -> p (b e)"), False, True) \
                .then_inc(s("b_pos"), 1)
            pe.wait_ge(s("b_slot"), 1)
            mm(PB[5][0:1, 0:NB], ones[0:T, 0:1], r1[:, 5, :], True, True).then_inc(s("b_pos"), 1)
            pe.wait_ge(s("o_flag"), 1)
            for u in range(2, 2 * FT):
                shared_gu(u)
            pe.wait_ge(s("b_hid"), 2 * FT)

            def slots_T(i):
                pe.wait_ge(s(f"b_xg{i // 2}"), 16)
                if i >= 1:
                    pe.wait_ge(s("b_xtsb"), i)
                for k in range(KT):
                    last = nc.tensor.transpose(PB[6][:, 128 * k:128 * k + 128], xg[:, i, 128 * k:128 * k + 128], ident)
                last.then_inc(s("b_xt"), 1)

            slots_T(0)
            for i in range(NPAIR + 1):
                if i < NPAIR:
                    pe.wait_ge(s("b_xtsb"), i + 1)
                    pe.wait_ge(s(f"ld_ring{i % RING}"), 32 * (i // RING + 1))
                    if i >= 2:
                        pe.wait_ge(s("b_au"), i - 1)
                    for w in range(2):
                        for k in range(KT):
                            for e in range(2):
                                at = (2 * k + w) * F
                                last = mm(PB[2 * (i % 2) + w][CAP * e:CAP * e + CAP, :], xgT[:, i % 2, k, CAP * e:CAP * e + CAP],
                                          pairs[i % RING][:, e, at:at + F], k == 0, k == KT - 1)
                    last.then_inc(s("b_gu"), 1)
                if i + 1 < NPAIR:
                    slots_T(i + 1)
                if i >= 1:
                    p = i - 1
                    pe.wait_ge(s("b_au"), p + 1)
                    if p >= 1:
                        pe.wait_ge(s("b_atsb"), p)
                    for f in range(FT):
                        last = nc.tensor.transpose(PB[4][:, 128 * f:128 * f + 128], au[:, p % 2, 128 * f:128 * f + 128], ident)
                    last.then_inc(s("b_at"), 1)
                    if p >= 1:
                        pe.wait_ge(s("b_sdres"), p)
                    for f in range(FT):
                        last = mm(PB[7][0:T, 0:D], hid[:, f, T * p:T * p + T], wdn[:, f, :], f == 0, f == FT - 1)
                    last.then_inc(s("b_sd"), 1)
                    pe.wait_ge(s("b_atsb"), p + 1)
                    pe.wait_ge(s(f"ld_down{p % RING}"), 32 * (p // RING + 1))
                    if p >= 1:
                        pe.wait_ge(s("b_ysb"), p)
                    for f in range(FT):
                        for e in range(2):
                            last = mm(PB[5][CAP * e:CAP * e + CAP, 0:D], auT[:, p % 2, f, CAP * e:CAP * e + CAP],
                                      pairs[p % RING][:, e, GU + D * f:GU + D * f + D], f == 0, f == FT - 1)
                    last.then_inc(s("b_y"), 1)
            over = pe.value_load(flag[0:1, 0:1], min_val=0, max_val=NT)
            with pe.If(over > 0):
                pe.wait_ge(s("b_ysb"), NPAIR)
                with pe.Fori(0, NE) as e:
                    pe.wait_ge(s("o_ld"), 32 * e + 32)
                    pe.wait_ge(s("o_col"), e + 1)
                    for b in range(NB):
                        pe.wait_ge(s("o_res"), NB * e + (b + 1))
                        for w in range(2):
                            for k in range(KT):
                                at = (2 * k + w) * F
                                last = mm(PB[w][0:T, :], hT[:, k, T * b:T * b + T], ring[:, 0, 0, at:at + F],
                                          k == 0, k == KT - 1)
                        last.then_inc(s("o_gu"), 1)
                        pe.wait_ge(s("o_au"), NB * e + (b + 1))
                        for f in range(FT):
                            last = nc.tensor.transpose(PB[4][:, T * f:T * f + T], au[0:T, 0, 128 * f:128 * f + 128],
                                                       ident[0:T, 0:T])
                        last.then_inc(s("o_at"), 1)
                        pe.wait_ge(s("o_atsb"), NB * e + (b + 1))
                        for f in range(FT):
                            last = mm(PB[5][0:T, 0:D], auT[:, 0, f, 0:T], ring[:, 0, 0, GU + D * f:GU + D * f + D],
                                      f == 0, f == FT - 1)
                        last.then_inc(s("o_y"), 1)
            pe.wait_ge(s("ld_wc"), 16 * 13)
            pe.wait_ge(s("ld_ctxT"), 32 * KT)

            def queries(st, w):
                base = 0 if st == "c" else 2 * KT
                pe.wait_ge(s("n_hT"), NB // 2 * (turn(st) + 1))
                for u in range(2 * KT):
                    half, n = u // KT, u % KT
                    if u >= 2:
                        pe.wait_ge(s("qry_sb"), base + u - 1)
                    for m in range(KT):
                        last = mm(PB[4 + u % 2][:, 0:HALF], w[:, m, 128 * n:128 * n + 128],
                                  hT[:, m, HALF * half:HALF * (half + 1)], m == 0, m == KT - 1)
                    last.then_inc(s("qry"), 1)

            def kv_part(b, i):
                if 5 * b + i >= 1:
                    pe.wait_ge(s("c_prsb"), 5 * b + i)
                if b >= 2 and i == 2:
                    pe.wait_ge(s("c_res"), b - 1)
                for k in range(KT):
                    if i < KT:
                        last = mm(PB[6][:, 0:CPAD], wc[:, 1, k, 128 * i:128 * i + 128], ctxT[:, k, b, :], k == 0, k == KT - 1)
                    else:
                        j = i - KT
                        last = mm(PB[6][0:KEYS, 0:D], ctxT[:, k, b, KEYS * j:KEYS * j + KEYS], wc[:, 2, k, :],
                                  k == 0, k == KT - 1)
                last.then_inc(s("c_pr"), 1)

            def out_projection(b, st, w, groups=range(NG)):
                if st == "c":
                    pe.wait_ge(s("c_prsb"), 5 * (b + 2) + 2 if b + 2 < NB else 5 * NB)
                    pe.wait_ge(s("c_att"), 2 * b + (groups[-1] + 1) // 2)
                else:
                    pe.wait_ge(s("d_vsb"), min(b + 3, NB))
                    pe.wait_ge(s("d_att"), b + 1)
                if b >= 1:
                    pe.wait_ge(s("c_res" if st == "c" else "d_x2"), b)
                for g in groups:
                    last = mm(PB[6][0:T, 0:D], attT[:, b % 2, g, :], w[:, g, :], g == 0, g == NG - 1)
                if groups[-1] == NG - 1:
                    last.then_inc(s(st + "_y"), 1)

            for b in range(2):
                for i in range(5):
                    kv_part(b, i)
            ln_pe("c")
            queries("c", wc[:, 0])
            pe.wait_ge(s("c_vones"), 1)
            pe.wait_ge(s("qry_sb"), 2 * KT)
            for n in range(NB * NH + 5):
                b, h = n // NH, n % NH
                if n < NB * NH:
                    if h == 0:
                        pe.wait_ge(s(f"c_k4_{b % 2}"), 128 * (b // 2 + 1))
                        pe.wait_ge(s(f"c_q4_{b // 2 % 2}"), 128 * (b // 4 + 1))
                    if n >= 4:
                        pe.wait_ge(s("c_p"), n - 3)
                    rows = slice(64 * (h % 2), 64 * (h % 2) + 64)
                    mm(PB[SBC[n % 4]][0:T, 0:CEV], q4[rows, b // 2 % 2, h // 2, T * (b % 2):T * (b % 2) + T],
                       k4[b % 2][rows, h // 2, :], True, True).then_inc(s("c_s"), 1)
                if 3 <= n <= NB * NH + 2:
                    m = n - 3
                    pe.wait_ge(s("c_p"), m + 1)
                    if m >= 2 and (m - 2) % 4 == ACT_COPIES:
                        pe.wait_ge(s("c_pta"), (m - 2) // 4 + 1)
                    elif m >= 2:
                        pe.wait_ge(s("c_ptsb"), m - 1 - (m - 2 - ACT_COPIES + 4) // 4)
                    for j in range(NJ):
                        last = nc.tensor.transpose(PB[2 + m % 2][0:KEYS, T * j:T * j + T],
                                                   prob[:, m % 4, KEYS * j:KEYS * j + KEYS], ident[0:T, 0:T])
                    last.then_inc(s("c_pt"), 1)
                if n >= 5 and (n - 5) % 4 == 3:
                    quad = (n - 5) // 4
                    bq, g = quad // NG, quad % NG
                    pe.wait_ge(s("c_ptsb"), 3 * quad + 3)
                    pe.wait_ge(s("c_pta"), quad + 1)
                    if g == 0:
                        pe.wait_ge(s("c_prsb"), 5 * bq + 5)
                    if quad >= 1:
                        pe.wait_ge(s("c_avsb"), quad)
                    for j in range(NJ):
                        for q in range(4):
                            hh = 4 * g + q
                            last = mm(PB[4][32 * q:32 * q + 32, 0:T],
                                      vpad[0:KEYS, bq % 2, j, 32 * hh:32 * hh + 32],
                                      pTq[0:KEYS, (4 * quad + q) % 8, T * j:T * j + T], j == 0, j == NJ - 1)
                    last.then_inc(s("c_av"), 1)
                if 1 <= b < NB - 1 and h in KV_AT:
                    kv_part(b + 1, KV_AT.index(h))
                if 1 <= b < NB and h in (8, 10):
                    out_projection(b - 1, "c", wo[:, 0], range(h // 2 % 4 * 2, h // 2 % 4 * 2 + 2))
            for groups in (range(0, 2), range(2, NG)):
                out_projection(NB - 1, "c", wo[:, 0], groups)
            ln_pe("d")
            pe.wait_ge(s("ld_wd"), 16 * 8)
            queries("d", wq2)
            for half in range(2):
                for k in range(KT):
                    last = mm(PB[6 + half][:, 0:HALF], wkvc[:, k, :], hT[:, k, HALF * half:HALF * (half + 1)],
                              k == 0, k == KT - 1)
                last.then_inc(s("d_kvc"), 1)
            pe.wait_ge(s("d_kvcsb"), 2)
            pe.wait_ge(s("qry_sb"), 4 * KT)
            for u in range(2 * KT):
                half, n = u // KT, u % KT
                if u >= 2:
                    pe.wait_ge(s("d_ksb"), u - 1)
                mm(PB[4 + u % 2][:, 0:HALF], wkv2[:, 0, 128 * n:128 * n + 128], kvcT[:, HALF * half:HALF * (half + 1)],
                   True, True).then_inc(s("d_k"), 1)

            def values(b):
                if b >= 1:
                    pe.wait_ge(s("d_vsb"), b)
                if b >= 3:
                    pe.wait_ge(s("d_x2"), b - 2)
                mm(PB[6][0:T, 0:D], kvcT[:, T * b:T * b + T], wkv2[:, 1, :], True, True).then_inc(s("d_v"), 1)

            values(0)
            for n in range(4 * NB + 3):
                b, g = n // 4, n % 4
                if n < 4 * NB:
                    if g == 0:
                        pe.wait_ge(s("d_qbd"), b + 1)
                        pe.wait_ge(s("d_rot"), 3 if b < NB // 2 else 4)
                    if n >= 3:
                        pe.wait_ge(s("d_p"), n - 2)
                    for q in range(4):
                        h = 4 * g + q
                        last = mm(PB[SB[n % 3]][0:T, T * q:T * q + T], qbd[:, b % 2, h // 8, T * (h % 8):T * (h % 8) + T],
                                  krT[:, h // 8, T * b:T * b + T], True, True)
                    last.then_inc(s("d_s"), 1)
                if 2 <= n <= 4 * NB + 1:
                    m = n - 2
                    pe.wait_ge(s("d_p"), m + 1)
                    if m >= 2:
                        pe.wait_ge(s("d_ptsb"), m - 1)
                    for q in range(4):
                        last = nc.tensor.transpose(PB[2 + m % 2][0:T, T * q:T * q + T], prob4[:, m % 3, T * q:T * q + T],
                                                   ident[0:T, 0:T])
                    last.then_inc(s("d_pt"), 1)
                if n >= 3:
                    m = n - 3
                    bq, g2 = m // 4, m % 4
                    pe.wait_ge(s("d_ptsb"), m + 1)
                    if g2 == 0:
                        pe.wait_ge(s("d_vsb"), bq + 1)
                        if bq >= 2:
                            pe.wait_ge(s("d_att"), bq - 1)
                    for q in range(4):
                        hh = 4 * g2 + q
                        last = mm(PB[4 + bq % 2][32 * q:32 * q + 32, T * g2:T * g2 + T],
                                  vpad[0:T, bq % 2, 0, 32 * hh:32 * hh + 32], pT4[0:T, m % 2, T * q:T * q + T], True, True)
                    last.then_inc(s("d_av"), 1)
                if g == 0 and 1 <= b < NB:
                    values(b)
                if 2 <= b < NB and g == 2:
                    out_projection(b - 2, "d", wo[:, 1])
            out_projection(NB - 2, "d", wo[:, 1])
            out_projection(NB - 1, "d", wo[:, 1])
            ln_pe("e")
            pe.wait_ge(s("n_hT"), NB // 2 * (turn("e") + 1))
            for half in range(2):
                for k in range(KT):
                    last = mm(PB[2 + half][0:2 + NX, 0:HALF], wge[:, k, :], hT[:, k, HALF * half:HALF * (half + 1)],
                              k == 0, k == KT - 1)
                last.then_inc(s("lgT"), 1)

            def e_gu(u):
                which, f, half = u // (2 * FT), u // 2 % FT, u % 2
                if u >= 4:
                    pe.wait_ge(s("e_hid"), u - 3)
                for w in range(2):
                    for k in range(KT):
                        last = mm(PB[(2 * u + w) % 8][:, 0:HALF], wgu2[:, which, k, F * w + 128 * f:F * w + 128 * f + 128],
                                  hT[:, k, HALF * half:HALF * (half + 1)], k == 0, k == KT - 1)
                last.then_inc(s("e_gu"), 1)

            pe.wait_ge(s("ld_we"), 16 * 6)
            e_gu(0)
            pe.wait_ge(s("lgTsb"), 2 + 3)
            for c, start in enumerate(STARTS):
                n = 2 + NX
                last = nc.tensor.transpose(PB[4][:, n * c:n * c + n], row_T[0:n, start:start + 128], ident[0:n, 0:n])
            last.then_inc(s("lg"), 1)
            e_gu(1)
            pe.wait_ge(s("e_gx"), 1)
            for u in range(2, 4 * FT):
                e_gu(u)
            pe.wait_ge(s("e_hid"), 4 * FT)
            for f in range(FT):
                for q in range(4):
                    last = mm(PB[1][32 * q:32 * q + 32, :], hid2[:, 1, f, NT - TAILN:NT],
                              w2[:, f, 2 * q:2 * q + 2, :].rearrange("p e d -> p (e d)"), f == 0, f == FT - 1)
            last.then_inc(s("e_tailx"), 1)
            for w, c in enumerate(WHOLE):
                cut = slice(STARTS[c], STARTS[c] + 128)
                for i in range(5):
                    v = 5 * w + i
                    bank = PB[2 + v % 6]
                    if v >= 6:
                        pe.wait_ge(s("e_comb"), v - 5)
                    for f in range(FT):
                        if i == 0:
                            last = mm(bank[:, 0:D], hid2[:, 0, f, cut], wdn[:, f, :], f == 0, f == FT - 1)
                        else:
                            last = mm(bank[:, :], hid2[:, 1, f, cut],
                                      w2[:, f, 2 * (i - 1):2 * i, :].rearrange("p e d -> p (e d)"), f == 0, f == FT - 1)
                    last.then_inc(s("e_down"), 1)
                if w == 0:
                    for f in range(FT):
                        mm(PB[0][0:TAILN, 0:D], hid2[:, 0, f, NT - TAILN:NT], wdn[:, f, :], f == 0, False)
                    pe.wait_ge(s("e_acc"), 1)
                    for q in range(4):
                        last = mm(PB[0][0:TAILN, 0:D], ident[:, 32 * q:32 * q + 32], acc, False, q == 3)
                    last.then_inc(s("e_tail"), 1)


def kernel(**inputs):
    import concourse.bacc as bacc
    from concourse.bass_utils import run_bass_kernel_spmd
    nc = bacc.Bacc("TRN2", target_bir_lowering=False, num_devices=1)
    arrays = {n: np.ascontiguousarray(v) for n, v in inputs.items()}
    arrays["x"] = np.ascontiguousarray(arrays["x"].transpose(1, 0, 2))
    context = arrays.pop("ctx_1024")
    arrays["ctx"] = context
    arrays["ctxT"] = np.ascontiguousarray(context.transpose(2, 0, 1))
    arrays["mask"] = np.ascontiguousarray(arrays.pop("mask_BxSxS2_bk1").transpose(1, 0, 2))
    for n in ("L0_xattn_Wv", "L0_ffn_w_router", "L0_ffn_w_gate", "L0_ffn_w_up", "L0_ffn_w_down",
              "L1_xattn_wq", "L1_xattn_wk", "L1_xattn_wv", "L1_xattn_wo"):
        arrays[n + "T"] = np.ascontiguousarray(arrays.pop(n).T)

    arrays["bqk"] = np.ascontiguousarray(
        np.stack([arrays.pop("L0_xattn_bq"), arrays.pop("L0_xattn_bk")]).reshape(2, KT, 128).transpose(2, 0, 1))

    cs, ncols = const_slices()
    c = np.zeros((128, ncols), np.float32)
    c[:, cs["ident"]] = np.eye(128)
    c[:, cs["headmask"]] = np.arange(128)[:, None] // DH == np.arange(8)[None, :]
    c[:T, cs["lower"]] = np.arange(T)[:, None] < np.arange(T)[None, :]
    freq = (1.0 / 10000.0 ** (np.arange(0, DH, 2, dtype=np.float32) / DH)).astype(np.float32)
    angle = (np.arange(T, dtype=np.float32)[None, :] * freq[:, None]).astype(np.float32)
    row = np.arange(128) % DH // 2
    c[:, cs["cos"]] = np.cos(angle)[row]
    c[:, cs["sin"]] = np.sin(angle)[row] * np.where(np.arange(128) % 2 == 0, -1.0, 1.0)[:, None]
    c[:, cs["rev16"]] = NE - np.arange(NE)
    c[:, cs["base16"]] = CAP * np.arange(NE)
    c[:, cs["rev8"]] = NX - np.arange(NX)
    arrays["consts"] = c

    A = {}
    for n, a in arrays.items():
        A[n] = nc.dram_tensor("in_" + n, a.shape, mybir.dt.from_np(a.dtype), kind="ExternalInput").ap()
    A["xs_dram"] = nc.dram_tensor("xs_dram", (NSLOT, D), mybir.dt.float32).ap()
    A["y_dram"] = nc.dram_tensor("y_dram", (NSLOT, D), mybir.dt.float32).ap()
    A["kx_dram"] = nc.dram_tensor("kx_dram", (NB, 2, D, CEV), mybir.dt.float32).ap()
    A["qx_dram"] = nc.dram_tensor("qx_dram", (2, D, NT), mybir.dt.float32).ap()
    out = nc.dram_tensor("out", (NB, T, D), mybir.dt.float32, kind="ExternalOutput").ap()
    build(nc, A, out)
    r = run_bass_kernel_spmd(nc, [{"in_" + n: a for n, a in arrays.items()}], core_ids=[0])
    return r.results[0]["out"]
```
